# Optimizing a Trainium2 kernel written in Bass

```python
import numpy as np
import jax
import jax.numpy as jnp

def _softmax(x, axis=-1):
    return jax.nn.softmax(x, axis=axis)

def _gelu(x):
    return jax.nn.gelu(x, approximate=True)

def _silu(x):
    return jax.nn.silu(x)

def _sigmoid(x):
    return jax.nn.sigmoid(x)

def _layernorm(x, axis=-1, eps=1e-05):
    m = jnp.mean(x, axis=axis, keepdims=True)
    v = jnp.var(x, axis=axis, keepdims=True)
    return (x - m) / jnp.sqrt(v + eps)

def _scatter_add(tgt, idx, src, axis=0):
    return tgt.at[idx].add(src)

def _segment_sum(src, seg, n):
    return jax.ops.segment_sum(src, seg, n)
kernel_name = 'mk_gnn_preln_d4_gnn_r16_8276aa'

def setup_inputs(seed: int=0):
    np.random.seed(seed)
    _w = jnp.asarray

    def _rec_inputs():
        import jax
        import jax.numpy as jnp
        _gk = jax.random.key(seed)
        x = -0.0003713 + 1 * jax.random.normal(jax.random.fold_in(_gk, 1), (6250, 256), jnp.float32)
        src = jax.random.randint(jax.random.fold_in(_gk, 2), (100000,), 0, 6250, jnp.int32)
        dst = jnp.minimum((6250 * jax.random.uniform(jax.random.fold_in(_gk, 3), (100000,)) ** 2.0).astype(jnp.int32), 99999)
        _o = jnp.argsort(dst, stable=True)
        src = src[_o]
        dst = dst[_o]
        edge_attr_3 = -0.000451519 + 1.00018 * jax.random.normal(jax.random.fold_in(_gk, 12), (100000, 3), jnp.float32)
        edge_type_8 = jax.random.randint(jax.random.fold_in(_gk, 14), (100000,), 0, 8, jnp.int32)
        return (x, src, dst, edge_attr_3, edge_type_8)
    x, src, dst, edge_attr_3, edge_type_8 = _rec_inputs()

    def _L0_gnn_setup():
        import jax, jax.numpy as jnp
        import numpy as np
        N_NODES = 3125
        N_EDGES = 50000
        key = jax.random.key(seed)
        k = jax.random.split(key, 7)
        in_feat, inter_dim, out_feat = (256, 256, 256)
        h = jax.random.normal(k[0], (N_NODES, in_feat), dtype=jnp.float32)
        w = jax.random.normal(k[1], (N_EDGES, 3), dtype=jnp.float32)
        edge_src = jax.random.randint(k[2], (N_EDGES,), 0, N_NODES, dtype=jnp.int32)
        edge_dst = jax.random.randint(k[3], (N_EDGES,), 0, N_NODES, dtype=jnp.int32)
        W1 = jax.random.normal(k[4], (inter_dim, in_feat + 3), dtype=jnp.float32) * jnp.sqrt(2.0 / (in_feat + 3 + inter_dim))
        b1 = jnp.zeros((inter_dim,), dtype=jnp.float32)
        W2 = jax.random.normal(k[5], (out_feat, in_feat + inter_dim), dtype=jnp.float32) * jnp.sqrt(2.0 / (in_feat + inter_dim + out_feat))
        return {'h': h, 'w': w, 'edge_src': edge_src, 'edge_dst': edge_dst, 'W1': W1, 'b1': b1, 'W2': W2}
    _L0_gnn_all = _L0_gnn_setup()
    _L0_gnn_in = {k: v for k, v in _L0_gnn_all.items() if k in ('W1', 'b1', 'W2')}
    del _L0_gnn_all

    def _L1_gnn_setup():
        import jax, jax.numpy as jnp
        import numpy as np
        N_NODES = 3125
        N_EDGES = 50000
        D_IN = 256
        D_OUT = 256
        N_REL = 8
        key = jax.random.key(seed)
        k_x, k_ei, k_et, k_w = jax.random.split(key, 4)
        x = jax.random.normal(k_x, (N_NODES, D_IN), dtype=jnp.float32)
        edge_index = jax.random.randint(k_ei, (2, N_EDGES), 0, N_NODES, dtype=jnp.int32)
        edge_type = jax.random.randint(k_et, (N_EDGES,), 0, N_REL, dtype=jnp.int32)
        limit = float(np.sqrt(6.0 / (D_IN + D_OUT)))
        weight = jax.random.uniform(k_w, (N_REL, D_IN, D_OUT), dtype=jnp.float32, minval=-limit, maxval=limit)
        bias = jnp.zeros((D_OUT,), dtype=jnp.float32)
        return {'x': x, 'edge_index': edge_index, 'edge_type': edge_type, 'weight': weight, 'bias': bias}
    _L1_gnn_all = _L1_gnn_setup()
    _L1_gnn_in = {k: v for k, v in _L1_gnn_all.items() if k in ('weight', 'bias')}
    del _L1_gnn_all

    def _L2_gnn_setup():
        import jax, jax.numpy as jnp
        import numpy as np
        N_NODES = 6250
        N_EDGES = 100000
        D_IN = 256
        HEADS = 8
        D_HEAD = 32
        NEG_SLOPE = 0.2
        BN_EPS = 1e-05
        key = jax.random.key(seed)
        ks = jax.random.split(key, 8)
        x = jax.random.normal(ks[0], (N_NODES, D_IN), dtype=jnp.float32)
        edge_index = jax.random.randint(ks[1], (2, N_EDGES), 0, N_NODES, dtype=jnp.int32)
        W = jax.random.normal(ks[2], (D_IN, HEADS * D_HEAD), dtype=jnp.float32) / np.sqrt(D_IN)
        att_src = jax.random.normal(ks[3], (HEADS, D_HEAD), dtype=jnp.float32) / np.sqrt(D_HEAD)
        att_dst = jax.random.normal(ks[4], (HEADS, D_HEAD), dtype=jnp.float32) / np.sqrt(D_HEAD)
        bias = jax.random.normal(ks[5], (HEADS * D_HEAD,), dtype=jnp.float32) * 0.01
        gamma = jnp.ones((HEADS * D_HEAD,), dtype=jnp.float32)
        beta = jnp.zeros((HEADS * D_HEAD,), dtype=jnp.float32)
        return {'x': x, 'edge_index': edge_index, 'W': W, 'att_src': att_src, 'att_dst': att_dst, 'bias': bias, 'gamma': gamma, 'beta': beta}
    _L2_gnn_all = _L2_gnn_setup()
    _L2_gnn_in = {k: v for k, v in _L2_gnn_all.items() if k in ('W', 'att_src', 'att_dst', 'bias', 'gamma', 'beta')}
    del _L2_gnn_all

    def _L3_gnn_setup():
        import jax, jax.numpy as jnp
        import numpy as np
        N_NODES = 6250
        N_EDGES = 200000
        D_FEAT = 256
        LEAKY_ALPHA = 0.2
        key = jax.random.key(seed)
        k1, k2, k3 = jax.random.split(key, 3)
        x = jax.random.normal(k1, (N_NODES, D_FEAT), dtype=jnp.float32)
        edge_index = jax.random.randint(k2, (2, N_EDGES), 0, N_NODES, dtype=jnp.int32)
        W = jax.random.normal(k3, (D_FEAT, D_FEAT), dtype=jnp.float32) * (1.0 / np.sqrt(D_FEAT))
        b = jnp.zeros((D_FEAT,), dtype=jnp.float32)
        return {'x': x, 'edge_index': edge_index, 'W': W, 'b': b}
    _L3_gnn_all = _L3_gnn_setup()
    _L3_gnn_in = {k: v for k, v in _L3_gnn_all.items() if k in ('W', 'b')}
    del _L3_gnn_all
    return {'x': x, 'src': src, 'dst': dst, 'edge_attr_3': edge_attr_3, 'edge_type_8': edge_type_8, 'L0_gnn_W1': _L0_gnn_in['W1'], 'L0_gnn_b1': _L0_gnn_in['b1'], 'L0_gnn_W2': _L0_gnn_in['W2'], 'L1_gnn_weight': _L1_gnn_in['weight'], 'L1_gnn_bias': _L1_gnn_in['bias'], 'L2_gnn_W': _L2_gnn_in['W'], 'L2_gnn_att_src': _L2_gnn_in['att_src'], 'L2_gnn_att_dst': _L2_gnn_in['att_dst'], 'L2_gnn_bias': _L2_gnn_in['bias'], 'L2_gnn_gamma': _L2_gnn_in['gamma'], 'L2_gnn_beta': _L2_gnn_in['beta'], 'L3_gnn_W': _L3_gnn_in['W'], 'L3_gnn_b': _L3_gnn_in['b']}

def reference(x, src, dst, edge_attr_3, edge_type_8, L0_gnn_W1, L0_gnn_b1, L0_gnn_W2, L1_gnn_weight, L1_gnn_bias, L2_gnn_W, L2_gnn_att_src, L2_gnn_att_dst, L2_gnn_bias, L2_gnn_gamma, L2_gnn_beta, L3_gnn_W, L3_gnn_b):
    import jax
    import jax.numpy as jnp

    def _L0_gnn_ref(h, w, edge_src, edge_dst, W1, b1, W2):
        import jax, jax.numpy as jnp
        import numpy as np
        N_NODES = 3125
        N_EDGES = 50000
        m = jnp.concatenate([h[edge_src], w], axis=1)
        tmp = jax.nn.relu(m @ W1.T + b1)
        h_N = jax.ops.segment_sum(tmp, edge_dst, num_segments=h.shape[0])
        h_total = jnp.concatenate([h, h_N], axis=1)
        h_lin = jax.nn.relu(h_total @ W2.T)
        norm = jnp.linalg.norm(h_lin, axis=-1, keepdims=True)
        return h_lin / jnp.maximum(norm, 1e-12)

    def _L1_gnn_ref(x, edge_index, edge_type, weight, bias):
        import jax, jax.numpy as jnp
        import numpy as np
        N_NODES = 3125
        N_EDGES = 50000
        D_IN = 256
        D_OUT = 256
        N_REL = 8
        num_nodes = x.shape[0]
        row, col = (edge_index[0], edge_index[1])
        xt = jnp.einsum('ni,rio->rno', x, weight)
        messages = xt[edge_type, col]
        out = jax.ops.segment_sum(messages, row, num_segments=num_nodes)
        return jax.nn.relu(out + bias)

    def _L2_gnn_ref(x, edge_index, W, att_src, att_dst, bias, gamma, beta):
        import jax, jax.numpy as jnp
        import numpy as np
        N_NODES = 6250
        N_EDGES = 100000
        D_IN = 256
        HEADS = 8
        D_HEAD = 32
        NEG_SLOPE = 0.2
        BN_EPS = 1e-05
        N = x.shape[0]
        H, D = att_src.shape
        xh = (x @ W).reshape(N, H, D)
        a_src = jnp.einsum('nhd,hd->nh', xh, att_src)
        a_dst = jnp.einsum('nhd,hd->nh', xh, att_dst)
        loops = jnp.arange(N, dtype=edge_index.dtype)
        src = jnp.concatenate([edge_index[0], loops])
        dst = jnp.concatenate([edge_index[1], loops])
        e = jax.nn.leaky_relu(a_src[src] + a_dst[dst], NEG_SLOPE)
        m = jax.ops.segment_max(e, dst, num_segments=N)
        e = jnp.exp(e - m[dst])
        denom = jax.ops.segment_sum(e, dst, num_segments=N)
        alpha = e / denom[dst]
        msg = xh[src] * alpha[:, :, None]
        out = jax.ops.segment_sum(msg, dst, num_segments=N).reshape(N, H * D) + bias
        mean = jnp.mean(out, axis=0)
        var = jnp.var(out, axis=0)
        out = (out - mean) * jax.lax.rsqrt(var + BN_EPS) * gamma + beta
        return out + x

    def _L3_gnn_ref(x, edge_index, W, b):
        import jax, jax.numpy as jnp
        import numpy as np
        N_NODES = 6250
        N_EDGES = 200000
        D_FEAT = 256
        LEAKY_ALPHA = 0.2
        N = x.shape[0]
        row = edge_index[0]
        col = edge_index[1]
        ones = jnp.ones(row.shape[0], dtype=x.dtype)
        deg = jax.ops.segment_sum(ones, row, num_segments=N)
        deg_safe = jnp.where(deg > 0, deg, 1.0)
        dinv_sqrt = jnp.where(deg > 0, jax.lax.rsqrt(deg_safe), 0.0)
        w = dinv_sqrt[row] * dinv_sqrt[col]
        h = jax.ops.segment_sum(w[:, None] * x[col], row, num_segments=N)
        h = h @ W + b
        return jnp.where(h >= 0, h, LEAKY_ALPHA * h)
    edge_index = jnp.stack([src, dst])
    h = jnp.maximum(_layernorm(x, axis=-1), 0.0)
    x = x + _L0_gnn_ref(h, edge_attr_3, src, dst, L0_gnn_W1, L0_gnn_b1, L0_gnn_W2)
    h = jnp.maximum(_layernorm(x, axis=-1), 0.0)
    x = x + _L1_gnn_ref(h, edge_index, edge_type_8, L1_gnn_weight, L1_gnn_bias)
    h = jnp.maximum(_layernorm(x, axis=-1), 0.0)
    x = x + _L2_gnn_ref(h, edge_index, L2_gnn_W, L2_gnn_att_src, L2_gnn_att_dst, L2_gnn_bias, L2_gnn_gamma, L2_gnn_beta)
    h = jnp.maximum(_layernorm(x, axis=-1), 0.0)
    x = x + _L3_gnn_ref(h, edge_index, L3_gnn_W, L3_gnn_b)
    return x

_drawn_inputs = setup_inputs


def setup_inputs(seed=0):
    import zlib

    import numpy as np

    out = dict(_drawn_inputs(seed))
    spreads = {'L0_gnn_b1': (0.0, 0.8),
     'L1_gnn_bias': (0.0, 0.304),
     'L2_gnn_gamma': (1.0, 0.2),
     'L2_gnn_beta': (0.0, 0.288),
     'L3_gnn_b': (0.0, 0.455)}
    factors = {'edge_attr_3': 8.0, 'L2_gnn_bias': 8.0}
    for name, (base, spread) in spreads.items():
        noise = np.random.default_rng([zlib.crc32(name.encode()), seed]).standard_normal(out[name].shape)
        drawn = base * np.exp(spread * noise) if base else spread * noise
        out[name] = jnp.asarray(drawn.astype(out[name].dtype))
    for name, factor in factors.items():
        out[name] = (out[name] * factor).astype(out[name].dtype)
    return out
```

```python
from contextlib import ExitStack

import numpy as np

import concourse.bass as bass
from concourse import mybir

F32 = mybir.dt.float32
BF16 = mybir.dt.bfloat16
I32 = mybir.dt.int32
ALU = mybir.AluOpType
ACT = mybir.ActivationFunctionType
AX = mybir.AxisListType
P = 128
D = 256
HEADS, DH = 8, 32
NREL = 8
EPS = 1e-5
SLOPE = 0.2
U = 16
REC = 8
AW = D + HEADS
BIG = 1e30


class Ring:

    def __init__(self, n, size):
        assert n % size == 0 and n // size >= 3
        self.n, self.size, self.rounds = n, size, n // size

    def at(self, i, u, back=0):
        q, s = divmod(u - back, self.size)
        j = i + q
        if isinstance(j, int) and not 0 <= self.size * j + s < self.n:
            return None
        return j, s

    def count(self, t, back=0):
        c = self.size * t[0] + t[1] + 1 - back
        return None if isinstance(c, int) and c <= 0 else c

    def run(self, eng, step, lag=0):
        for u in range(self.size):
            step(0, u)
        with eng.Fori(1, self.rounds - 1) as i:
            for u in range(self.size):
                step(i, u)
        for u in range(self.size):
            step(self.rounds - 1, u)
        for u in range(lag):
            step(self.rounds, u)


def wait_count(eng, sem, count):
    if count is not None:
        eng.wait_ge(sem, count)


class Gate:

    def __init__(self, eng, semaphore):
        self.eng, self.semaphore = eng, semaphore

    def step(self):
        self.eng.sem_inc(self.semaphore, 1)


class Shapes:
    def __init__(self, n_nodes, n_edges):
        self.N, self.E = n_nodes, n_edges
        self.NB = -(-n_nodes // P)
        self.LAST = n_nodes - (self.NB - 1) * P
        cols = -(-n_edges // P)
        self.COLS = -(-cols // U) * U
        self.EP = P * self.COLS
        tiles = (n_edges + self.NB * (P - 1)) // P
        self.NT = -(-tiles // U) * U
        assert n_edges > (P - 1) * self.COLS
        self.NOWHERE = float(P * (self.NB + 3))


def constants(nc, c, ctx):
    sh = c.sh
    sb = lambda name, shape, dt: ctx.enter_context(nc.sbuf_tensor(name, shape, dt))
    c.iota = sb("iota", [P, P], F32)
    c.iota_bf = sb("iota_bf", [P, P], BF16)
    c.ident = sb("ident", [P, P], F32)
    c.ident_bf = sb("ident_bf", [P, P], BF16)
    c.ones = sb("ones", [P, P], F32)
    c.x = sb("x_sb", [P, sh.NB, D], F32)
    c.stat = sb("stat", [P, sh.NB, 2], F32)
    c.rstd = sb("rstd", [P, sh.NB], F32)
    c.nbias = sb("nbias", [P, sh.NB], F32)
    with ExitStack() as st:
        sem = lambda name: nc.alloc_semaphore(name)
        made, x_zero, x_in = sem("made"), sem("x_zero"), sem("x_in")
        block = st.enter_context(nc.Block())

        @block.gpsimd
        def _(pool):
            nc.gpsimd.iota(c.iota[:, :], pattern=[[1, P]], base=0, channel_multiplier=0,
                           allow_small_or_imprecise_dtypes=True)
            nc.gpsimd.iota(c.iota_bf[:, :], pattern=[[1, P]], base=0, channel_multiplier=0,
                           allow_small_or_imprecise_dtypes=True)
            nc.gpsimd.memset(c.ones[:, :], 1.0).then_inc(made, 1)
            nc.gpsimd.memset(c.ident[:, :], 0.0).then_inc(made, 1)
            nc.gpsimd.memset(c.ident_bf[:, :], 0.0).then_inc(made, 1)
            pool.wait_ge(made, 3)
            for m in (c.ident, c.ident_bf):
                nc.gpsimd.affine_select(out=m[:, :], in_=m[:, :], compare_op=ALU.not_equal, fill=1.0,
                                        base=0, pattern=[[-1, P]], channel_multiplier=1)

        @block.vector
        def _(dve):
            nc.vector.memset(c.x[:, sh.NB - 1, :], 0.0).then_inc(x_zero, 1)

        @block.sync
        def _(sp):
            full = (sh.NB - 1) * P
            sp.dma_start(c.x[:, 0:sh.NB - 1, :],
                         c.x_in[0:full, :].rearrange("(i p) d -> p i d", p=P)).then_inc(x_in, 16)
            sp.wait_ge(x_zero, 1)
            sp.dma_start(c.x[0:sh.LAST, sh.NB - 1, :], c.x_in[full:sh.N, :]).then_inc(x_in, 16)
            sp.wait_ge(x_in, 32)


def sort_stage(nc, c, kind):
    sh = c.sh
    NB, COLS, NT = sh.NB, sh.COLS, sh.NT
    by_dst = kind == "dst"
    rec_out = c.rec_dst if by_dst else c.rec_src
    base_f, place_i, off_i = c.tiles[kind]
    own = sh.E - (P - 1) * COLS
    HALF = U // 2
    with ExitStack() as st:
        sb = lambda name, shape, dt: st.enter_context(nc.sbuf_tensor(f"{name}_{kind}", shape, dt))
        sem = lambda name: nc.alloc_semaphore(f"{name}_{kind}")
        src_i, dst_i = sb("src_i", [P, COLS], I32), sb("dst_i", [P, COLS], I32)
        third = sb("third", [P, COLS * 3] if by_dst else [P, COLS], F32 if by_dst else I32)
        rec = sb("rec", [P, COLS, REC], F32)
        key_i, key = sb("key_i", [P, COLS], I32), sb("key", [P, COLS], F32)
        mask, run, pos = sb("mask", [P, COLS], F32), sb("run", [P, COLS], F32), sb("pos", [P, COLS], F32)
        allone = sb("allone", [P, COLS], F32)
        pos_i = sb("pos_i", [P, COLS], I32)
        digits = sb("digits", [P, NB], F32)
        counts, offs = sb("counts", [P, NB], F32), sb("offs", [P, NB], F32)
        tot, incl = sb("tot", [P, NB], F32), sb("incl", [P, NB], F32)
        before = sb("before", [P, P], F32)
        upto = sb("upto", [P, P], F32)
        nb = sb("nb", [P, 1], F32)
        nt_i, nt, step_ = sb("nt_i", [P, 1], I32), sb("nt", [P, 1], F32), sb("step_", [P, 1], F32)
        past, tile_no = sb("past", [P, NT], F32), sb("tile_no", [P, NT], F32)
        off_f, place_f = sb("off_f", [P, NT], F32), sb("place_f", [P, NT], F32)
        stage_rec = sb("stage_rec", [P, 2, HALF, REC], F32)
        stage_pos = sb("stage_pos", [P, 2, HALF], I32)
        ps = [st.enter_context(nc.psum_tensor(f"ps{k}_{kind}", [P, 512], F32)) for k in range(7)]
        loaded, zeroed, tri = sem("loaded"), sem("zeroed"), sem("tri")
        counted, totals, starts, tiled = sem("counted"), sem("totals"), sem("starts"), sem("tiled")
        prefixed, listed, stepped, summed = sem("prefixed"), sem("listed"), sem("stepped"), sem("summed")
        staged = sem("staged")
        out_a, out_b = [sem(f"out_{h}") for h in "ab"]
        chain = sem("chain")
        block = st.enter_context(nc.Block())
        halves = ((0, 512), (512, NT)) if NT > 512 else ((0, NT),)

        @block.sync
        def _(sp):
            sp.wait_ge(zeroed, 2)
            for to, of, w in ((src_i, c.src_in, 1), (dst_i, c.dst_in, 1),
                              (third, c.attr_in if by_dst else c.type_in, 3 if by_dst else 1)):
                full = (P - 1) * COLS * w
                sp.dma_start(to[0:P - 1, :], of[0:full].rearrange("(p n) -> p n", p=P - 1)).then_inc(loaded, 16)
                sp.dma_start(to[P - 1:P, 0:own * w], of[full:full + own * w].rearrange("(p n) -> p n", p=1)).then_inc(loaded, 16)
            sp.wait_ge(loaded, 96)

        @block.gpsimd
        def _(pool):
            nc.gpsimd.memset(third[:, :], 0.0 if by_dst else 0).then_inc(zeroed, 1)
            nc.gpsimd.iota(digits[:, :], pattern=[[1, NB]], base=0, channel_multiplier=0,
                           allow_small_or_imprecise_dtypes=True)
            nc.gpsimd.iota(tile_no[:, :], pattern=[[1, NT]], base=0, channel_multiplier=0,
                           allow_small_or_imprecise_dtypes=True)
            nc.gpsimd.memset(before[:, :], 1.0)
            nc.gpsimd.memset(upto[:, :], 1.0)
            nc.gpsimd.iota(pos[:, :], pattern=[[1, COLS]], base=0, channel_multiplier=COLS,
                           allow_small_or_imprecise_dtypes=True).then_inc(tri, 1)
            pool.wait_ge(tri, 1)
            nc.gpsimd.affine_select(out=before[:, :], in_=before[:, :], compare_op=ALU.is_gt, fill=0.0,
                                    base=0, pattern=[[1, P]], channel_multiplier=-1)
            nc.gpsimd.affine_select(out=upto[:, :], in_=upto[:, :], compare_op=ALU.is_ge, fill=0.0,
                                    base=0, pattern=[[1, P]], channel_multiplier=-1)
            nc.gpsimd.affine_select(out=pos[:, :], in_=pos[:, :], compare_op=ALU.is_ge, fill=0.0,
                                    base=-sh.E, pattern=[[1, COLS]], channel_multiplier=COLS).then_inc(tri, 1)
            ring = Ring(COLS, U)
            gate = Gate(pool, c.passed["pool"])

            def step(i, u):
                h, k = divmod(u, HALF)
                if k == 0:
                    pool.wait_ge(staged, 2 * i + h + 1)
                    gate.step()
                nc.gpsimd.indirect_dma_start(
                    rec_out, bass.IndirectOffsetOnAxis(stage_pos[:, h, k:k + 1], 0),
                    stage_rec[:, h, k, :], None).then_inc((out_a, out_b)[h], 16)

            ring.run(pool, step)
            pool.wait_ge(out_a, 16 * COLS // 2)
            pool.wait_ge(out_b, 16 * COLS // 2)

        @block.vector
        def _(dve):
            chained = [0]

            def link(instruction):
                chained[0] += 1
                instruction.then_inc(chain, 1)
                dve.wait_ge(chain, chained[0])

            nc.vector.memset(allone[:, :], 1.0)
            nc.vector.memset(src_i[:, :], 0 if by_dst else int(sh.NOWHERE))
            link(nc.vector.memset(dst_i[:, :], int(sh.NOWHERE) if by_dst else 0))
            nc.vector.memset(rec[:, :, :], 0.0).then_inc(zeroed, 1)
            dve.wait_ge(loaded, 96)
            node_i = dst_i if by_dst else src_i
            rec_i = rec[:, :, :].bitcast(I32)
            nc.vector.tensor_copy(rec[:, :, 1], node_i[:, :])
            if by_dst:
                nc.vector.tensor_copy(rec_i[:, :, 0], src_i[:, :])
                nc.vector.tensor_copy(rec[:, :, 2:5], third[:, :].rearrange("p (n k) -> p n k", k=3))
            else:
                nc.vector.tensor_copy(rec_i[:, :, 2], dst_i[:, :])
                link(nc.vector.tensor_scalar(rec_i[:, :, 0], third[:, :], sh.N, None, ALU.mult))
                link(nc.vector.tensor_tensor(rec_i[:, :, 0], rec_i[:, :, 0], dst_i[:, :], ALU.add))
            link(nc.vector.tensor_single_scalar(key_i[:, :], node_i[:, :], 7, ALU.arith_shift_right))
            link(nc.vector.tensor_copy(key[:, :], key_i[:, :]))
            dve.wait_ge(tri, 2)
            with dve.Fori(0, NB) as d:
                dve.wait_ge(counted, d)
                nc.vector.tensor_scalar(mask[:, :], key[:, :], digits[:, bass.ds(d, 1)], None, ALU.is_equal,
                                        ALU.add, accum_out=counts[:, bass.ds(d, 1)]).then_inc(counted, 1)
            dve.wait_ge(counted, NB)
            dve.wait_ge(totals, 2)
            link(nc.vector.tensor_copy(tot[:, :], ps[1][:, 0:NB]))
            link(nc.vector.tensor_tensor_scan(incl[:, :], allone[:, 0:NB], tot[:, :], 0.0, ALU.mult, ALU.add))
            link(nc.vector.tensor_tensor(incl[:, :], incl[:, :], tot[:, :], ALU.subtract))
            link(nc.vector.scalar_tensor_tensor(offs[:, :], incl[:, :], -1.0, ps[0][:, 0:NB], ALU.add, ALU.add))
            dve.wait_ge(totals, 3)
            link(nc.vector.tensor_copy(nb[0:NB, :], ps[2][0:NB, 0:1]))
            link(nc.vector.tensor_scalar(nt[0:NB, :], nb[0:NB, :], float(P - 1), None, ALU.add))
            link(nc.vector.tensor_copy(nt_i[0:NB, :], nt[0:NB, :]))
            link(nc.vector.tensor_single_scalar(nt_i[0:NB, :], nt_i[0:NB, :], 7, ALU.arith_shift_right))
            link(nc.vector.tensor_copy(nt[0:NB, :], nt_i[0:NB, :]))
            nc.vector.scalar_tensor_tensor(step_[0:NB, :], nt[0:NB, :], float(-P), nb[0:NB, :],
                                           ALU.mult, ALU.add).then_inc(tiled, 1)
            dve.wait_ge(prefixed, 1)
            link(nc.vector.tensor_copy(nb[0:NB, :], ps[2][0:NB, 8:9]))
            nc.vector.tensor_scalar(past[0:NB, :], tile_no[0:NB, :], nb[0:NB, 0:1], None,
                                    ALU.is_ge).then_inc(listed, 1)
            dve.wait_ge(summed, 2 * len(halves))
            for k, (a, z) in enumerate(halves):
                link(nc.vector.tensor_scalar(base_f[:, a:z], ps[3 + k][:, 0:z - a], float(P), None, ALU.mult))
                link(nc.vector.tensor_scalar(place_f[:, a:z], ps[3 + k][:, 0:z - a], float(AW), None, ALU.mult))
                link(nc.vector.scalar_tensor_tensor(off_f[:, a:z], tile_no[:, a:z], float(P), ps[5 + k][:, 0:z - a],
                                                    ALU.mult, ALU.add))
            link(nc.vector.tensor_scalar(off_f[:, :], off_f[:, :], float(sh.EP - P), None, ALU.min))
            link(nc.vector.tensor_copy(off_i[:, :], off_f[0:1, :]))
            link(nc.vector.tensor_copy(place_i[:, :], place_f[0:1, :]))
            if by_dst:
                link(nc.vector.tensor_scalar(place_f[0:1, :], base_f[0:1, :], 2 * HEADS / P, None, ALU.mult))
                link(nc.vector.tensor_copy(c.node_i[:, :], place_f[0:1, :]))
            with dve.Fori(0, NB) as d:
                nc.vector.tensor_scalar(mask[:, :], key[:, :], digits[:, bass.ds(d, 1)], None,
                                        ALU.is_equal).then_inc(stepped, 1)
                dve.wait_ge(stepped, 4 * d + 1)
                nc.vector.tensor_tensor_scan(run[:, :], allone[:, :], mask[:, :], 0.0, ALU.mult,
                                             ALU.add).then_inc(stepped, 1)
                dve.wait_ge(stepped, 4 * d + 2)
                nc.vector.scalar_tensor_tensor(run[:, :], run[:, :], offs[:, bass.ds(d, 1)], mask[:, :],
                                               ALU.add, ALU.mult).then_inc(stepped, 1)
                dve.wait_ge(stepped, 4 * d + 3)
                nc.vector.tensor_tensor(pos[:, :], pos[:, :], run[:, :], ALU.add).then_inc(stepped, 1)
                dve.wait_ge(stepped, 4 * d + 4)
            link(nc.vector.tensor_copy(pos_i[:, :], pos[:, :]))
            ring = Ring(COLS // HALF, 2)

            def step(i, h):
                t = ring.at(i, h)
                if not (isinstance(i, int) and i == 0):
                    dve.wait_ge((out_a, out_b)[h], 16 * HALF * i)
                col = (2 * i + h) * HALF
                nc.vector.tensor_copy(stage_rec[:, h, :, :], rec[:, bass.ds(col, HALF), :])
                nc.vector.tensor_copy(stage_pos[:, h, :], pos_i[:, bass.ds(col, HALF)]).then_inc(staged, 1)

            ring.run(dve, step)

        @block.tensor
        def _(pe):
            pe.wait_ge(tri, 2)
            pe.wait_ge(counted, NB)
            nc.tensor.matmul(ps[0][:, 0:NB], before[:, :], counts[:, :], start=True, stop=True).then_inc(totals, 1)
            nc.tensor.matmul(ps[1][:, 0:NB], c.ones[:, :], counts[:, :], start=True, stop=True).then_inc(totals, 1)
            nc.tensor.matmul(ps[2][0:NB, 0:1], counts[:, :], c.ones[:, 0:1], start=True, stop=True).then_inc(totals, 1)
            pe.wait_ge(tiled, 1)
            nc.tensor.matmul(ps[2][0:NB, 8:9], upto[0:NB, 0:NB], nt[0:NB, 0:1], start=True, stop=True).then_inc(prefixed, 1)
            pe.wait_ge(listed, 1)
            for k, (a, z) in enumerate(halves):
                nc.tensor.matmul(ps[3 + k][:, 0:z - a], c.ones[0:NB, :], past[0:NB, a:z], start=True, stop=True).then_inc(summed, 1)
                nc.tensor.matmul(ps[5 + k][:, 0:z - a], step_[0:NB, 0:1].to_broadcast([NB, P]), past[0:NB, a:z],
                                 start=True, stop=True).then_inc(summed, 1)


def edge_pass(nc, c, kind, table, width, index_word, mode):
    sh = c.sh
    NT = sh.NT
    base_f, place_i, off_i = c.tiles[kind]
    rec_d = c.rec_dst if kind == "dst" else c.rec_src
    ring = Ring(NT, U)
    lag = 8
    nm = f"{mode}_{index_word}_{kind}"
    cols = {"plain": D + 1, "edge_mlp": D, "attend": AW, "max": 0}[mode]
    with ExitStack() as st:
        sb = lambda name, shape, dt: st.enter_context(nc.sbuf_tensor(f"{name}_{nm}", shape, dt))
        pt = lambda name, shape=(P, 512): st.enter_context(nc.psum_tensor(f"{name}_{nm}", list(shape), F32))
        sem = lambda name: nc.alloc_semaphore(f"{name}_{nm}")
        rec = sb("recs", [P, U, REC], F32)
        rec_i = rec[:, :, :].bitcast(I32)
        got = sb("got", [P, U, HEADS if mode == "max" else AW], F32)
        hot = sb("hot", [P, U, P], BF16 if mode == "max" else F32)
        rec_in = [sem(f"rec_in{s}") for s in range(U)]
        row_in = [sem(f"row_in{s}") for s in range(U)]
        hots, sums, added, start = sem("hots"), sem("sums"), sem("added"), sem("start")
        cleared = sem("cleared")
        if mode == "edge_mlp":
            feat = sb("feat", [3, 4, P], F32)
            msg = sb("msg", [P, 8, D], F32)
            pre = sb("pre", [P, 4, D], F32)
            w1b = sb("w1b", [3, D], F32)
            turned, feats, edged, pres, msgs, w_in = [sem(x) for x in ("turned", "feats", "edged", "pres", "msgs", "w_in")]
            psF = [pt("psF0"), pt("psF1")]
            psE = [pt("psE0"), pt("psE1")]
        if mode == "attend":
            hotT = sb("hotT", [P, 4, P], F32)
            z, zc = sb("z", [P, 4, HEADS], F32), sb("zc", [P, 4, HEADS], F32)
            msg = sb("msg", [P, 8, AW], F32)
            turned, hotTs, nodes, zs, ws, msgs, zchain = [sem(x) for x in ("turned", "hotTs", "nodes", "zs", "ws", "msgs", "zchain")]
            psF = [pt("psF0"), pt("psF1")]
            psN = [pt("psN0"), pt("psN1")]
        if mode == "max":
            out_of = sb("out_of", [P, 4, P], BF16)
            diag = sb("diag", [P, 4, HEADS, P], BF16)
            ident4 = sb("ident4", [P, 4, P], BF16)
            top = sb("top", [P, 4, HEADS], F32)
            diag_a, diag_v, outs_, tops = [sem(x) for x in ("diag_a", "diag_v", "outs", "tops")]
            psM = [pt(f"psM{k}", (P, 1024)) for k in range(4)]
        else:
            psS = [pt(f"psS{k}") for k in range(4)]
        NPS = 4
        block = st.enter_context(nc.Block())

        @block.sync
        def _(sp):
            if mode == "edge_mlp":
                sp.dma_start(w1b[:, :], c.w1t_in[D:D + 3, :]).then_inc(w_in, 16)
            gate = Gate(sp, c.passed["sp"])

            def step(i, u):
                t = ring.at(i, u)
                off = nc.sync.value_load(off_i[0:1, bass.ds(ring.count(t) - 1, 1)], min_val=0, max_val=sh.EP - P)
                if (old := ring.at(i, u, U)) is not None:
                    sp.wait_ge(row_in[u], 16 * (old[0] + 1))
                    gate.step()
                    wait_count(sp, hots, ring.count(old))
                    gate.step()
                    if mode == "edge_mlp":
                        wait_count(sp, turned, ring.count(old))
                        gate.step()
                sp.dma_start(rec[:, u, :], rec_d[bass.ds(off, P), :]).then_inc(rec_in[u], 16)

            ring.run(sp, step)
            if mode == "edge_mlp":
                sp.wait_ge(w_in, 16)

        @block.gpsimd
        def _(pool):
            nc.gpsimd.memset(got[:, :, :], 1.0).then_inc(start, 1)
            pool.wait_ge(start, 1)
            gate = Gate(pool, c.passed["pool"])

            def step(i, u):
                t = ring.at(i, u)
                free = msgs if mode in ("edge_mlp", "attend") else sums
                if (old := ring.at(i, u, U)) is not None:
                    wait_count(pool, free, ring.count(old))
                pool.wait_ge(rec_in[u], 16 * (t[0] + 1))
                gate.step()
                w = HEADS if mode == "max" else width
                nc.gpsimd.indirect_dma_start(got[:, u, 0:w], None, table,
                                             bass.IndirectOffsetOnAxis(rec_i[:, u, index_word:index_word + 1], 0)
                                             ).then_inc(row_in[u], 16)

            ring.run(pool, step)

        @block.vector
        def _(dve):
            if mode == "max":
                for k in range(4):
                    nc.vector.tensor_copy(ident4[:, k, :], c.ident_bf[:, :])
                nc.vector.memset(c.top[:, :, :], -BIG).then_inc(cleared, 1)
            else:
                nc.vector.memset(c.acc[:, :, :], 0.0).then_inc(cleared, 1)
            dve.wait_ge(cleared, 1)

            def add(i, u, back):
                t = ring.at(i, u, back)
                if t is None:
                    return
                place = nc.vector.value_load((c.node_i if mode == "max" else place_i)[0:1, bass.ds(ring.count(t) - 1, 1)], min_val=0, max_val=sh.NB * (2 * HEADS if mode == "max" else AW))
                dve.wait_ge(sums, ring.count(t))
                wait_count(dve, added, ring.count(t, 1))
                if mode == "max":
                    k = t[1] % 4
                    nc.vector.tensor_reduce(top[:, k, :], psM[k][:, :].rearrange("p (h e) -> p h e", e=P),
                                            AX.X, ALU.max).then_inc(tops, 1)
                    dve.wait_ge(tops, ring.count(t))
                    here = c.top[:, :, :].rearrange("p b h -> p (b h)")[:, bass.ds(place, HEADS)]
                    nc.vector.tensor_tensor(here, here, top[:, k, :], ALU.max).then_inc(added, 1)
                else:
                    here = c.acc[:, :, :].rearrange("p b w -> p (b w)")[:, bass.ds(place, cols)]
                    nc.vector.tensor_tensor(here, here, psS[t[1] % NPS][:, 0:cols], ALU.add).then_inc(added, 1)

            def one_hot(i, u):
                t = ring.at(i, u)
                if t is None:
                    return
                dve.wait_ge(rec_in[u], 16 * (t[0] + 1))
                iota = c.iota_bf if mode == "max" else c.iota
                nc.vector.tensor_scalar(hot[:, u, :], iota[:, :], base_f[:, bass.ds(ring.count(t) - 1, 1)],
                                        rec[:, u, 1:2], ALU.add, ALU.is_equal).then_inc(hots, 1)

            if mode == "plain":
                def step(i, u):
                    one_hot(i, u)
                    add(i, u, lag)
            elif mode == "edge_mlp":
                def step(i, u):
                    one_hot(i, u)
                    if (t := ring.at(i, u, 4)) is not None:
                        dve.wait_ge(row_in[t[1]], 16 * (t[0] + 1))
                        dve.wait_ge(edged, ring.count(t))
                        wait_count(dve, msgs, ring.count(t, 4))
                        nc.vector.tensor_tensor(pre[:, t[1] % 4, :], got[:, t[1], 0:D],
                                                psE[t[1] % 2][:, 0:D], ALU.add).then_inc(pres, 1)
                    add(i, u, lag)
            elif mode == "attend":
                def step(i, u):
                    one_hot(i, u)
                    if (t := ring.at(i, u, 4)) is not None:
                        k = t[1] % 4
                        dve.wait_ge(row_in[t[1]], 16 * (t[0] + 1))
                        dve.wait_ge(nodes, ring.count(t))
                        n = psN[k % 2][:, 0:2 * HEADS]
                        q = 4 * (ring.count(t) - 1)
                        wait_count(dve, ws, ring.count(t, 4))
                        nc.vector.tensor_tensor(z[:, k, :], n[:, 0:HEADS], got[:, t[1], D:AW], ALU.add).then_inc(zchain, 1)
                        dve.wait_ge(zchain, q + 1)
                        nc.vector.scalar_tensor_tensor(zc[:, k, :], z[:, k, :], SLOPE, z[:, k, :], ALU.mult, ALU.max).then_inc(zchain, 1)
                        dve.wait_ge(zchain, q + 2)
                        nc.vector.tensor_tensor(zc[:, k, :], zc[:, k, :], n[:, HEADS:2 * HEADS], ALU.subtract).then_inc(zchain, 1)
                        dve.wait_ge(zchain, q + 3)
                        nc.vector.tensor_scalar(zc[:, k, :], zc[:, k, :], 60.0, None, ALU.min).then_inc(zchain, 1)
                    if (t := ring.at(i, u, 6)) is not None:
                        dve.wait_ge(ws, ring.count(t))
                        nc.vector.tensor_tensor(
                            msg[:, t[1] % 8, 0:D].rearrange("p (h d) -> p h d", d=DH),
                            got[:, t[1], 0:D].rearrange("p (h d) -> p h d", d=DH),
                            msg[:, t[1] % 8, D:AW].unsqueeze(2).to_broadcast([P, HEADS, DH]), ALU.mult).then_inc(msgs, 1)
                    add(i, u, lag + 1)
            else:
                def step(i, u):
                    one_hot(i, u)
                    if (t := ring.at(i, u)) is not None:
                        k = u % 4
                        dve.wait_ge(hots, ring.count(t))
                        wait_count(dve, sums, ring.count(t, 4))
                        nc.vector.tensor_scalar(out_of[:, k, :], hot[:, u, :], -1.0, BIG, ALU.add, ALU.mult).then_inc(outs_, 1)
                    if (t := ring.at(i, u, 3)) is not None:
                        k = t[1] % 4
                        dve.wait_ge(row_in[t[1]], 16 * (t[0] + 1))
                        wait_count(dve, sums, ring.count(t, 4))
                        for h in range(HEADS // 2):
                            last = nc.vector.tensor_scalar(diag[:, k, h, :], c.ident_bf[:, :], got[:, t[1], h:h + 1], None, ALU.mult)
                        last.then_inc(diag_v, 1)
                    add(i, u, 5)
            ring.run(dve, step, lag={"max": 5, "attend": lag + 1}.get(mode, lag))

        @block.scalar
        def _(act):
            if mode == "edge_mlp":
                def step(i, u):
                    if (t := ring.at(i, u)) is not None:
                        act.wait_ge(turned, ring.count(t))
                        wait_count(act, edged, ring.count(t, 4))
                        nc.scalar.copy(feat[:, u % 4, :], psF[u % 2][0:3, 0:P]).then_inc(feats, 1)
                    if (t := ring.at(i, u, 4)) is not None:
                        act.wait_ge(pres, ring.count(t))
                        wait_count(act, sums, ring.count(t, 8))
                        nc.scalar.activation(msg[:, t[1] % 8, :], pre[:, t[1] % 4, :], ACT.Relu).then_inc(msgs, 1)
                ring.run(act, step, lag=4)
            elif mode == "attend":
                def step(i, u):
                    if (t := ring.at(i, u)) is not None:
                        act.wait_ge(turned, ring.count(t))
                        wait_count(act, nodes, ring.count(t, 4))
                        nc.scalar.copy(hotT[:, u % 4, :], psF[u % 2][:, 0:P]).then_inc(hotTs, 1)
                    if (t := ring.at(i, u, 4)) is not None:
                        act.wait_ge(zchain, 4 * ring.count(t))
                        wait_count(act, sums, ring.count(t, 8))
                        nc.scalar.activation(msg[:, t[1] % 8, D:AW], zc[:, t[1] % 4, :], ACT.Exp).then_inc(ws, 1)
                ring.run(act, step, lag=4)
            elif mode == "max":
                def step(i, u):
                    if (t := ring.at(i, u, 3)) is not None:
                        k = t[1] % 4
                        act.wait_ge(row_in[t[1]], 16 * (t[0] + 1))
                        wait_count(act, sums, ring.count(t, 4))
                        for h in range(HEADS // 2, HEADS):
                            last = nc.scalar.activation(diag[:, k, h, :], c.ident_bf[:, :], ACT.Copy, scale=got[:, t[1], h:h + 1])
                        last.then_inc(diag_a, 1)
                ring.run(act, step, lag=3)

        @block.tensor
        def _(pe):
            if mode == "edge_mlp":
                pe.wait_ge(w_in, 16)

            def gather_sum(i, u, back, rows, ready):
                t = ring.at(i, u, back)
                if t is None:
                    return
                for s_, n_ in ready(t):
                    pe.wait_ge(s_, n_)
                wait_count(pe, added, ring.count(t, NPS))
                nc.tensor.matmul(psS[t[1] % NPS][:, 0:cols], hot[:, t[1], :], rows(t), start=True, stop=True).then_inc(sums, 1)

            if mode == "plain":
                def step(i, u):
                    gather_sum(i, u, 0, lambda t: got[:, t[1], 0:cols],
                               lambda t: [(row_in[t[1]], 16 * (t[0] + 1)), (hots, ring.count(t))])
                ring.run(pe, step)
            elif mode == "edge_mlp":
                def step(i, u):
                    if (t := ring.at(i, u)) is not None:
                        pe.wait_ge(rec_in[u], 16 * (t[0] + 1))
                        wait_count(pe, feats, ring.count(t, 2))
                        nc.tensor.transpose(psF[u % 2][0:3, 0:P], rec[:, u, 2:5], c.ident[:, :]).then_inc(turned, 1)
                    if (t := ring.at(i, u, 2)) is not None:
                        pe.wait_ge(feats, ring.count(t))
                        wait_count(pe, pres, ring.count(t, 2))
                        nc.tensor.matmul(psE[t[1] % 2][:, 0:D], feat[:, t[1] % 4, :], w1b[:, :], start=True, stop=True).then_inc(edged, 1)
                    gather_sum(i, u, 6, lambda t: msg[:, t[1] % 8, :],
                               lambda t: [(msgs, ring.count(t)), (hots, ring.count(t))])
                ring.run(pe, step, lag=6)
            elif mode == "attend":
                def step(i, u):
                    if (t := ring.at(i, u)) is not None:
                        pe.wait_ge(hots, ring.count(t))
                        wait_count(pe, hotTs, ring.count(t, 2))
                        nc.tensor.transpose(psF[u % 2][:, 0:P], hot[:, u, :], c.ident[:, :]).then_inc(turned, 1)
                    if (t := ring.at(i, u, 2)) is not None:
                        k = t[1] % 4
                        place = nc.tensor.value_load(c.node_i[0:1, bass.ds(ring.count(t) - 1, 1)], min_val=0, max_val=sh.NB * 16)
                        pe.wait_ge(hotTs, ring.count(t))
                        wait_count(pe, zchain, None if ring.count(t, 2) is None else 4 * ring.count(t, 2))
                        nc.tensor.matmul(psN[k % 2][:, 0:2 * HEADS], hotT[:, k, :],
                                         c.node[:, :, :].rearrange("p b w -> p (b w)")[:, bass.ds(place, 16)],
                                         start=True, stop=True).then_inc(nodes, 1)
                    gather_sum(i, u, 7, lambda t: msg[:, t[1] % 8, :],
                               lambda t: [(msgs, ring.count(t))])
                ring.run(pe, step, lag=7)
            else:
                def step(i, u):
                    if (t := ring.at(i, u, 4)) is not None:
                        k = t[1] % 4
                        ps = psM[k]
                        pe.wait_ge(outs_, ring.count(t))
                        wait_count(pe, tops, ring.count(t, 4))
                        pe.wait_ge(diag_v, ring.count(t))
                        pe.wait_ge(diag_a, ring.count(t))
                        for half in range(2):
                            o = ps[:, 512 * half:512 * half + 512]
                            nc.tensor.matmul(o, out_of[:, k, :], ident4[:, :, :], start=True, stop=False)
                            last = nc.tensor.matmul(o, hot[:, t[1], :], diag[:, k, 4 * half:4 * half + 4, :], start=False, stop=True)
                        last.then_inc(sums, 1)
                ring.run(pe, step, lag=4)


def norm_steps(nc, c, dve, gate, ring, i, buf, stated):
    stats, moments = buf
    G = ring.size
    for u in range(G):
        last = nc.vector.bn_stats(stats[:, u, :], c.x[:, bass.ds(G * i + u, 1), :].rearrange("p a d -> p (a d)"))
    last.then_inc(stated, 1)
    dve.wait_ge(stated, 3 * i + 1)
    gate.step()
    for u in range(G):
        last = nc.vector.bn_aggr(moments[:, u, :], stats[:, u, :])
    last.then_inc(stated, 1)
    dve.wait_ge(stated, 3 * i + 2)
    nc.vector.tensor_copy(c.stat[:, bass.ds(G * i, G), :], moments[:, :, :]).then_inc(stated, 1)
    dve.wait_ge(stated, 3 * i + 3)
    gate.step()


def norm_ends(nc, c, dve, roots):
    begun, rooted, ended = roots
    nc.vector.tensor_scalar(c.rstd[:, :], c.stat[:, :, 1], EPS, None, ALU.add).then_inc(begun, 1)
    dve.wait_ge(rooted, 1)
    nc.vector.reciprocal(c.rstd[:, :], c.rstd[:, :]).then_inc(ended, 1)
    dve.wait_ge(ended, 1)
    nc.vector.scalar_tensor_tensor(c.nbias[:, :], c.stat[:, :, 0], -1.0, c.rstd[:, :], ALU.mult, ALU.mult)


def norm_roots(nc, c, act, roots):
    begun, rooted, ended = roots
    act.wait_ge(begun, 1)
    nc.scalar.sqrt(c.rstd[:, :], c.rstd[:, :]).then_inc(rooted, 1)


def row(ap, n):
    return ap.rearrange("(a n) -> a n", a=1).to_broadcast([P, n])


def stats_stage(nc, c):
    sh = c.sh
    ring = Ring(sh.NB, 7)
    nm = f"st{c.stage()}"
    with ExitStack() as st:
        sb = lambda name, shape, dt=F32: st.enter_context(nc.sbuf_tensor(f"{name}_{nm}", shape, dt))
        stats, moments = sb("stats", [P, 7, 6]), sb("moments", [P, 7, 2])
        stated = nc.alloc_semaphore(f"stated_{nm}")
        roots = [nc.alloc_semaphore(f"{x}_{nm}") for x in ("begun", "rooted", "ended")]
        block = st.enter_context(nc.Block())

        @block.vector
        def _(dve):
            gate = Gate(dve, c.passed["dve"])
            with dve.Fori(0, ring.rounds) as i:
                norm_steps(nc, c, dve, gate, ring, i, (stats, moments), stated)
            norm_ends(nc, c, dve, roots)

        @block.scalar
        def _(act):
            norm_roots(nc, c, act, roots)


def table_stage(nc, c, layer):
    sh = c.sh
    G = 7
    ring = Ring(sh.NB, G)
    nm = f"tab{layer}"
    width = {0: D, 1: NREL * D, 2: D + 2 * HEADS, 3: D}[layer]
    blocks = [(a, min(a + 512, width)) for a in range(0, width, 512)]
    NBK = len(blocks)
    with ExitStack() as st:
        sb = lambda name, shape, dt=F32: st.enter_context(nc.sbuf_tensor(f"{name}_{nm}", shape, dt))
        pt = lambda name: st.enter_context(nc.psum_tensor(f"{name}_{nm}", [P, 512], F32))
        sem = lambda name: nc.alloc_semaphore(f"{name}_{nm}")
        w = sb("w", [P, 2, width])
        h = sb("h", [P, G, D])
        hT = sb("hT", [P, G, D])
        SL = G if width < 512 else 3
        out = sb("out", [P, SL, width])
        bias = sb("bias", [P, D])
        att = sb("att", [P, 2, D]) if layer == 2 else None
        prod = sb("prod", [P, 2, D]) if layer == 2 else None
        psT = [pt("psT0"), pt("psT1")]
        psO = [pt(f"psO{k}") for k in range(4)]
        w_in, w_made, hs, turned, hTs, made, outs, noted = [
            sem(x) for x in ("w_in", "w_made", "hs", "turned", "hTs", "made", "outs", "noted")]
        left = [sem(f"left{s}") for s in range(SL)]
        block = st.enter_context(nc.Block())

        def slot(t):
            return t[1] % SL

        @block.sync
        def _(sp):
            n = 0
            if layer == 0:
                sp.dma_start(w[:, :, :], c.w1t_in[0:D, :].rearrange("(k p) n -> p k n", p=P)).then_inc(w_in, 16)
                sp.dma_start(bias[:, :], row(c.b1_in, D)).then_inc(w_in, 16)
                n = 2
            elif layer == 1:
                for r in range(NREL):
                    sp.dma_start(w[:, :, r * D:(r + 1) * D],
                                 c.wrel_in[r, :, :].rearrange("(k p) n -> p k n", p=P)).then_inc(w_in, 16)
                n = NREL
            elif layer == 2:
                sp.dma_start(w[:, :, 0:D], c.watt_in.rearrange("(k p) n -> p k n", p=P)).then_inc(w_in, 16)
                sp.dma_start(att[:, 0, :], row(c.att_src_in.rearrange("h d -> (h d)"), D)).then_inc(w_in, 16)
                sp.dma_start(att[:, 1, :], row(c.att_dst_in.rearrange("h d -> (h d)"), D)).then_inc(w_in, 16)
                n = 3
            if n:
                sp.wait_ge(w_in, 16 * n)

            def step(i, u):
                t = ring.at(i, u)
                T = ring.count(t) - 1
                rows = sh.LAST if isinstance(T, int) and T == sh.NB - 1 else P
                s = slot(t)
                sp.wait_ge(outs, NBK * ring.count(t))
                if layer == 1:
                    to = c.xtab.rearrange("(r n) d -> n r d", r=NREL)[bass.ds(P * T, rows), :, :]
                    sp.dma_start(to, out[0:rows, s, :].rearrange("p (r d) -> p r d", d=D)).then_inc(left[s], 16)
                elif layer == 2:
                    sp.dma_start(c.gtab[bass.ds(P * T, rows), :], out[0:rows, s, 0:AW]).then_inc(left[s], 16)
                    sp.dma_start(c.stab[bass.ds(P * T, rows), :], out[0:rows, s, D:AW]).then_inc(left[s], 16)
                else:
                    to = c.ptab if layer == 0 else c.htab
                    sp.dma_start(to[bass.ds(P * T, rows), :], out[0:rows, s, :]).then_inc(left[s], 16)

            ring.run(sp, step)
            for s in range(SL):
                per = len([u for u in range(G) if u % SL == s]) * ring.rounds
                sp.wait_ge(left[s], 16 * per * (2 if layer == 2 else 1))

        def wait_left(eng, t):
            s = slot(t)
            per = len([u for u in range(G) if u % SL == s])
            n = per * t[0] + t[1] // SL
            if isinstance(n, int) and n <= 0:
                return
            eng.wait_ge(left[s], (32 if layer == 2 else 16) * n)

        @block.scalar
        def _(act):
            def step(i, u):
                if (t := ring.at(i, u)) is not None:
                    T = ring.count(t) - 1
                    if layer == 3:
                        wait_left(act, t)
                    else:
                        wait_count(act, turned, ring.count(t, G))
                    nc.scalar.activation(h[:, u, :], c.x[:, bass.ds(T, 1), :].rearrange("p a d -> p (a d)"), ACT.Relu,
                                         bias=c.nbias[:, bass.ds(T, 1)], scale=c.rstd[:, bass.ds(T, 1)]).then_inc(hs, 1)
                if layer != 3 and (t := ring.at(i, u, 2)) is not None:
                    act.wait_ge(turned, ring.count(t))
                    wait_count(act, made, ring.count(t, G - 2))
                    nc.scalar.copy(hT[:, t[1], :], psT[t[1] % 2][:, 0:D]).then_inc(hTs, 1)
            ring.run(act, step, lag=2)

        @block.vector
        def _(dve):
            if layer == 2:
                dve.wait_ge(w_in, 48)
                n = 0
                for a in range(2):
                    for k in range(2):
                        nc.vector.tensor_tensor(prod[:, k, :], w[:, k, 0:D], att[:, a, :], ALU.mult).then_inc(w_made, 1)
                        n += 1
                        dve.wait_ge(w_made, n)
                        nc.vector.tensor_reduce(w[:, k, D + HEADS * a:D + HEADS * (a + 1)],
                                                prod[:, k, :].rearrange("p (h d) -> p h d", d=DH), AX.X, ALU.add).then_inc(w_made, 1)
                        n += 1
                        dve.wait_ge(w_made, n)

            def step(i, u):
                t = ring.at(i, u)
                T = ring.count(t) - 1
                wait_left(dve, t)
                if layer == 3:
                    dve.wait_ge(hs, ring.count(t))
                    nc.vector.tensor_scalar(out[:, slot(t), :], h[:, u, :], c.dinv[:, bass.ds(T, 1)], None, ALU.mult).then_inc(outs, 1)
                    return
                if layer == 0:
                    dve.wait_ge(w_in, 32)
                for b, (a, z) in enumerate(blocks):
                    dve.wait_ge(made, NBK * (ring.count(t) - 1) + b + 1)
                    ps = psO[(NBK * u + b) % 4][:, 0:z - a]
                    o = out[:, slot(t), a:z]
                    if layer == 0:
                        last = nc.vector.tensor_tensor(o, ps, bias[:, :], ALU.add)
                    else:
                        last = nc.vector.tensor_copy(o, ps)
                    last.then_inc(outs, 1)
                if layer == 2:
                    nc.vector.tensor_copy(c.node[:, bass.ds(T, 1), 0:2 * HEADS].rearrange("p a w -> p (a w)"),
                                          ps[:, D:D + 2 * HEADS]).then_inc(noted, 1)
            ring.run(dve, step)

        if layer == 3:
            return

        @block.tensor
        def _(pe):
            if layer == 2:
                pe.wait_ge(w_made, 8)
            pe.wait_ge(w_in, {0: 32, 1: 16 * NREL, 2: 48}[layer])

            def step(i, u):
                if (t := ring.at(i, u)) is not None:
                    pe.wait_ge(hs, ring.count(t))
                    wait_count(pe, hTs, ring.count(t, 1 if u == 0 else 2))
                    for k in range(2):
                        last = nc.tensor.transpose(psT[u % 2][:, k * P:(k + 1) * P], h[:, u, k * P:(k + 1) * P], c.ident[:, :])
                    last.then_inc(turned, 1)
                if (t := ring.at(i, u, 1)) is not None:
                    pe.wait_ge(hTs, ring.count(t))
                    for b, (a, z) in enumerate(blocks):
                        n = NBK * (ring.count(t) - 1) + b
                        back = 4 if NBK * t[1] + b >= 4 else (4 if (NBK * G) % 4 == 0 else (NBK * t[1] + b) + 1)
                        if not (isinstance(n, int) and n - back + 1 <= 0):
                            pe.wait_ge(outs, n - back + 1)
                            if layer == 2:
                                pe.wait_ge(noted, n - back + 1)
                        for k in range(2):
                            last = nc.tensor.matmul(psO[(NBK * t[1] + b) % 4][:, 0:z - a], hT[:, t[1], k * P:(k + 1) * P],
                                                    w[:, k, a:z], start=(k == 0), stop=(k == 1))
                        last.then_inc(made, 1)
            ring.run(pe, step, lag=1)


def sage_update(nc, c):
    sh = c.sh
    G = 7
    ring = Ring(sh.NB, G)
    with ExitStack() as st:
        sb = lambda name, shape, dt=F32: st.enter_context(nc.sbuf_tensor(f"{name}_sage", shape, dt))
        pt = lambda name: st.enter_context(nc.psum_tensor(f"{name}_sage", [P, 512], F32))
        sem = lambda name: nc.alloc_semaphore(f"{name}_sage")
        w = sb("w", [P, 4, D])
        hn = sb("hn", [P, G, 2 * D])
        hnT = sb("hnT", [P, G, 2 * D])
        r, sq = sb("r", [P, G, D]), sb("sq", [P, G, D])
        ss, nrm = sb("ss", [P, G]), sb("nrm", [P, G])
        stats, moments = sb("stats", [P, G, 6]), sb("moments", [P, G, 2])
        psT = [pt("psT0"), pt("psT1")]
        psO = [pt("psO0"), pt("psO1")]
        w_in, hns, turned, turned_back, made, rs, sqs, step_, stated = [sem(x) for x in (
            "w_in", "hns", "turned", "turned_back", "made", "rs", "sqs", "step_", "stated")]
        rooted = sem("rooted")
        roots = [sem(x) for x in ("begun", "rooted_all", "ended")]
        block = st.enter_context(nc.Block())

        @block.sync
        def _(sp):
            sp.dma_start(w[:, :, :], c.w2t_in.rearrange("(k p) n -> p k n", p=P)).then_inc(w_in, 16)
            sp.wait_ge(w_in, 16)

        @block.scalar
        def _(act):
            def step(i, u):
                if (t := ring.at(i, u)) is not None:
                    T = ring.count(t) - 1
                    wait_count(act, turned, ring.count(t, G))
                    nc.scalar.activation(hn[:, u, 0:D], c.x[:, bass.ds(T, 1), :].rearrange("p a d -> p (a d)"), ACT.Relu,
                                         bias=c.nbias[:, bass.ds(T, 1)], scale=c.rstd[:, bass.ds(T, 1)])
                    nc.scalar.copy(hn[:, u, D:2 * D], c.acc[:, bass.ds(T, 1), 0:D].rearrange("p a d -> p (a d)")).then_inc(hns, 1)
                if (t := ring.at(i, u, 4)) is not None:
                    act.wait_ge(made, ring.count(t))
                    if not (isinstance(t[0], int) and t[0] == 0):
                        act.wait_ge(step_, 3 * t[0])
                    nc.scalar.activation(r[:, t[1], :], psO[t[1] % 2][:, 0:D], ACT.Relu).then_inc(rs, 1)
                    act.wait_ge(rs, ring.count(t))
                    nc.scalar.activation(sq[:, t[1], :], r[:, t[1], :], ACT.Square,
                                         accum_out=ss[:, t[1]:t[1] + 1]).then_inc(sqs, 1)
                    if t[1] == G - 1:
                        act.wait_ge(sqs, ring.count(t))
                        nc.scalar.sqrt(nrm[:, :], ss[:, :]).then_inc(rooted, 1)
            ring.run(act, step, lag=4)
            norm_roots(nc, c, act, roots)

        @block.tensor
        def _(pe):
            pe.wait_ge(w_in, 16)

            def step(i, u):
                if (t := ring.at(i, u)) is not None:
                    pe.wait_ge(hns, ring.count(t))
                    wait_count(pe, turned_back, ring.count(t, 1 if u == 0 else 2))
                    for k in range(4):
                        last = nc.tensor.transpose(psT[u % 2][:, k * P:(k + 1) * P], hn[:, u, k * P:(k + 1) * P], c.ident[:, :])
                    last.then_inc(turned, 1)
                if (t := ring.at(i, u, 2)) is not None:
                    pe.wait_ge(turned_back, ring.count(t))
                    wait_count(pe, rs, ring.count(t, 1 if t[1] == 0 else 2))
                    for k in range(4):
                        last = nc.tensor.matmul(psO[t[1] % 2][:, 0:D], hnT[:, t[1], k * P:(k + 1) * P], w[:, k, :],
                                                start=(k == 0), stop=(k == 3))
                    last.then_inc(made, 1)
            ring.run(pe, step, lag=2)

        @block.vector
        def _(dve):
            def round_end(i):
                dve.wait_ge(rooted, i + 1)
                nc.vector.tensor_scalar(nrm[:, :], nrm[:, :], 1e-12, None, ALU.max).then_inc(step_, 1)
                dve.wait_ge(step_, 3 * i + 1)
                nc.vector.reciprocal(nrm[:, :], nrm[:, :]).then_inc(step_, 1)
                dve.wait_ge(step_, 3 * i + 2)
                for s in range(G):
                    here = c.x[:, bass.ds(G * i + s, 1), :].rearrange("p a d -> p (a d)")
                    last = nc.vector.scalar_tensor_tensor(here, r[:, s, :], nrm[:, s:s + 1], here, ALU.mult, ALU.add)
                last.then_inc(step_, 1)
                dve.wait_ge(step_, 3 * i + 3)
                gate.step()
                norm_steps(nc, c, dve, gate, ring, i, (stats, moments), stated)

            gate = Gate(dve, c.passed["dve"])
            with dve.Fori(0, ring.rounds) as i:
                for s in range(G):
                    t = (i, s)
                    dve.wait_ge(turned, ring.count(t))
                    nc.vector.tensor_copy(hnT[:, s, :], psT[s % 2][:, :]).then_inc(turned_back, 1)
                round_end(i)
            norm_ends(nc, c, dve, roots)


def rgcn_update(nc, c):
    sh = c.sh
    G = 7
    ring = Ring(sh.NB, G)
    with ExitStack() as st:
        sb = lambda name, shape, dt=F32: st.enter_context(nc.sbuf_tensor(f"{name}_rgcn", shape, dt))
        sem = lambda name: nc.alloc_semaphore(f"{name}_rgcn")
        bias = sb("bias", [P, D])
        t1, t2 = sb("t1", [P, G, D]), sb("t2", [P, G, D])
        deg, pos, = sb("deg", [P, sh.NB]), sb("pos", [P, sh.NB])
        stats, moments = sb("stats", [P, G, 6]), sb("moments", [P, G, 2])
        b_in, degs, rooted, t1s, t2s, xs, stated = [sem(x) for x in ("b_in", "degs", "rooted", "t1s", "t2s", "xs", "stated")]
        roots = [sem(x) for x in ("begun", "rooted_all", "ended")]
        block = st.enter_context(nc.Block())

        @block.sync
        def _(sp):
            sp.dma_start(bias[:, :], row(c.bias1_in, D)).then_inc(b_in, 16)
            sp.wait_ge(b_in, 16)

        @block.scalar
        def _(act):
            act.wait_ge(degs, 1)
            nc.scalar.sqrt(deg[:, :], deg[:, :]).then_inc(rooted, 1)
            with act.Fori(0, ring.rounds) as i:
                for s in range(G):
                    act.wait_ge(t1s, G * i + s + 1)
                    if s == 0:
                        act.wait_ge(xs, i)
                    nc.scalar.activation(t2[:, s, :], t1[:, s, :], ACT.Relu).then_inc(t2s, 1)
            norm_roots(nc, c, act, roots)

        @block.vector
        def _(dve):
            gate = Gate(dve, c.passed["dve"])
            counts = c.acc[:, 0:sh.NB, D]
            nc.vector.tensor_scalar(deg[:, :], counts, 1.0, None, ALU.max).then_inc(degs, 1)
            nc.vector.tensor_scalar(pos[:, :], counts, 0.0, None, ALU.is_gt).then_inc(degs, 1)
            dve.wait_ge(rooted, 1)
            nc.vector.reciprocal(deg[:, :], deg[:, :]).then_inc(degs, 1)
            dve.wait_ge(degs, 3)
            nc.vector.tensor_tensor(c.dinv[:, :], deg[:, :], pos[:, :], ALU.mult)
            dve.wait_ge(b_in, 16)
            with dve.Fori(0, ring.rounds) as i:
                dve.wait_ge(t2s, G * i)
                for s in range(G):
                    nc.vector.tensor_tensor(t1[:, s, :], c.acc[:, bass.ds(G * i + s, 1), 0:D].rearrange("p a d -> p (a d)"),
                                            bias[:, :], ALU.add).then_inc(t1s, 1)
                for s in range(G):
                    dve.wait_ge(t2s, G * i + s + 1)
                    here = c.x[:, bass.ds(G * i + s, 1), :].rearrange("p a d -> p (a d)")
                    last = nc.vector.tensor_tensor(here, here, t2[:, s, :], ALU.add)
                last.then_inc(xs, 1)
                dve.wait_ge(xs, i + 1)
                gate.step()
                norm_steps(nc, c, dve, gate, ring, i, (stats, moments), stated)
            norm_ends(nc, c, dve, roots)


def attention_guard(nc, c):
    sh = c.sh
    with ExitStack() as st:
        sb = lambda name, shape, dt=F32: st.enter_context(nc.sbuf_tensor(f"{name}_guard", shape, dt))
        m, z = sb("m", [P, sh.NB, HEADS]), sb("z", [P, sh.NB, HEADS])
        chain, zs = nc.alloc_semaphore("chain_guard"), nc.alloc_semaphore("zs_guard")
        block = st.enter_context(nc.Block())
        a_src, a_dst = c.node[:, 0:sh.NB, 0:HEADS], c.node[:, 0:sh.NB, HEADS:2 * HEADS]
        top = c.top[:, 0:sh.NB, 0:HEADS]

        @block.vector
        def _(dve):
            n = [0]

            def link(instruction):
                n[0] += 1
                instruction.then_inc(chain, 1)
                dve.wait_ge(chain, n[0])

            nc.vector.tensor_copy(c.own[:, :, :], a_src)
            link(nc.vector.tensor_tensor(m[:, :, :], top, a_src, ALU.max))
            link(nc.vector.tensor_tensor(m[:, :, :], m[:, :, :], a_dst, ALU.add))
            link(nc.vector.tensor_tensor(z[:, :, :], a_src, a_dst, ALU.add))
            link(nc.vector.scalar_tensor_tensor(m[:, :, :], m[:, :, :], SLOPE, m[:, :, :], ALU.mult, ALU.max))
            link(nc.vector.scalar_tensor_tensor(z[:, :, :], z[:, :, :], SLOPE, z[:, :, :], ALU.mult, ALU.max))
            link(nc.vector.tensor_tensor(z[:, :, :], z[:, :, :], m[:, :, :], ALU.subtract))
            link(nc.vector.tensor_copy(c.node[:, 0:sh.NB, 0:HEADS], a_dst))
            nc.vector.tensor_copy(c.node[:, 0:sh.NB, HEADS:2 * HEADS], m[:, :, :]).then_inc(zs, 1)
            nc.vector.memset(c.node[:, sh.NB, :], 0.0)

        @block.scalar
        def _(act):
            act.wait_ge(zs, 1)
            nc.scalar.activation(c.own[:, :, :], z[:, :, :], ACT.Exp)


def attention_update(nc, c):
    sh = c.sh
    G = 7
    ring = Ring(sh.NB, G)
    N = sh.N
    with ExitStack() as st:
        sb = lambda name, shape, dt=F32: st.enter_context(nc.sbuf_tensor(f"{name}_gat", shape, dt))
        pt = lambda name: st.enter_context(nc.psum_tensor(f"{name}_gat", [P, 512], F32))
        sem = lambda name: nc.alloc_semaphore(f"{name}_gat")
        own_row = sb("own_row", [P, G, AW])
        prod = sb("prod", [P, G, D])
        sq, h = sb("sq", [P, G, D]), sb("h", [P, G, D])
        bias, gamma, beta = sb("bias", [P, D]), sb("gamma", [P, D]), sb("beta", [P, D])
        mean, scale = sb("mean", [P, D]), sb("scale", [P, D])
        rden = sb("rden", [P, sh.NB, HEADS])
        stats, moments = sb("stats", [P, G, 6]), sb("moments", [P, G, 2])
        psM, psV = pt("psM"), pt("psV")
        par_in, rowed, chain, summed, centred, squared, varied, hs, xs, stated, freed = [sem(x) for x in (
            "par_in", "rowed", "chain", "summed", "centred", "squared", "varied", "hs", "xs", "stated", "freed")]
        zeroed, varied_rows = sem("zeroed"), sem("varied_rows")
        roots = [sem(x) for x in ("begun", "rooted_all", "ended")]
        var_in, var_root = sem("var_in"), sem("var_root")
        own_in = [sem(f"own_in{s}") for s in range(G)]
        block = st.enter_context(nc.Block())
        flat = lambda ap: ap.rearrange("p a d -> p (a d)")
        heads = lambda ap: ap.rearrange("p (h d) -> p h d", d=DH)
        spread = lambda ap: ap.rearrange("p a h -> p (a h)").unsqueeze(2).to_broadcast([P, HEADS, DH])

        @block.sync
        def _(sp):
            for to, of in ((bias, c.bias2_in), (gamma, c.gamma_in), (beta, c.beta_in)):
                sp.dma_start(to[:, :], row(of, D)).then_inc(par_in, 16)
            sp.wait_ge(zeroed, 1)

            def step(i, u):
                t = ring.at(i, u)
                T = ring.count(t) - 1
                rows = sh.LAST if isinstance(T, int) and T == sh.NB - 1 else P
                wait_count(sp, freed, ring.count(t, G))
                sp.dma_start(own_row[0:rows, u, :], c.gtab[bass.ds(P * T, rows), :]).then_inc(own_in[u], 16)
            ring.run(sp, step)
            sp.wait_ge(par_in, 48)

        @block.vector
        def _(dve):
            gate = Gate(dve, c.passed["dve"])
            nc.vector.memset(own_row[:, :, :], 0.0).then_inc(zeroed, 1)
            nc.vector.tensor_tensor(rden[:, :, :], c.acc[:, 0:sh.NB, D:AW], c.own[:, :, :], ALU.add).then_inc(chain, 1)
            dve.wait_ge(chain, 1)
            nc.vector.reciprocal(rden[:, :, :], rden[:, :, :]).then_inc(chain, 1)
            dve.wait_ge(chain, 2)
            dve.wait_ge(par_in, 48)

            def mean_rows(i):
                dve.wait_ge(rowed, 3 * i)
                for s in range(G):
                    dve.wait_ge(own_in[s], 16 * (i + 1))
                    nc.vector.tensor_tensor(heads(prod[:, s, :]), heads(own_row[:, s, 0:D]),
                                            spread(c.own[:, bass.ds(G * i + s, 1), :]), ALU.mult).then_inc(freed, 1)
                dve.wait_ge(freed, G * i + G)
                for s in range(G):
                    last = nc.vector.tensor_tensor(prod[:, s, :], prod[:, s, :], flat(c.acc[:, bass.ds(G * i + s, 1), 0:D]), ALU.add)
                last.then_inc(rowed, 1)
                dve.wait_ge(rowed, 3 * i + 1)
                for s in range(G):
                    last = nc.vector.tensor_tensor(heads(prod[:, s, :]), heads(prod[:, s, :]),
                                                   spread(rden[:, bass.ds(G * i + s, 1), :]), ALU.mult)
                last.then_inc(rowed, 1)
                dve.wait_ge(rowed, 3 * i + 2)
                for s in range(G):
                    last = nc.vector.tensor_tensor(flat(c.acc[:, bass.ds(G * i + s, 1), 0:D]), prod[:, s, :], bias[:, :], ALU.add)
                last.then_inc(rowed, 1)

            with dve.Fori(0, ring.rounds) as i:
                mean_rows(i)
            dve.wait_ge(summed, 1)
            nc.vector.tensor_scalar(mean[:, :], psM[:, 0:D], 1.0 / N, None, ALU.mult).then_inc(chain, 1)
            dve.wait_ge(chain, 3)
            with dve.Fori(0, sh.NB) as T:
                here = flat(c.acc[:, bass.ds(T, 1), 0:D])
                nc.vector.tensor_tensor(here, here, mean[:, :], ALU.subtract).then_inc(centred, 1)
            dve.wait_ge(varied, 1)
            nc.vector.tensor_scalar(scale[:, :], psV[:, 0:D], 1.0 / N, EPS, ALU.mult, ALU.add).then_inc(var_in, 1)
            dve.wait_ge(var_root, 1)
            nc.vector.reciprocal(scale[:, :], scale[:, :]).then_inc(chain, 1)
            dve.wait_ge(chain, 4)
            nc.vector.tensor_tensor(scale[:, :], scale[:, :], gamma[:, :], ALU.mult).then_inc(chain, 1)
            dve.wait_ge(chain, 5)
            dve.wait_ge(centred, sh.NB)
            with dve.Fori(0, ring.rounds) as i:
                dve.wait_ge(xs, 3 * i)
                for s in range(G):
                    nc.vector.tensor_tensor(prod[:, s, :], flat(c.acc[:, bass.ds(G * i + s, 1), 0:D]), scale[:, :], ALU.mult)
                    dve.wait_ge(hs, G * i + s + 1)
                    here = flat(c.x[:, bass.ds(G * i + s, 1), :])
                    last = nc.vector.tensor_tensor(here, here, h[:, s, :], ALU.add)
                last.then_inc(xs, 1)
                dve.wait_ge(xs, 3 * i + 1)
                for s in range(G):
                    last = nc.vector.tensor_tensor(prod[:, s, :], prod[:, s, :], beta[:, :], ALU.add)
                last.then_inc(xs, 1)
                dve.wait_ge(xs, 3 * i + 2)
                for s in range(G):
                    here = flat(c.x[:, bass.ds(G * i + s, 1), :])
                    last = nc.vector.tensor_tensor(here, here, prod[:, s, :], ALU.add)
                last.then_inc(xs, 1)
                dve.wait_ge(xs, 3 * i + 3)
                gate.step()
                norm_steps(nc, c, dve, gate, ring, i, (stats, moments), stated)
            norm_ends(nc, c, dve, roots)

        @block.scalar
        def _(act):
            with act.Fori(0, ring.rounds) as i:
                for s in range(G):
                    act.wait_ge(centred, G * i + s + 1)
                    if s == 0:
                        act.wait_ge(varied_rows, G * i)
                    nc.scalar.activation(sq[:, s, :], flat(c.acc[:, bass.ds(G * i + s, 1), 0:D]), ACT.Square).then_inc(squared, 1)
            act.wait_ge(var_in, 1)
            nc.scalar.sqrt(scale[:, :], scale[:, :]).then_inc(var_root, 1)
            with act.Fori(0, ring.rounds) as i:
                act.wait_ge(xs, 3 * i)
                for s in range(G):
                    T = G * i + s
                    nc.scalar.activation(h[:, s, :], flat(c.x[:, bass.ds(T, 1), :]), ACT.Relu,
                                         bias=c.nbias[:, bass.ds(T, 1)], scale=c.rstd[:, bass.ds(T, 1)]).then_inc(hs, 1)
            norm_roots(nc, c, act, roots)

        @block.tensor
        def _(pe):
            def over_nodes(rows_of, ps, ready, done, each):
                def step(i, u):
                    t = ring.at(i, u)
                    T = ring.count(t) - 1
                    rows = sh.LAST if isinstance(T, int) and T == sh.NB - 1 else P
                    ready(t)
                    last = nc.tensor.matmul(ps[:, 0:D], c.ones[0:rows, :], rows_of(T, u, rows),
                                            start=isinstance(T, int) and T == 0, stop=isinstance(T, int) and T == sh.NB - 1,
                                            skip_group_check=True)
                    if each is not None:
                        last.then_inc(each, 1)
                ring.run(pe, step)
                nc.tensor.matmul(ps[:, 256:258], c.ones[:, :], c.ones[:, 0:2], start=False, stop=True,
                                 skip_group_check=True).then_inc(done, 1)

            over_nodes(lambda T, u, rows: c.acc[0:rows, bass.ds(T, 1), 0:D].rearrange("p a d -> p (a d)"), psM,
                       lambda t: pe.wait_ge(rowed, 3 * t[0] + 3) if t[1] == 0 else None, summed, None)
            over_nodes(lambda T, u, rows: sq[0:rows, u, :], psV,
                       lambda t: pe.wait_ge(squared, ring.count(t)), varied, varied_rows)


def gcn_output(nc, c):
    sh = c.sh
    G = 7
    ring = Ring(sh.NB, G)
    with ExitStack() as st:
        sb = lambda name, shape, dt=F32: st.enter_context(nc.sbuf_tensor(f"{name}_gcn", shape, dt))
        pt = lambda name: st.enter_context(nc.psum_tensor(f"{name}_gcn", [P, 512], F32))
        sem = lambda name: nc.alloc_semaphore(f"{name}_gcn")
        w, bias = sb("w", [P, 2, D]), sb("bias", [P, D])
        a, aT = sb("a", [P, G, D]), sb("aT", [P, G, D])
        y, z = sb("y", [P, G, D]), sb("z", [P, G, D])
        psT = [pt("psT0"), pt("psT1")]
        psO = [pt("psO0"), pt("psO1")]
        w_in, scaled, turned, aTs, made, ys, zs, outs = [sem(x) for x in (
            "w_in", "scaled", "turned", "aTs", "made", "ys", "zs", "outs")]
        left = [sem(f"left{s}") for s in range(G)]
        block = st.enter_context(nc.Block())
        flat = lambda ap: ap.rearrange("p a d -> p (a d)")

        @block.sync
        def _(sp):
            sp.dma_start(w[:, :, :], c.w3_in.rearrange("(k p) n -> p k n", p=P)).then_inc(w_in, 16)
            sp.dma_start(bias[:, :], row(c.bias3_in, D)).then_inc(w_in, 16)

            def step(i, u):
                t = ring.at(i, u)
                T = ring.count(t) - 1
                rows = sh.LAST if isinstance(T, int) and T == sh.NB - 1 else P
                sp.wait_ge(outs, ring.count(t))
                sp.dma_start(c.out[bass.ds(P * T, rows), :], z[0:rows, u, :]).then_inc(left[u], 16)
            ring.run(sp, step)
            sp.wait_ge(w_in, 32)
            for s in range(G):
                sp.wait_ge(left[s], 16 * ring.rounds)

        @block.scalar
        def _(act):
            def step(i, u):
                if (t := ring.at(i, u)) is not None:
                    T = ring.count(t) - 1
                    wait_count(act, turned, ring.count(t, G))
                    nc.scalar.activation(a[:, u, :], flat(c.acc[:, bass.ds(T, 1), 0:D]), ACT.Copy,
                                         scale=c.dinv[:, bass.ds(T, 1)]).then_inc(scaled, 1)
                if (t := ring.at(i, u, 2)) is not None:
                    act.wait_ge(turned, ring.count(t))
                    wait_count(act, made, ring.count(t, G - 2))
                    nc.scalar.copy(aT[:, t[1], :], psT[t[1] % 2][:, 0:D]).then_inc(aTs, 1)
            ring.run(act, step, lag=2)

        @block.tensor
        def _(pe):
            pe.wait_ge(w_in, 32)

            def step(i, u):
                if (t := ring.at(i, u)) is not None:
                    pe.wait_ge(scaled, ring.count(t))
                    wait_count(pe, aTs, ring.count(t, 1 if u == 0 else 2))
                    for k in range(2):
                        last = nc.tensor.transpose(psT[u % 2][:, k * P:(k + 1) * P], a[:, u, k * P:(k + 1) * P], c.ident[:, :])
                    last.then_inc(turned, 1)
                if (t := ring.at(i, u, 1)) is not None:
                    pe.wait_ge(aTs, ring.count(t))
                    wait_count(pe, ys, ring.count(t, 1 if t[1] == 0 else 2))
                    for k in range(2):
                        last = nc.tensor.matmul(psO[t[1] % 2][:, 0:D], aT[:, t[1], k * P:(k + 1) * P], w[:, k, :],
                                                start=(k == 0), stop=(k == 1))
                    last.then_inc(made, 1)
            ring.run(pe, step, lag=1)

        @block.vector
        def _(dve):
            dve.wait_ge(w_in, 32)

            def step(i, u):
                if (t := ring.at(i, u)) is not None:
                    dve.wait_ge(made, ring.count(t))
                    wait_count(dve, outs, ring.count(t, G))
                    nc.vector.tensor_tensor(y[:, u, :], psO[u % 2][:, 0:D], bias[:, :], ALU.add).then_inc(ys, 1)
                if (t := ring.at(i, u, 2)) is not None:
                    dve.wait_ge(ys, ring.count(t))
                    if not (isinstance(t[0], int) and t[0] == 0):
                        dve.wait_ge(left[t[1]], 16 * t[0])
                    nc.vector.scalar_tensor_tensor(z[:, t[1], :], y[:, t[1], :], SLOPE, y[:, t[1], :], ALU.mult, ALU.max).then_inc(zs, 1)
                if (t := ring.at(i, u, 4)) is not None:
                    dve.wait_ge(zs, ring.count(t))
                    nc.vector.tensor_tensor(z[:, t[1], :], z[:, t[1], :], flat(c.x[:, bass.ds(ring.count(t) - 1, 1), :]),
                                            ALU.add).then_inc(outs, 1)
            ring.run(dve, step, lag=4)


class Core:

    def __init__(self, sh):
        self.sh = sh
        self.stages = 0

    def stage(self):
        self.stages += 1
        return self.stages


def stage(nc, build, *args):
    with nc.cleanup_on_exit():
        build(nc, *args)


def gnn_stack(nc, x_in, src_in, dst_in, attr_in, type_in, w1t_in, b1_in, w2t_in, wrel_in, bias1_in, watt_in,
              att_src_in, att_dst_in, bias2_in, gamma_in, beta_in, w3_in, bias3_in, out):
    sh = Shapes(x_in.shape[0], src_in.shape[0])
    c = Core(sh)
    c.x_in, c.src_in, c.dst_in, c.attr_in, c.type_in = x_in, src_in, dst_in, attr_in, type_in
    c.w1t_in, c.b1_in, c.w2t_in = w1t_in, b1_in, w2t_in
    c.wrel_in, c.bias1_in = wrel_in, bias1_in
    c.watt_in, c.att_src_in, c.att_dst_in = watt_in, att_src_in, att_dst_in
    c.bias2_in, c.gamma_in, c.beta_in, c.w3_in, c.bias3_in, c.out = bias2_in, gamma_in, beta_in, w3_in, bias3_in, out
    dram = lambda name, shape: nc.dram_tensor("dram_" + name, shape, F32, kind="Internal").ap()
    c.rec_dst, c.rec_src = dram("rec_dst", [sh.EP, REC]), dram("rec_src", [sh.EP, REC])
    c.ptab, c.xtab = dram("ptab", [sh.N, D]), dram("xtab", [NREL * sh.N, D])
    c.gtab, c.stab, c.htab = dram("gtab", [sh.N, AW]), dram("stab", [sh.N, HEADS]), dram("htab", [sh.N, D])
    with ExitStack() as ctx:
        sb = lambda name, shape, dt=F32: ctx.enter_context(nc.sbuf_tensor(name, shape, dt))
        c.tiles = {k: (sb(f"base_{k}", [P, sh.NT]), sb(f"place_{k}", [1, sh.NT], I32), sb(f"off_{k}", [1, sh.NT], I32))
                   for k in ("dst", "src")}
        c.node_i = sb("node_i", [1, sh.NT], I32)
        c.passed = {e: ctx.enter_context(nc.semaphore(f"passed_{e}")) for e in ("sp", "dve", "pool")}
        constants(nc, c, ctx)
        stage(nc, sort_stage, c, "dst")
        stage(nc, sort_stage, c, "src")
        c.acc = sb("sums", [P, sh.NB + 1, AW])
        c.top, c.node = sb("top", [P, sh.NB + 1, 2 * HEADS]), sb("node", [P, sh.NB + 1, 2 * HEADS])
        c.own = sb("own", [P, sh.NB, HEADS])
        c.dinv = sb("dinv", [P, sh.NB])
        stage(nc, stats_stage, c)
        stage(nc, table_stage, c, 0)
        stage(nc, edge_pass, c, "dst", c.ptab, D, 0, "edge_mlp")
        stage(nc, sage_update, c)
        stage(nc, table_stage, c, 1)
        stage(nc, edge_pass, c, "src", c.xtab, D, 0, "plain")
        stage(nc, rgcn_update, c)
        stage(nc, table_stage, c, 2)
        stage(nc, edge_pass, c, "dst", c.stab, HEADS, 0, "max")
        stage(nc, attention_guard, c)
        stage(nc, edge_pass, c, "dst", c.gtab, AW, 0, "attend")
        stage(nc, attention_update, c)
        stage(nc, table_stage, c, 3)
        stage(nc, edge_pass, c, "src", c.htab, D, 2, "plain")
        stage(nc, gcn_output, c)


def kernel(x, src, dst, edge_attr_3, edge_type_8, L0_gnn_W1, L0_gnn_b1, L0_gnn_W2, L1_gnn_weight, L1_gnn_bias,
           L2_gnn_W, L2_gnn_att_src, L2_gnn_att_dst, L2_gnn_bias, L2_gnn_gamma, L2_gnn_beta, L3_gnn_W, L3_gnn_b):
    import concourse.bacc as bacc
    from concourse.bass_utils import run_bass_kernel_spmd

    arrays = {
        "x_in": x, "src_in": src, "dst_in": dst, "attr_in": np.asarray(edge_attr_3).reshape(-1), "type_in": edge_type_8,
        "w1t_in": np.asarray(L0_gnn_W1).T, "b1_in": L0_gnn_b1, "w2t_in": np.asarray(L0_gnn_W2).T,
        "wrel_in": L1_gnn_weight, "bias1_in": L1_gnn_bias, "watt_in": L2_gnn_W, "att_src_in": L2_gnn_att_src,
        "att_dst_in": L2_gnn_att_dst, "bias2_in": L2_gnn_bias, "gamma_in": L2_gnn_gamma, "beta_in": L2_gnn_beta,
        "w3_in": L3_gnn_W, "bias3_in": L3_gnn_b,
    }
    arrays = {k: np.ascontiguousarray(v) for k, v in arrays.items()}
    nc = bacc.Bacc("TRN2", target_bir_lowering=False, num_devices=1)
    args = {k: nc.dram_tensor(k, v.shape, mybir.dt.from_np(v.dtype), kind="ExternalInput").ap() for k, v in arrays.items()}
    out = nc.dram_tensor("out", arrays["x_in"].shape, F32, kind="ExternalOutput").ap()
    gnn_stack(nc, **args, out=out)
    r = run_bass_kernel_spmd(nc, [arrays], core_ids=[0])
    return r.results[0]["out"]
```

```python
from contextlib import ExitStack

import numpy as np

import concourse.bass as bass
from concourse import mybir

F32 = mybir.dt.float32
BF16 = mybir.dt.bfloat16
I32 = mybir.dt.int32
ALU = mybir.AluOpType
ACT = mybir.ActivationFunctionType
AX = mybir.AxisListType
P = 128
D = 256
HEADS, DH = 8, 32
NREL = 8
EPS = 1e-5
SLOPE = 0.2
U = 16
REC = 8
AW = D + HEADS
BIG = 1e30
SPAN = 60.0


class Ring:

    def __init__(self, n, size):
        assert n % size == 0 and n // size >= 3
        self.n, self.size, self.rounds = n, size, n // size

    def at(self, i, u, back=0):
        q, s = divmod(u - back, self.size)
        j = i + q
        if isinstance(j, int) and not 0 <= self.size * j + s < self.n:
            return None
        return j, s

    def count(self, t, back=0):
        c = self.size * t[0] + t[1] + 1 - back
        return None if isinstance(c, int) and c <= 0 else c

    def run(self, eng, step, lag=0):
        for u in range(self.size):
            step(0, u)
        with eng.Fori(1, self.rounds - 1) as i:
            for u in range(self.size):
                step(i, u)
        for u in range(self.size):
            step(self.rounds - 1, u)
        for u in range(lag):
            step(self.rounds, u)


def wait_count(eng, sem, count):
    if count is not None:
        eng.wait_ge(sem, count)


class Places:

    def __init__(self, eng, values, ring, back, max_val):
        self.eng, self.values, self.ring, self.back, self.max_val = eng, values, ring, back, max_val

    def load(self, i):
        there = [(u, t) for u in range(self.ring.size) if (t := self.ring.at(i, u, self.back)) is not None]
        first, n = self.ring.count(there[0][1]) - 1, len(there)
        _, held = self.eng.bass.values_load_multi_w_load_instructions(
            self.values[0:1, bass.ds(first, n)], engines=[self.eng.engine], min_val=0, max_val=self.max_val,
            skip_runtime_bounds_check_because="the lists hold at most NB buckets' places, and offsets up to EP - P")
        self.held = {u: v for (u, _), v in zip(there, held)}

    def of(self, u):
        return self.held[u]


class Gate:

    def __init__(self, eng, semaphore):
        self.eng, self.semaphore = eng, semaphore

    def step(self):
        self.eng.sem_inc(self.semaphore, 1)


class Shapes:
    def __init__(self, n_nodes, n_edges):
        self.N, self.E = n_nodes, n_edges
        self.NB = -(-n_nodes // P)
        self.LAST = n_nodes - (self.NB - 1) * P
        cols = -(-n_edges // P)
        self.COLS = -(-cols // U) * U
        self.EP = P * self.COLS
        tiles = (n_edges + self.NB * (P - 1)) // P
        self.NT = -(-tiles // U) * U
        self.ND = self.NB + self.NB % 2
        assert n_edges > (P - 1) * self.COLS
        self.NOWHERE = float(P * (self.NB + 3))


def constants(nc, c, ctx):
    sh = c.sh
    sb = lambda name, shape, dt: ctx.enter_context(nc.sbuf_tensor(name, shape, dt))
    c.iota = sb("iota", [P, P], F32)
    c.iota_bf = sb("iota_bf", [P, P], BF16)
    c.ident = sb("ident", [P, P], F32)
    c.ident_bf = sb("ident_bf", [P, P], BF16)
    c.ones = sb("ones", [P, P], F32)
    c.x = sb("x_sb", [P, sh.NB, D], F32)
    c.stat = sb("stat", [P, sh.NB, 2], F32)
    c.rstd = sb("rstd", [P, sh.NB], F32)
    c.nbias = sb("nbias", [P, sh.NB], F32)
    with ExitStack() as st:
        sem = lambda name: nc.alloc_semaphore(name)
        made, x_zero, x_in = sem("made"), sem("x_zero"), sem("x_in")
        block = st.enter_context(nc.Block())

        @block.gpsimd
        def _(pool):
            nc.gpsimd.iota(c.iota[:, :], pattern=[[1, P]], base=0, channel_multiplier=0,
                           allow_small_or_imprecise_dtypes=True)
            nc.gpsimd.iota(c.iota_bf[:, :], pattern=[[1, P]], base=0, channel_multiplier=0,
                           allow_small_or_imprecise_dtypes=True)
            nc.gpsimd.memset(c.ones[:, :], 1.0).then_inc(made, 1)
            nc.gpsimd.memset(c.ident[:, :], 0.0).then_inc(made, 1)
            nc.gpsimd.memset(c.ident_bf[:, :], 0.0).then_inc(made, 1)
            pool.wait_ge(made, 3)
            for m in (c.ident, c.ident_bf):
                nc.gpsimd.affine_select(out=m[:, :], in_=m[:, :], compare_op=ALU.not_equal, fill=1.0,
                                        base=0, pattern=[[-1, P]], channel_multiplier=1)

        @block.vector
        def _(dve):
            nc.vector.memset(c.x[:, sh.NB - 1, :], 0.0).then_inc(x_zero, 1)

        @block.sync
        def _(sp):
            full = (sh.NB - 1) * P
            sp.dma_start(c.x[:, 0:sh.NB - 1, :],
                         c.x_in[0:full, :].rearrange("(i p) d -> p i d", p=P)).then_inc(x_in, 16)
            sp.wait_ge(x_zero, 1)
            sp.dma_start(c.x[0:sh.LAST, sh.NB - 1, :], c.x_in[full:sh.N, :]).then_inc(x_in, 16)
            sp.wait_ge(x_in, 32)


class Edges:

    def __init__(self, nc, c, kind, ctx):
        sh = c.sh
        sb = lambda name, shape, dt=F32: ctx.enter_context(nc.sbuf_tensor(f"{name}_{kind}", shape, dt))
        self.kind = kind
        self.rec = sb("rec", [P, sh.COLS, REC])
        self.key = sb("key", [P, sh.COLS])
        self.pos_i = sb("pos_i", [P, sh.COLS], I32)
        self.offs = sb("offs", [P, sh.ND])
        self.digits = sb("digits", [P, sh.ND])
        self.stage_rec = sb("stage_rec", [P, 2, U // 2, REC])
        self.stage_pos = sb("stage_pos", [P, 2, U // 2], I32)
        self.to = c.rec_dst if kind == "dst" else c.rec_src


def list_stage(nc, c, edges):
    sh = c.sh
    NB, ND, COLS, NT = sh.NB, sh.ND, sh.COLS, sh.NT
    kind = edges.kind
    by_dst = kind == "dst"
    rec, key, offs, digits = edges.rec, edges.key, edges.offs, edges.digits
    base_f, place_i, off_i = c.tiles[kind]
    own = sh.E - (P - 1) * COLS
    with ExitStack() as st:
        sb = lambda name, shape, dt=F32: st.enter_context(nc.sbuf_tensor(f"{name}_{kind}", shape, dt))
        sem = lambda name: nc.alloc_semaphore(f"{name}_{kind}")
        src_i, dst_i = sb("src_i", [P, COLS], I32), sb("dst_i", [P, COLS], I32)
        third = sb("third", [P, COLS * 3] if by_dst else [P, COLS], F32 if by_dst else I32)
        next_i = sb("next_i", [P, COLS], I32) if by_dst else None
        rest = sb("rest", [P, COLS * 3]) if by_dst else None
        key_i, mask = sb("key_i", [P, COLS], I32), sb("mask", [P, COLS])
        allone = sb("allone", [P, ND])
        falls, fall_i = sb("falls", [P, 1]), sb("fall_i", [P, 1], I32)
        counts, tot, incl = sb("counts", [P, ND]), sb("tot", [P, ND]), sb("incl", [P, ND])
        before = sb("before", [P, P])
        upto = sb("upto", [P, P])
        nb, nt_i, nt, over = sb("nb", [P, 1]), sb("nt_i", [P, 1], I32), sb("nt", [P, 1]), sb("over", [P, 1])
        past, tile_no = sb("past", [P, NT]), sb("tile_no", [P, NT])
        off_f = sb("off_f", [P, NT])
        ps = [st.enter_context(nc.psum_tensor(f"ps{k}_{kind}", [P, 512], F32)) for k in range(8)]
        loaded, zeroed, tri = sem("loaded"), sem("zeroed"), sem("tri")
        counted, totals, tiled = sem("counted"), sem("totals"), sem("tiled")
        prefixed, listed, summed, compared, fallen = [sem(x) for x in ("prefixed", "listed", "summed", "compared", "fallen")]
        chain, recorded, written = sem("chain"), sem("recorded"), sem("written")
        block = st.enter_context(nc.Block())
        halves = ((0, 512), (512, NT)) if NT > 512 else ((0, NT),)
        loads = 3 * 2 + (2 if by_dst else 0)

        @block.sync
        def _(sp):
            sp.wait_ge(zeroed, 2)
            parts = [(src_i, c.src_in, 1, 0), (dst_i, c.dst_in, 1, 0),
                     (third, c.attr_in if by_dst else c.type_in, 3 if by_dst else 1, 0)]
            if by_dst:
                parts.append((next_i, c.dst_in, 1, 1))
            for to, of, w, ahead in parts:
                full = (P - 1) * COLS * w
                sp.dma_start(to[0:P - 1, :], of[ahead:full + ahead].rearrange("(p n) -> p n", p=P - 1)).then_inc(loaded, 16)
                sp.dma_start(to[P - 1:P, 0:own * w - ahead], of[full + ahead:full + own * w].rearrange("(p n) -> p n", p=1)
                             ).then_inc(loaded, 16)
            sp.wait_ge(loaded, 16 * loads)
            if by_dst:
                sp.wait_ge(recorded, 1)
                sp.dma_start(edges.to.rearrange("(p n) w -> p (n w)", p=P), rec[:, :, :].rearrange("p n w -> p (n w)")).then_inc(written, 16)
                sp.wait_ge(written, 16)

        @block.gpsimd
        def _(pool):
            nc.gpsimd.memset(third[:, :], 0.0 if by_dst else 0).then_inc(zeroed, 1)
            nc.gpsimd.iota(digits[:, :], pattern=[[1, ND]], base=0, channel_multiplier=0,
                           allow_small_or_imprecise_dtypes=True)
            nc.gpsimd.iota(tile_no[:, :], pattern=[[1, NT]], base=0, channel_multiplier=0,
                           allow_small_or_imprecise_dtypes=True)
            nc.gpsimd.memset(before[:, :], 1.0)
            nc.gpsimd.memset(upto[:, :], 1.0).then_inc(tri, 1)
            pool.wait_ge(tri, 1)
            nc.gpsimd.affine_select(out=before[:, :], in_=before[:, :], compare_op=ALU.is_gt, fill=0.0,
                                    base=0, pattern=[[1, P]], channel_multiplier=-1)
            nc.gpsimd.affine_select(out=upto[:, :], in_=upto[:, :], compare_op=ALU.is_ge, fill=0.0,
                                    base=0, pattern=[[1, P]], channel_multiplier=-1).then_inc(tri, 1)

        @block.vector
        def _(dve):
            chained = [0]

            def link(instruction):
                chained[0] += 1
                instruction.then_inc(chain, 1)
                dve.wait_ge(chain, chained[0])

            nc.vector.memset(allone[:, :], 1.0)
            nc.vector.memset(src_i[:, :], 0 if by_dst else int(sh.NOWHERE))
            if by_dst:
                nc.vector.memset(next_i[:, :], int(sh.NOWHERE))
            link(nc.vector.memset(dst_i[:, :], int(sh.NOWHERE) if by_dst else 0))
            nc.vector.memset(rec[:, :, :], 0.0).then_inc(zeroed, 1)
            dve.wait_ge(loaded, 16 * loads)
            node_i = dst_i if by_dst else src_i
            rec_i = rec[:, :, :].bitcast(I32)
            link(nc.vector.tensor_single_scalar(key_i[:, :], node_i[:, :], 7, ALU.arith_shift_right))
            nc.vector.tensor_copy(rec[:, :, 1], node_i[:, :])
            link(nc.vector.tensor_copy(key[:, :], key_i[:, :]))
            dve.wait_ge(tri, 2)
            with dve.Fori(0, ND) as d:
                dve.wait_ge(counted, d)
                nc.vector.tensor_scalar(mask[:, :], key[:, :], digits[:, bass.ds(d, 1)], None, ALU.is_equal,
                                        ALU.add, accum_out=counts[:, bass.ds(d, 1)]).then_inc(counted, 1)
            dve.wait_ge(counted, ND)
            if by_dst:
                nc.vector.tensor_copy(rec_i[:, :, 0], src_i[:, :])
                part = lambda k: rec[:, :, :].bitcast(BF16)[:, :, 4 + 3 * k:7 + 3 * k]
                of3 = lambda ap: ap[:, :].rearrange("p (n k) -> p n k", k=3)
                link(nc.vector.tensor_copy(part(0), of3(third)))
                link(nc.vector.tensor_tensor(of3(rest), of3(third), part(0), ALU.subtract))
                link(nc.vector.tensor_copy(part(1), of3(rest)))
                link(nc.vector.tensor_tensor(of3(rest), of3(rest), part(1), ALU.subtract))
                nc.vector.tensor_copy(part(2), of3(rest)).then_inc(recorded, 1)
                nc.vector.tensor_tensor(mask[:, :], dst_i[:, :], next_i[:, :], ALU.is_gt).then_inc(compared, 1)
                dve.wait_ge(compared, 1)
                nc.vector.tensor_reduce(falls[:, :], mask[:, :], AX.X, ALU.add).then_inc(compared, 1)
            else:
                nc.vector.tensor_copy(rec_i[:, :, 2], dst_i[:, :])
                link(nc.vector.tensor_scalar(rec_i[:, :, 0], third[:, :], sh.N, None, ALU.mult))
                link(nc.vector.tensor_tensor(rec_i[:, :, 0], rec_i[:, :, 0], dst_i[:, :], ALU.add))
            dve.wait_ge(totals, 2)
            link(nc.vector.tensor_copy(tot[:, :], ps[1][:, 0:ND]))
            link(nc.vector.tensor_tensor_scan(incl[:, :], allone[:, :], tot[:, :], 0.0, ALU.mult, ALU.add))
            link(nc.vector.tensor_tensor(incl[:, :], incl[:, :], tot[:, :], ALU.subtract))
            link(nc.vector.scalar_tensor_tensor(offs[:, :], incl[:, :], -1.0, ps[0][:, 0:ND], ALU.add, ALU.add))
            dve.wait_ge(totals, 3)
            link(nc.vector.tensor_copy(nb[0:NB, :], ps[2][0:NB, 0:1]))
            link(nc.vector.tensor_scalar(nt[0:NB, :], nb[0:NB, :], float(P - 1), None, ALU.add))
            link(nc.vector.tensor_copy(nt_i[0:NB, :], nt[0:NB, :]))
            link(nc.vector.tensor_single_scalar(nt_i[0:NB, :], nt_i[0:NB, :], 7, ALU.arith_shift_right))
            link(nc.vector.tensor_copy(nt[0:NB, :], nt_i[0:NB, :]))
            nc.vector.scalar_tensor_tensor(over[0:NB, :], nt[0:NB, :], float(-P), nb[0:NB, :],
                                           ALU.mult, ALU.add).then_inc(tiled, 1)
            dve.wait_ge(prefixed, 1)
            link(nc.vector.tensor_copy(nb[0:NB, :], ps[2][0:NB, 8:9]))
            nc.vector.tensor_scalar(past[0:NB, :], tile_no[0:NB, :], nb[0:NB, 0:1], None,
                                    ALU.is_ge).then_inc(listed, 1)
            dve.wait_ge(summed, 2 * len(halves))
            for k, (a, z) in enumerate(halves):
                nc.vector.tensor_scalar(base_f[:, a:z], ps[3 + k][:, 0:z - a], float(P), None, ALU.mult)
                nc.vector.tensor_scalar(place_i[:, a:z], ps[3 + k][0:1, 0:z - a], float(AW), None, ALU.mult)
                if by_dst:
                    nc.vector.tensor_scalar(c.node_i[:, a:z], ps[3 + k][0:1, 0:z - a], float(2 * HEADS), None, ALU.mult)
                link(nc.vector.scalar_tensor_tensor(off_f[:, a:z], tile_no[:, a:z], float(P), ps[5 + k][:, 0:z - a],
                                                    ALU.mult, ALU.add))
            link(nc.vector.tensor_scalar(off_i[:, :], off_f[0:1, :], float(sh.EP - P), None, ALU.min))
            if by_dst:
                dve.wait_ge(fallen, 1)
                link(nc.vector.tensor_copy(c.unsorted[:, :], ps[7][0:1, 0:1]))

        @block.tensor
        def _(pe):
            pe.wait_ge(tri, 2)
            pe.wait_ge(counted, ND)
            nc.tensor.matmul(ps[0][:, 0:ND], before[:, :], counts[:, :], start=True, stop=True).then_inc(totals, 1)
            nc.tensor.matmul(ps[1][:, 0:ND], c.ones[:, :], counts[:, :], start=True, stop=True).then_inc(totals, 1)
            nc.tensor.matmul(ps[2][0:ND, 0:1], counts[:, :], c.ones[:, 0:1], start=True, stop=True).then_inc(totals, 1)
            if by_dst:
                pe.wait_ge(compared, 2)
                nc.tensor.matmul(ps[7][:, 0:1], c.ones[:, :], falls[:, :], start=True, stop=True).then_inc(fallen, 1)
            pe.wait_ge(tiled, 1)
            nc.tensor.matmul(ps[2][0:NB, 8:9], upto[0:NB, 0:NB], nt[0:NB, 0:1], start=True, stop=True).then_inc(prefixed, 1)
            pe.wait_ge(listed, 1)
            for k, (a, z) in enumerate(halves):
                nc.tensor.matmul(ps[3 + k][:, 0:z - a], c.ones[0:NB, :], past[0:NB, a:z], start=True, stop=True).then_inc(summed, 1)
                nc.tensor.matmul(ps[5 + k][:, 0:z - a], over[0:NB, 0:1].to_broadcast([NB, P]), past[0:NB, a:z],
                                 start=True, stop=True).then_inc(summed, 1)


def place_stage(nc, c, edges):
    sh = c.sh
    ND, COLS = sh.ND, sh.COLS
    kind = edges.kind
    ring = Ring(ND, 2)
    with ExitStack() as st:
        sb = lambda name, shape, dt=F32: st.enter_context(nc.sbuf_tensor(f"{name}_{kind}", shape, dt))
        sem = lambda name: nc.alloc_semaphore(f"{name}_{kind}")
        pos, allone = sb("pos", [P, COLS]), sb("alls", [P, COLS])
        minus = sb("minus", [P, ND])
        gap, mask, run = sb("gap", [P, 2, COLS]), sb("masks", [P, 2, COLS]), sb("run", [P, 2, COLS])
        ready, gaps, masks, runs, found, added = [sem(x) for x in ("ready", "gaps", "masks", "runs", "found", "added")]
        block = st.enter_context(nc.Block())

        @block.gpsimd
        def _(pool):
            nc.gpsimd.iota(pos[:, :], pattern=[[1, COLS]], base=0, channel_multiplier=COLS,
                           allow_small_or_imprecise_dtypes=True).then_inc(added, 1)
            pool.wait_ge(added, 1)
            nc.gpsimd.affine_select(out=pos[:, :], in_=pos[:, :], compare_op=ALU.is_ge, fill=0.0,
                                    base=-sh.E, pattern=[[1, COLS]], channel_multiplier=COLS).then_inc(added, 1)

            def step(i, u):
                t = ring.at(i, u)
                pool.wait_ge(found, ring.count(t))
                pool.wait_ge(added, ring.count(t) + 1)
                nc.gpsimd.tensor_tensor(pos[:, :], pos[:, :], run[:, u, :], ALU.add).then_inc(added, 1)
            ring.run(pool, step)

        @block.scalar
        def _(act):
            act.wait_ge(ready, 1)

            def step(i, u):
                t = ring.at(i, u)
                wait_count(act, masks, ring.count(t, 2))
                nc.scalar.activation(gap[:, u, :], edges.key[:, :], ACT.Abs, bias=minus[:, bass.ds(ring.count(t) - 1, 1)]).then_inc(gaps, 1)
                act.wait_ge(gaps, ring.count(t))
                wait_count(act, found, ring.count(t, 2))
                nc.scalar.activation(mask[:, u, :], gap[:, u, :], ACT.Relu, bias=c.ones[:, 0:1], scale=-1.0).then_inc(masks, 1)
            ring.run(act, step)

        @block.vector
        def _(dve):
            nc.vector.memset(allone[:, :], 1.0)
            nc.vector.tensor_scalar(minus[:, :], edges.digits[:, :], -1.0, None, ALU.mult).then_inc(ready, 1)
            dve.wait_ge(ready, 1)

            def step(i, u):
                t = ring.at(i, u)
                dve.wait_ge(masks, ring.count(t))
                back = ring.count(t, 2)
                if back is not None:
                    dve.wait_ge(added, back + 2)
                nc.vector.tensor_tensor_scan(run[:, u, :], allone[:, :], mask[:, u, :], 0.0, ALU.mult, ALU.add).then_inc(runs, 1)
                dve.wait_ge(runs, ring.count(t))
                nc.vector.scalar_tensor_tensor(run[:, u, :], run[:, u, :], edges.offs[:, bass.ds(ring.count(t) - 1, 1)],
                                               mask[:, u, :], ALU.add, ALU.mult).then_inc(found, 1)
            ring.run(dve, step)
            dve.wait_ge(added, ND + 2)
            nc.vector.tensor_copy(edges.pos_i[:, :], pos[:, :])

        @block.tensor
        def _(pe):
            pe.wait_ge(added, ND + 2)

        @block.sync
        def _(sp):
            sp.wait_ge(added, ND + 2)


class Scatter:

    def __init__(self, nc, c, edges, first, end):
        self.nc, self.edges, self.first, self.end = nc, edges, first, end
        self.gate = Gate(nc.gpsimd, c.passed["pool"])
        if end > first:
            self.staged = nc.alloc_semaphore(f"staged_{edges.kind}_{first}")
            self.left = [nc.alloc_semaphore(f"left{h}_{edges.kind}_{first}") for h in range(2)]

    def run(self, pool):
        if self.end <= self.first:
            return
        nc, edges, half = self.nc, self.edges, U // 2

        def a_round(i):
            for h in range(2):
                column = U * (self.first + i) + half * h
                if not (isinstance(i, int) and i == 0):
                    pool.wait_ge(self.left[h], 16 * half * i)
                    self.gate.step()
                nc.gpsimd.tensor_copy(edges.stage_rec[:, h, :, :], edges.rec[:, bass.ds(column, half), :])
                nc.gpsimd.tensor_copy(edges.stage_pos[:, h, :], edges.pos_i[:, bass.ds(column, half)]).then_inc(self.staged, 1)
                pool.wait_ge(self.staged, 2 * i + h + 1)
                self.gate.step()
                for k in range(half):
                    nc.gpsimd.indirect_dma_start(
                        edges.to, bass.IndirectOffsetOnAxis(edges.stage_pos[:, h, k:k + 1], 0),
                        edges.stage_rec[:, h, k, :], None).then_inc(self.left[h], 16)

        rounds = self.end - self.first
        a_round(0)
        if rounds > 1:
            with pool.Fori(1, rounds) as i:
                a_round(i)
        for h in range(2):
            pool.wait_ge(self.left[h], 16 * half * rounds)


def scatter_stage(nc, c, edges, first, end):
    with nc.Block() as block:
        scatter = Scatter(nc, c, edges, first, end)

        @block.gpsimd
        def _(pool):
            scatter.run(pool)


def edge_pass(nc, c, kind, table, width, index_word, mode):
    sh = c.sh
    NT = sh.NT
    base_f, place_i, off_i = c.tiles[kind]
    rec_d = c.rec_dst if kind == "dst" else c.rec_src
    ring = Ring(NT, U)
    lag = 8
    nm = f"{mode}_{index_word}_{kind}"
    cols = {"plain": D + 1, "edge_mlp": D, "attend": AW, "max": 0}[mode]
    with ExitStack() as st:
        sb = lambda name, shape, dt: st.enter_context(nc.sbuf_tensor(f"{name}_{nm}", shape, dt))
        pt = lambda name, shape=(P, 512): st.enter_context(nc.psum_tensor(f"{name}_{nm}", list(shape), F32))
        sem = lambda name: nc.alloc_semaphore(f"{name}_{nm}")
        rec = sb("recs", [P, U, REC], F32)
        rec_i = rec[:, :, :].bitcast(I32)
        got = sb("got", [P, U, HEADS if mode == "max" else AW], F32)
        hot = sb("hot", [P, U, P], BF16 if mode == "max" else F32)
        rec_in = [sem(f"rec_in{s}") for s in range(U)]
        row_in = [sem(f"row_in{s}") for s in range(U)]
        hots, sums, added, start = sem("hots"), sem("sums"), sem("added"), sem("start")
        cleared = sem("cleared")
        if mode == "edge_mlp":
            spread = sb("spread", [P, 4, 27], BF16)
            feat = sb("feat", [27, 4, P], BF16)
            w27 = sb("w27", [27, D], BF16)
            w_part = sb("w_part", [3, 3, D], BF16)
            w_rest = sb("w_rest", [3, D], F32)
            msg = sb("msg", [P, 8, D], F32)
            pre = sb("pre", [P, 4, D], F32)
            w1b = sb("w1b", [3, D], F32)
            turned, feats, edged, pres, msgs, w_in = [sem(x) for x in ("turned", "feats", "edged", "pres", "msgs", "w_in")]
            spreads, w_split, w_laid = sem("spreads"), sem("w_split"), sem("w_laid")
            psF = [st.enter_context(nc.psum_tensor(f"psF{k}_{nm}", [P, 1024], BF16)) for k in range(2)]
            psE = [pt("psE0"), pt("psE1")]
        if mode == "attend":
            hotT = sb("hotT", [P, 4, P], F32)
            z, zc = sb("z", [P, 2, 2, HEADS], F32), sb("zc", [P, 2, 2, HEADS], F32)
            msg = sb("msg", [P, 8, AW], F32)
            turned, hotTs, nodes, zs, ws, msgs, zchain = [sem(x) for x in ("turned", "hotTs", "nodes", "zs", "ws", "msgs", "zchain")]
            psF = [pt("psF0"), pt("psF1")]
            psN = [pt("psN0"), pt("psN1")]
        if mode == "max":
            out_of = sb("out_of", [P, 4, P], BF16)
            diag = sb("diag", [P, 4, HEADS, P], BF16)
            ident4 = sb("ident4", [P, 4, P], BF16)
            top = sb("top", [P, 4, HEADS], F32)
            diag_a, diag_v, outs_, tops = [sem(x) for x in ("diag_a", "diag_v", "outs", "tops")]
            psM = [pt(f"psM{k}", (P, 1024)) for k in range(4)]
        else:
            psS = [pt(f"psS{k}") for k in range(4)]
        NPS = 4

        def pair(t):
            return U // 2 * t[0] + t[1] // 2

        def pairs_done(t, back):
            n = pair(t) + 1 - back
            return None if isinstance(n, int) and n <= 0 else n

        block = st.enter_context(nc.Block())

        @block.sync
        def _(sp):
            if mode == "edge_mlp":
                sp.dma_start(w1b[:, :], c.w1t_in[D:D + 3, :]).then_inc(w_in, 16)
                sp.wait_ge(w_split, 5)
                for i in range(3):
                    for j in range(3):
                        r = 9 * i + 3 * j
                        sp.dma_start(w27[r:r + 3, :], w_part[:, j, :]).then_inc(w_laid, 16)
            gate = Gate(sp, c.passed["sp"])
            offs = Places(nc.sync, off_i, ring, 0, sh.EP - P)

            def step(i, u):
                t = ring.at(i, u)
                if u == 0:
                    offs.load(i)
                off = offs.of(u)
                if (old := ring.at(i, u, U)) is not None:
                    sp.wait_ge(row_in[u], 16 * (old[0] + 1))
                    gate.step()
                    wait_count(sp, hots, ring.count(old))
                    gate.step()
                    if mode == "edge_mlp":
                        wait_count(sp, spreads, ring.count(old))
                        gate.step()
                sp.dma_start(rec[:, u, :], rec_d[bass.ds(off, P), :]).then_inc(rec_in[u], 16)

            ring.run(sp, step)
            if mode == "edge_mlp":
                sp.wait_ge(w_laid, 9 * 16)

        @block.gpsimd
        def _(pool):
            nc.gpsimd.memset(got[:, :, :], 1.0).then_inc(start, 1)
            pool.wait_ge(start, 1)
            gate = Gate(pool, c.passed["pool"])

            def step(i, u):
                t = ring.at(i, u)
                free = msgs if mode in ("edge_mlp", "attend") else sums
                if (old := ring.at(i, u, U)) is not None:
                    wait_count(pool, free, ring.count(old))
                pool.wait_ge(rec_in[u], 16 * (t[0] + 1))
                gate.step()
                w = HEADS if mode == "max" else width
                nc.gpsimd.indirect_dma_start(got[:, u, 0:w], None, table,
                                             bass.IndirectOffsetOnAxis(rec_i[:, u, index_word:index_word + 1], 0)
                                             ).then_inc(row_in[u], 16)

            ring.run(pool, step)

        @block.vector
        def _(dve):
            if mode == "max":
                for k in range(4):
                    nc.vector.tensor_copy(ident4[:, k, :], c.ident_bf[:, :])
                nc.vector.memset(c.top[:, :, :], -BIG).then_inc(cleared, 1)
            else:
                nc.vector.memset(c.acc[:, :, :], 0.0).then_inc(cleared, 1)
            if mode == "edge_mlp":
                dve.wait_ge(w_in, 16)
                for n, instruction in enumerate((
                        lambda: nc.vector.tensor_copy(w_part[:, 0, :], w1b[:, :]),
                        lambda: nc.vector.tensor_tensor(w_rest[:, :], w1b[:, :], w_part[:, 0, :], ALU.subtract),
                        lambda: nc.vector.tensor_copy(w_part[:, 1, :], w_rest[:, :]),
                        lambda: nc.vector.tensor_tensor(w_rest[:, :], w_rest[:, :], w_part[:, 1, :], ALU.subtract),
                        lambda: nc.vector.tensor_copy(w_part[:, 2, :], w_rest[:, :]))):
                    instruction().then_inc(w_split, 1)
                    dve.wait_ge(w_split, n + 1)
            dve.wait_ge(cleared, 1)

            places = Places(nc.vector, c.node_i if mode == "max" else place_i, ring,
                            {"max": 5, "attend": lag + 1}.get(mode, lag), sh.NB * (2 * HEADS if mode == "max" else AW))

            def add(i, u, back):
                if u == 0:
                    places.load(i)
                t = ring.at(i, u, back)
                if t is None:
                    return
                place = places.of(u)
                dve.wait_ge(sums, ring.count(t))
                wait_count(dve, added, ring.count(t, 1))
                if mode == "max":
                    k = t[1] % 4
                    nc.vector.tensor_reduce(top[:, k, :], psM[k][:, :].rearrange("p (h e) -> p h e", e=P),
                                            AX.X, ALU.max).then_inc(tops, 1)
                    dve.wait_ge(tops, ring.count(t))
                    here = c.top[:, :, :].rearrange("p b h -> p (b h)")[:, bass.ds(place, HEADS)]
                    nc.vector.tensor_tensor(here, here, top[:, k, :], ALU.max).then_inc(added, 1)
                else:
                    here = c.acc[:, :, :].rearrange("p b w -> p (b w)")[:, bass.ds(place, cols)]
                    nc.vector.tensor_tensor(here, here, psS[t[1] % NPS][:, 0:cols], ALU.add).then_inc(added, 1)

            def one_hot(i, u):
                t = ring.at(i, u)
                if t is None:
                    return
                dve.wait_ge(rec_in[u], 16 * (t[0] + 1))
                iota = c.iota_bf if mode == "max" else c.iota
                nc.vector.tensor_scalar(hot[:, u, :], iota[:, :], base_f[:, bass.ds(ring.count(t) - 1, 1)],
                                        rec[:, u, 1:2], ALU.add, ALU.is_equal).then_inc(hots, 1)

            if mode == "plain":
                def step(i, u):
                    one_hot(i, u)
                    add(i, u, lag)
            elif mode == "edge_mlp":
                def step(i, u):
                    one_hot(i, u)
                    if (t := ring.at(i, u, 4)) is not None:
                        dve.wait_ge(row_in[t[1]], 16 * (t[0] + 1))
                        dve.wait_ge(edged, ring.count(t))
                        wait_count(dve, msgs, ring.count(t, 4))
                        nc.vector.tensor_tensor(pre[:, t[1] % 4, :], got[:, t[1], 0:D],
                                                psE[t[1] % 2][:, 0:D], ALU.add).then_inc(pres, 1)
                    add(i, u, lag)
            elif mode == "attend":
                def step(i, u):
                    one_hot(i, u)
                    if (t := ring.at(i, u, 4)) is not None and t[1] % 2:
                        k, q = t[1] // 2 % 2, 4 * pair(t)
                        for s_ in (t[1] - 1, t[1]):
                            dve.wait_ge(row_in[s_], 16 * (t[0] + 1))
                        dve.wait_ge(nodes, ring.count(t))
                        n = psN[k][:, 0:4 * HEADS].rearrange("p (t w) -> p t w", t=2)
                        wait_count(dve, ws, pairs_done(t, 2))
                        nc.vector.tensor_tensor(z[:, k, :, :], n[:, :, 0:HEADS], got[:, t[1] - 1:t[1] + 1, D:AW], ALU.add).then_inc(zchain, 1)
                        dve.wait_ge(zchain, q + 1)
                        nc.vector.scalar_tensor_tensor(zc[:, k, :, :], z[:, k, :, :], SLOPE, z[:, k, :, :], ALU.mult, ALU.max).then_inc(zchain, 1)
                        dve.wait_ge(zchain, q + 2)
                        nc.vector.tensor_tensor(zc[:, k, :, :], zc[:, k, :, :], n[:, :, HEADS:2 * HEADS], ALU.subtract).then_inc(zchain, 1)
                        dve.wait_ge(zchain, q + 3)
                        nc.vector.tensor_scalar(zc[:, k, :, :], zc[:, k, :, :], 60.0, None, ALU.min).then_inc(zchain, 1)
                    if (t := ring.at(i, u, 6)) is not None:
                        dve.wait_ge(ws, pair(t) + 1)
                        nc.vector.tensor_tensor(
                            msg[:, t[1] % 8, 0:D].rearrange("p (h d) -> p h d", d=DH),
                            got[:, t[1], 0:D].rearrange("p (h d) -> p h d", d=DH),
                            msg[:, t[1] % 8, D:AW].unsqueeze(2).to_broadcast([P, HEADS, DH]), ALU.mult).then_inc(msgs, 1)
                    add(i, u, lag + 1)
            else:
                def step(i, u):
                    one_hot(i, u)
                    if (t := ring.at(i, u)) is not None:
                        k = u % 4
                        dve.wait_ge(hots, ring.count(t))
                        wait_count(dve, sums, ring.count(t, 4))
                        nc.vector.tensor_scalar(out_of[:, k, :], hot[:, u, :], -1.0, BIG, ALU.add, ALU.mult).then_inc(outs_, 1)
                    if (t := ring.at(i, u, 3)) is not None:
                        k = t[1] % 4
                        dve.wait_ge(row_in[t[1]], 16 * (t[0] + 1))
                        wait_count(dve, sums, ring.count(t, 4))
                        for h in range(HEADS // 2):
                            last = nc.vector.tensor_scalar(diag[:, k, h, :], c.ident_bf[:, :], got[:, t[1], h:h + 1], None, ALU.mult)
                        last.then_inc(diag_v, 1)
                    add(i, u, 5)
            ring.run(dve, step, lag={"max": 5, "attend": lag + 1}.get(mode, lag))

        @block.scalar
        def _(act):
            if mode == "edge_mlp":
                def step(i, u):
                    if (t := ring.at(i, u)) is not None:
                        act.wait_ge(rec_in[u], 16 * (t[0] + 1))
                        wait_count(act, turned, ring.count(t, 4))
                        parts = rec[:, u, :].bitcast(BF16)[:, 4:13].rearrange("p (i k) -> p i k", k=3)
                        nc.scalar.copy(spread[:, u % 4, :].rearrange("p (i j k) -> p i j k", j=3, k=3),
                                       parts.unsqueeze(2).to_broadcast([P, 3, 3, 3])).then_inc(spreads, 1)
                    if (t := ring.at(i, u, 1)) is not None:
                        act.wait_ge(turned, ring.count(t))
                        wait_count(act, edged, ring.count(t, 4))
                        nc.scalar.copy(feat[:, t[1] % 4, :], psF[t[1] % 2][0:27, 0:P]).then_inc(feats, 1)
                    if (t := ring.at(i, u, 4)) is not None:
                        act.wait_ge(pres, ring.count(t))
                        wait_count(act, sums, ring.count(t, 8))
                        nc.scalar.activation(msg[:, t[1] % 8, :], pre[:, t[1] % 4, :], ACT.Relu).then_inc(msgs, 1)
                ring.run(act, step, lag=4)
            elif mode == "attend":
                def step(i, u):
                    if (t := ring.at(i, u)) is not None:
                        act.wait_ge(turned, ring.count(t))
                        wait_count(act, nodes, ring.count(t, 4))
                        nc.scalar.copy(hotT[:, u % 4, :], psF[u % 2][:, 0:P]).then_inc(hotTs, 1)
                    if (t := ring.at(i, u, 4)) is not None and t[1] % 2:
                        act.wait_ge(zchain, 4 * pair(t) + 4)
                        wait_count(act, sums, ring.count(t, 8))
                        m = t[1] % 8
                        nc.scalar.activation(msg[:, m - 1:m + 1, D:AW], zc[:, t[1] // 2 % 2, :, :], ACT.Exp).then_inc(ws, 1)
                ring.run(act, step, lag=4)
            elif mode == "max":
                def step(i, u):
                    if (t := ring.at(i, u, 3)) is not None:
                        k = t[1] % 4
                        act.wait_ge(row_in[t[1]], 16 * (t[0] + 1))
                        wait_count(act, sums, ring.count(t, 4))
                        for h in range(HEADS // 2, HEADS):
                            last = nc.scalar.activation(diag[:, k, h, :], c.ident_bf[:, :], ACT.Copy, scale=got[:, t[1], h:h + 1])
                        last.then_inc(diag_a, 1)
                ring.run(act, step, lag=3)

        @block.tensor
        def _(pe):
            if mode == "edge_mlp":
                pe.wait_ge(w_laid, 9 * 16)

            def gather_sum(i, u, back, rows, ready):
                t = ring.at(i, u, back)
                if t is None:
                    return
                for s_, n_ in ready(t):
                    pe.wait_ge(s_, n_)
                wait_count(pe, added, ring.count(t, NPS))
                nc.tensor.matmul(psS[t[1] % NPS][:, 0:cols], hot[:, t[1], :], rows(t), start=True, stop=True).then_inc(sums, 1)

            if mode == "plain":
                def step(i, u):
                    gather_sum(i, u, 0, lambda t: got[:, t[1], 0:cols],
                               lambda t: [(row_in[t[1]], 16 * (t[0] + 1)), (hots, ring.count(t))])
                ring.run(pe, step)
            elif mode == "edge_mlp":
                def step(i, u):
                    if (t := ring.at(i, u)) is not None:
                        pe.wait_ge(spreads, ring.count(t))
                        wait_count(pe, feats, ring.count(t, 2))
                        nc.tensor.transpose(psF[u % 2][0:27, 0:P], spread[:, u % 4, :],
                                            c.ident_bf[:, :]).then_inc(turned, 1)
                    if (t := ring.at(i, u, 2)) is not None:
                        pe.wait_ge(feats, ring.count(t))
                        wait_count(pe, pres, ring.count(t, 2))
                        nc.tensor.matmul(psE[t[1] % 2][:, 0:D], feat[:, t[1] % 4, :], w27[:, :], start=True, stop=True).then_inc(edged, 1)
                    gather_sum(i, u, 6, lambda t: msg[:, t[1] % 8, :],
                               lambda t: [(msgs, ring.count(t)), (hots, ring.count(t))])
                ring.run(pe, step, lag=6)
            elif mode == "attend":
                places = Places(nc.tensor, c.node_i, ring, 2, sh.NB * 2 * HEADS)

                def step(i, u):
                    if u == 0:
                        places.load(i)
                    if (t := ring.at(i, u)) is not None:
                        pe.wait_ge(hots, ring.count(t))
                        wait_count(pe, hotTs, ring.count(t, 2))
                        nc.tensor.transpose(psF[u % 2][:, 0:P], hot[:, u, :], c.ident[:, :]).then_inc(turned, 1)
                    if (t := ring.at(i, u, 2)) is not None:
                        k = t[1] // 2 % 2
                        place = places.of(u)
                        pe.wait_ge(hotTs, ring.count(t))
                        done = pairs_done(t, 2)
                        wait_count(pe, zchain, None if done is None else 4 * done)
                        at = 2 * HEADS * (t[1] % 2)
                        nc.tensor.matmul(psN[k][:, at:at + 2 * HEADS], hotT[:, t[1] % 4, :],
                                         c.node[:, :, :].rearrange("p b w -> p (b w)")[:, bass.ds(place, 16)],
                                         start=True, stop=True).then_inc(nodes, 1)
                    gather_sum(i, u, 7, lambda t: msg[:, t[1] % 8, :],
                               lambda t: [(msgs, ring.count(t))])
                ring.run(pe, step, lag=7)
            else:
                def step(i, u):
                    if (t := ring.at(i, u, 4)) is not None:
                        k = t[1] % 4
                        ps = psM[k]
                        pe.wait_ge(outs_, ring.count(t))
                        wait_count(pe, tops, ring.count(t, 4))
                        pe.wait_ge(diag_v, ring.count(t))
                        pe.wait_ge(diag_a, ring.count(t))
                        for half in range(2):
                            o = ps[:, 512 * half:512 * half + 512]
                            nc.tensor.matmul(o, out_of[:, k, :], ident4[:, :, :], start=True, stop=False)
                            last = nc.tensor.matmul(o, hot[:, t[1], :], diag[:, k, 4 * half:4 * half + 4, :], start=False, stop=True)
                        last.then_inc(sums, 1)
                ring.run(pe, step, lag=4)


def norm_steps(nc, c, dve, gate, ring, i, buf, stated):
    stats, moments = buf
    G = ring.size
    for u in range(G):
        last = nc.vector.bn_stats(stats[:, u, :], c.x[:, bass.ds(G * i + u, 1), :].rearrange("p a d -> p (a d)"))
    last.then_inc(stated, 1)
    dve.wait_ge(stated, 3 * i + 1)
    gate.step()
    for u in range(G):
        last = nc.vector.bn_aggr(moments[:, u, :], stats[:, u, :])
    last.then_inc(stated, 1)
    dve.wait_ge(stated, 3 * i + 2)
    nc.vector.tensor_copy(c.stat[:, bass.ds(G * i, G), :], moments[:, :, :]).then_inc(stated, 1)
    dve.wait_ge(stated, 3 * i + 3)
    gate.step()


def norm_ends(nc, c, dve, roots):
    begun, rooted, ended = roots
    nc.vector.tensor_scalar(c.rstd[:, :], c.stat[:, :, 1], EPS, None, ALU.add).then_inc(begun, 1)
    dve.wait_ge(rooted, 1)
    nc.vector.reciprocal(c.rstd[:, :], c.rstd[:, :]).then_inc(ended, 1)
    dve.wait_ge(ended, 1)
    nc.vector.scalar_tensor_tensor(c.nbias[:, :], c.stat[:, :, 0], -1.0, c.rstd[:, :], ALU.mult, ALU.mult)


def norm_roots(nc, c, act, roots):
    begun, rooted, ended = roots
    act.wait_ge(begun, 1)
    nc.scalar.sqrt(c.rstd[:, :], c.rstd[:, :]).then_inc(rooted, 1)


def row(ap, n):
    return ap.rearrange("(a n) -> a n", a=1).to_broadcast([P, n])


def stats_stage(nc, c):
    sh = c.sh
    ring = Ring(sh.NB, 7)
    nm = f"st{c.stage()}"
    with ExitStack() as st:
        sb = lambda name, shape, dt=F32: st.enter_context(nc.sbuf_tensor(f"{name}_{nm}", shape, dt))
        stats, moments = sb("stats", [P, 7, 6]), sb("moments", [P, 7, 2])
        stated = nc.alloc_semaphore(f"stated_{nm}")
        roots = [nc.alloc_semaphore(f"{x}_{nm}") for x in ("begun", "rooted", "ended")]
        block = st.enter_context(nc.Block())

        @block.vector
        def _(dve):
            gate = Gate(dve, c.passed["dve"])
            with dve.Fori(0, ring.rounds) as i:
                norm_steps(nc, c, dve, gate, ring, i, (stats, moments), stated)
            norm_ends(nc, c, dve, roots)

        @block.scalar
        def _(act):
            norm_roots(nc, c, act, roots)


def table_stage(nc, c, layer, edges=None, first=0, end=0):
    sh = c.sh
    G = 7
    ring = Ring(sh.NB, G)
    nm = f"tab{layer}"
    width = {0: D, 1: NREL * D, 2: D + 2 * HEADS, 3: D}[layer]
    blocks = [(a, min(a + 512, width)) for a in range(0, width, 512)]
    NBK = len(blocks)
    with ExitStack() as st:
        sb = lambda name, shape, dt=F32: st.enter_context(nc.sbuf_tensor(f"{name}_{nm}", shape, dt))
        pt = lambda name: st.enter_context(nc.psum_tensor(f"{name}_{nm}", [P, 512], F32))
        sem = lambda name: nc.alloc_semaphore(f"{name}_{nm}")
        w = sb("w", [P, 2, width])
        h = sb("h", [P, G, D])
        hT = sb("hT", [P, G, D])
        SL = G if width < 512 else 3
        out = sb("out", [P, SL, width])
        bias = sb("bias", [P, D])
        att = sb("att", [P, 2, D]) if layer == 2 else None
        prod = sb("prod", [P, 2, D]) if layer == 2 else None
        psT = [pt("psT0"), pt("psT1")]
        psO = [pt(f"psO{k}") for k in range(4)]
        w_in, w_made, hs, turned, hTs, made, outs, noted = [
            sem(x) for x in ("w_in", "w_made", "hs", "turned", "hTs", "made", "outs", "noted")]
        left = [sem(f"left{s}") for s in range(SL)]
        scatter = Scatter(nc, c, edges, first, end)
        block = st.enter_context(nc.Block())

        @block.gpsimd
        def _(pool):
            scatter.run(pool)

        def slot(t):
            return t[1] % SL

        @block.sync
        def _(sp):
            n = 0
            if layer == 0:
                sp.dma_start(w[:, :, :], c.w1t_in[0:D, :].rearrange("(k p) n -> p k n", p=P)).then_inc(w_in, 16)
                sp.dma_start(bias[:, :], row(c.b1_in, D)).then_inc(w_in, 16)
                n = 2
            elif layer == 1:
                for r in range(NREL):
                    sp.dma_start(w[:, :, r * D:(r + 1) * D],
                                 c.wrel_in[r, :, :].rearrange("(k p) n -> p k n", p=P)).then_inc(w_in, 16)
                n = NREL
            elif layer == 2:
                sp.dma_start(w[:, :, 0:D], c.watt_in.rearrange("(k p) n -> p k n", p=P)).then_inc(w_in, 16)
                sp.dma_start(att[:, 0, :], row(c.att_src_in.rearrange("h d -> (h d)"), D)).then_inc(w_in, 16)
                sp.dma_start(att[:, 1, :], row(c.att_dst_in.rearrange("h d -> (h d)"), D)).then_inc(w_in, 16)
                n = 3
            if n:
                sp.wait_ge(w_in, 16 * n)

            def step(i, u):
                t = ring.at(i, u)
                T = ring.count(t) - 1
                rows = sh.LAST if isinstance(T, int) and T == sh.NB - 1 else P
                s = slot(t)
                sp.wait_ge(outs, NBK * ring.count(t))
                if layer == 1:
                    to = c.xtab.rearrange("(r n) d -> n r d", r=NREL)[bass.ds(P * T, rows), :, :]
                    sp.dma_start(to, out[0:rows, s, :].rearrange("p (r d) -> p r d", d=D)).then_inc(left[s], 16)
                elif layer == 2:
                    sp.dma_start(c.gtab[bass.ds(P * T, rows), :], out[0:rows, s, 0:AW]).then_inc(left[s], 16)
                    sp.dma_start(c.stab[bass.ds(P * T, rows), :], out[0:rows, s, D:AW]).then_inc(left[s], 16)
                else:
                    to = c.ptab if layer == 0 else c.htab
                    sp.dma_start(to[bass.ds(P * T, rows), :], out[0:rows, s, :]).then_inc(left[s], 16)

            ring.run(sp, step)
            for s in range(SL):
                per = len([u for u in range(G) if u % SL == s]) * ring.rounds
                sp.wait_ge(left[s], 16 * per * (2 if layer == 2 else 1))

        def wait_left(eng, t):
            s = slot(t)
            per = len([u for u in range(G) if u % SL == s])
            n = per * t[0] + t[1] // SL
            if isinstance(n, int) and n <= 0:
                return
            eng.wait_ge(left[s], (32 if layer == 2 else 16) * n)

        @block.scalar
        def _(act):
            def step(i, u):
                if (t := ring.at(i, u)) is not None:
                    T = ring.count(t) - 1
                    if layer == 3:
                        wait_left(act, t)
                    else:
                        wait_count(act, turned, ring.count(t, G))
                    nc.scalar.activation(h[:, u, :], c.x[:, bass.ds(T, 1), :].rearrange("p a d -> p (a d)"), ACT.Relu,
                                         bias=c.nbias[:, bass.ds(T, 1)], scale=c.rstd[:, bass.ds(T, 1)]).then_inc(hs, 1)
                if layer != 3 and (t := ring.at(i, u, 2)) is not None:
                    act.wait_ge(turned, ring.count(t))
                    wait_count(act, made, ring.count(t, G - 2))
                    nc.scalar.copy(hT[:, t[1], :], psT[t[1] % 2][:, 0:D]).then_inc(hTs, 1)
            ring.run(act, step, lag=2)

        @block.vector
        def _(dve):
            if layer == 2:
                dve.wait_ge(w_in, 48)
                n = 0
                for a in range(2):
                    for k in range(2):
                        nc.vector.tensor_tensor(prod[:, k, :], w[:, k, 0:D], att[:, a, :], ALU.mult).then_inc(w_made, 1)
                        n += 1
                        dve.wait_ge(w_made, n)
                        nc.vector.tensor_reduce(w[:, k, D + HEADS * a:D + HEADS * (a + 1)],
                                                prod[:, k, :].rearrange("p (h d) -> p h d", d=DH), AX.X, ALU.add).then_inc(w_made, 1)
                        n += 1
                        dve.wait_ge(w_made, n)

            def step(i, u):
                t = ring.at(i, u)
                T = ring.count(t) - 1
                wait_left(dve, t)
                if layer == 3:
                    dve.wait_ge(hs, ring.count(t))
                    nc.vector.tensor_scalar(out[:, slot(t), :], h[:, u, :], c.dinv[:, bass.ds(T, 1)], None, ALU.mult).then_inc(outs, 1)
                    return
                if layer == 0:
                    dve.wait_ge(w_in, 32)
                for b, (a, z) in enumerate(blocks):
                    dve.wait_ge(made, NBK * (ring.count(t) - 1) + b + 1)
                    ps = psO[(NBK * u + b) % 4][:, 0:z - a]
                    o = out[:, slot(t), a:z]
                    if layer == 0:
                        last = nc.vector.tensor_tensor(o, ps, bias[:, :], ALU.add)
                    else:
                        last = nc.vector.tensor_copy(o, ps)
                    last.then_inc(outs, 1)
                if layer == 2:
                    nc.vector.tensor_copy(c.node[:, bass.ds(T, 1), 0:2 * HEADS].rearrange("p a w -> p (a w)"),
                                          ps[:, D:D + 2 * HEADS]).then_inc(noted, 1)
            ring.run(dve, step)

        if layer == 3:
            return

        @block.tensor
        def _(pe):
            if layer == 2:
                pe.wait_ge(w_made, 8)
            pe.wait_ge(w_in, {0: 32, 1: 16 * NREL, 2: 48}[layer])

            def step(i, u):
                if (t := ring.at(i, u)) is not None:
                    pe.wait_ge(hs, ring.count(t))
                    wait_count(pe, hTs, ring.count(t, 1 if u == 0 else 2))
                    for k in range(2):
                        last = nc.tensor.transpose(psT[u % 2][:, k * P:(k + 1) * P], h[:, u, k * P:(k + 1) * P], c.ident[:, :])
                    last.then_inc(turned, 1)
                if (t := ring.at(i, u, 1)) is not None:
                    pe.wait_ge(hTs, ring.count(t))
                    for b, (a, z) in enumerate(blocks):
                        n = NBK * (ring.count(t) - 1) + b
                        back = 4 if NBK * t[1] + b >= 4 else (4 if (NBK * G) % 4 == 0 else (NBK * t[1] + b) + 1)
                        if not (isinstance(n, int) and n - back + 1 <= 0):
                            pe.wait_ge(outs, n - back + 1)
                            if layer == 2:
                                pe.wait_ge(noted, n - back + 1)
                        for k in range(2):
                            last = nc.tensor.matmul(psO[(NBK * t[1] + b) % 4][:, 0:z - a], hT[:, t[1], k * P:(k + 1) * P],
                                                    w[:, k, a:z], start=(k == 0), stop=(k == 1))
                        last.then_inc(made, 1)
            ring.run(pe, step, lag=1)


def sage_update(nc, c, edges, first, end):
    sh = c.sh
    G = 7
    ring = Ring(sh.NB, G)
    with ExitStack() as st:
        sb = lambda name, shape, dt=F32: st.enter_context(nc.sbuf_tensor(f"{name}_sage", shape, dt))
        pt = lambda name: st.enter_context(nc.psum_tensor(f"{name}_sage", [P, 512], F32))
        sem = lambda name: nc.alloc_semaphore(f"{name}_sage")
        w = sb("w", [P, 4, D])
        hn = sb("hn", [P, G, 2 * D])
        hnT = sb("hnT", [P, G, 2 * D])
        r, sq = sb("r", [P, G, D]), sb("sq", [P, G, D])
        ss, nrm = sb("ss", [P, G]), sb("nrm", [P, G])
        stats, moments = sb("stats", [P, G, 6]), sb("moments", [P, G, 2])
        psT = [pt("psT0"), pt("psT1")]
        psO = [pt("psO0"), pt("psO1")]
        w_in, hns, turned, turned_back, made, rs, sqs, step_, stated = [sem(x) for x in (
            "w_in", "hns", "turned", "turned_back", "made", "rs", "sqs", "step_", "stated")]
        rooted = sem("rooted")
        roots = [sem(x) for x in ("begun", "rooted_all", "ended")]
        scatter = Scatter(nc, c, edges, first, end)
        block = st.enter_context(nc.Block())

        @block.gpsimd
        def _(pool):
            scatter.run(pool)

        @block.sync
        def _(sp):
            sp.dma_start(w[:, :, :], c.w2t_in.rearrange("(k p) n -> p k n", p=P)).then_inc(w_in, 16)
            sp.wait_ge(w_in, 16)

        @block.scalar
        def _(act):
            def step(i, u):
                if (t := ring.at(i, u)) is not None:
                    T = ring.count(t) - 1
                    wait_count(act, turned, ring.count(t, G))
                    nc.scalar.activation(hn[:, u, 0:D], c.x[:, bass.ds(T, 1), :].rearrange("p a d -> p (a d)"), ACT.Relu,
                                         bias=c.nbias[:, bass.ds(T, 1)], scale=c.rstd[:, bass.ds(T, 1)])
                    nc.scalar.copy(hn[:, u, D:2 * D], c.acc[:, bass.ds(T, 1), 0:D].rearrange("p a d -> p (a d)")).then_inc(hns, 1)
                if (t := ring.at(i, u, 4)) is not None:
                    act.wait_ge(made, ring.count(t))
                    if not (isinstance(t[0], int) and t[0] == 0):
                        act.wait_ge(step_, 3 * t[0])
                    nc.scalar.activation(r[:, t[1], :], psO[t[1] % 2][:, 0:D], ACT.Relu).then_inc(rs, 1)
                    act.wait_ge(rs, ring.count(t))
                    nc.scalar.activation(sq[:, t[1], :], r[:, t[1], :], ACT.Square,
                                         accum_out=ss[:, t[1]:t[1] + 1]).then_inc(sqs, 1)
                    if t[1] == G - 1:
                        act.wait_ge(sqs, ring.count(t))
                        nc.scalar.sqrt(nrm[:, :], ss[:, :]).then_inc(rooted, 1)
            ring.run(act, step, lag=4)
            norm_roots(nc, c, act, roots)

        @block.tensor
        def _(pe):
            pe.wait_ge(w_in, 16)

            def step(i, u):
                if (t := ring.at(i, u)) is not None:
                    pe.wait_ge(hns, ring.count(t))
                    wait_count(pe, turned_back, ring.count(t, 1 if u == 0 else 2))
                    for k in range(4):
                        last = nc.tensor.transpose(psT[u % 2][:, k * P:(k + 1) * P], hn[:, u, k * P:(k + 1) * P], c.ident[:, :])
                    last.then_inc(turned, 1)
                if (t := ring.at(i, u, 2)) is not None:
                    pe.wait_ge(turned_back, ring.count(t))
                    wait_count(pe, rs, ring.count(t, 1 if t[1] == 0 else 2))
                    for k in range(4):
                        last = nc.tensor.matmul(psO[t[1] % 2][:, 0:D], hnT[:, t[1], k * P:(k + 1) * P], w[:, k, :],
                                                start=(k == 0), stop=(k == 3))
                    last.then_inc(made, 1)
            ring.run(pe, step, lag=2)

        @block.vector
        def _(dve):
            def round_end(i):
                dve.wait_ge(rooted, i + 1)
                nc.vector.tensor_scalar(nrm[:, :], nrm[:, :], 1e-12, None, ALU.max).then_inc(step_, 1)
                dve.wait_ge(step_, 3 * i + 1)
                nc.vector.reciprocal(nrm[:, :], nrm[:, :]).then_inc(step_, 1)
                dve.wait_ge(step_, 3 * i + 2)
                for s in range(G):
                    here = c.x[:, bass.ds(G * i + s, 1), :].rearrange("p a d -> p (a d)")
                    last = nc.vector.scalar_tensor_tensor(here, r[:, s, :], nrm[:, s:s + 1], here, ALU.mult, ALU.add)
                last.then_inc(step_, 1)
                dve.wait_ge(step_, 3 * i + 3)
                gate.step()
                norm_steps(nc, c, dve, gate, ring, i, (stats, moments), stated)

            gate = Gate(dve, c.passed["dve"])
            with dve.Fori(0, ring.rounds) as i:
                for s in range(G):
                    t = (i, s)
                    dve.wait_ge(turned, ring.count(t))
                    nc.vector.tensor_copy(hnT[:, s, :], psT[s % 2][:, :]).then_inc(turned_back, 1)
                round_end(i)
            norm_ends(nc, c, dve, roots)


def rgcn_update(nc, c):
    sh = c.sh
    G = 7
    ring = Ring(sh.NB, G)
    with ExitStack() as st:
        sb = lambda name, shape, dt=F32: st.enter_context(nc.sbuf_tensor(f"{name}_rgcn", shape, dt))
        sem = lambda name: nc.alloc_semaphore(f"{name}_rgcn")
        bias = sb("bias", [P, D])
        t1, t2 = sb("t1", [P, G, D]), sb("t2", [P, G, D])
        deg, pos, = sb("deg", [P, sh.NB]), sb("pos", [P, sh.NB])
        stats, moments = sb("stats", [P, G, 6]), sb("moments", [P, G, 2])
        b_in, degs, rooted, t1s, t2s, xs, stated = [sem(x) for x in ("b_in", "degs", "rooted", "t1s", "t2s", "xs", "stated")]
        roots = [sem(x) for x in ("begun", "rooted_all", "ended")]
        block = st.enter_context(nc.Block())

        @block.sync
        def _(sp):
            sp.dma_start(bias[:, :], row(c.bias1_in, D)).then_inc(b_in, 16)
            sp.wait_ge(b_in, 16)

        @block.scalar
        def _(act):
            act.wait_ge(degs, 1)
            nc.scalar.sqrt(deg[:, :], deg[:, :]).then_inc(rooted, 1)
            with act.Fori(0, ring.rounds) as i:
                for s in range(G):
                    act.wait_ge(t1s, G * i + s + 1)
                    if s == 0:
                        act.wait_ge(xs, i)
                    nc.scalar.activation(t2[:, s, :], t1[:, s, :], ACT.Relu).then_inc(t2s, 1)
            norm_roots(nc, c, act, roots)

        @block.vector
        def _(dve):
            gate = Gate(dve, c.passed["dve"])
            counts = c.acc[:, 0:sh.NB, D]
            nc.vector.tensor_scalar(deg[:, :], counts, 1.0, None, ALU.max).then_inc(degs, 1)
            nc.vector.tensor_scalar(pos[:, :], counts, 0.0, None, ALU.is_gt).then_inc(degs, 1)
            dve.wait_ge(rooted, 1)
            nc.vector.reciprocal(deg[:, :], deg[:, :]).then_inc(degs, 1)
            dve.wait_ge(degs, 3)
            nc.vector.tensor_tensor(c.dinv[:, :], deg[:, :], pos[:, :], ALU.mult)
            dve.wait_ge(b_in, 16)
            with dve.Fori(0, ring.rounds) as i:
                dve.wait_ge(t2s, G * i)
                for s in range(G):
                    nc.vector.tensor_tensor(t1[:, s, :], c.acc[:, bass.ds(G * i + s, 1), 0:D].rearrange("p a d -> p (a d)"),
                                            bias[:, :], ALU.add).then_inc(t1s, 1)
                for s in range(G):
                    dve.wait_ge(t2s, G * i + s + 1)
                    here = c.x[:, bass.ds(G * i + s, 1), :].rearrange("p a d -> p (a d)")
                    last = nc.vector.tensor_tensor(here, here, t2[:, s, :], ALU.add)
                last.then_inc(xs, 1)
                dve.wait_ge(xs, i + 1)
                gate.step()
                norm_steps(nc, c, dve, gate, ring, i, (stats, moments), stated)
            norm_ends(nc, c, dve, roots)


def range_stage(nc, c):
    sh = c.sh
    with ExitStack() as st:
        sb = lambda name, shape, dt=F32: st.enter_context(nc.sbuf_tensor(f"{name}_range", shape, dt))
        sem = lambda name: nc.alloc_semaphore(f"{name}_range")
        most, every = sb("most", [P, 2 * HEADS]), sb("every", [P, 2 * HEADS])
        span = sb("span", [P, HEADS])
        widest = sb("widest", [P, 1])
        tops, alls, chain = sem("tops"), sem("alls"), sem("chain")
        block = st.enter_context(nc.Block())
        by_head = c.node[:, 0:sh.NB, 0:HEADS].rearrange("p b h -> p h b")

        @block.gpsimd
        def _(pool):
            pool.wait_ge(tops, 3)
            nc.gpsimd.partition_all_reduce(every[:, :], most[:, :], P, bass.bass_isa.ReduceOp.max).then_inc(alls, 1)

        @block.vector
        def _(dve):
            nc.vector.tensor_reduce(most[:, 0:HEADS], by_head, AX.X, ALU.max).then_inc(tops, 1)
            nc.vector.tensor_reduce(most[:, HEADS:2 * HEADS], by_head, AX.X, ALU.min).then_inc(tops, 1)
            dve.wait_ge(tops, 2)
            nc.vector.tensor_scalar(most[:, HEADS:2 * HEADS], most[:, HEADS:2 * HEADS], -1.0, None, ALU.mult).then_inc(tops, 1)
            dve.wait_ge(alls, 1)
            nc.vector.tensor_tensor(span[:, :], every[:, 0:HEADS], every[:, HEADS:2 * HEADS], ALU.add).then_inc(chain, 1)
            nc.vector.tensor_copy(c.top[:, :, 0:HEADS], every[:, 0:HEADS].unsqueeze(1).to_broadcast([P, sh.NB + 1, HEADS]))
            dve.wait_ge(chain, 1)
            nc.vector.tensor_reduce(widest[:, :], span[:, :], AX.X, ALU.max).then_inc(chain, 1)
            dve.wait_ge(chain, 2)
            nc.vector.tensor_scalar(c.wide[:, :], widest[0:1, :], SPAN, None, ALU.is_gt)


def attention_guard(nc, c):
    sh = c.sh
    with ExitStack() as st:
        sb = lambda name, shape, dt=F32: st.enter_context(nc.sbuf_tensor(f"{name}_guard", shape, dt))
        m, z = sb("m", [P, sh.NB, HEADS]), sb("z", [P, sh.NB, HEADS])
        chain, zs = nc.alloc_semaphore("chain_guard"), nc.alloc_semaphore("zs_guard")
        block = st.enter_context(nc.Block())
        a_src, a_dst = c.node[:, 0:sh.NB, 0:HEADS], c.node[:, 0:sh.NB, HEADS:2 * HEADS]
        top = c.top[:, 0:sh.NB, 0:HEADS]

        @block.vector
        def _(dve):
            n = [0]

            def link(instruction):
                n[0] += 1
                instruction.then_inc(chain, 1)
                dve.wait_ge(chain, n[0])

            nc.vector.tensor_copy(c.own[:, :, :], a_src)
            link(nc.vector.tensor_tensor(m[:, :, :], top, a_src, ALU.max))
            link(nc.vector.tensor_tensor(m[:, :, :], m[:, :, :], a_dst, ALU.add))
            link(nc.vector.tensor_tensor(z[:, :, :], a_src, a_dst, ALU.add))
            link(nc.vector.scalar_tensor_tensor(m[:, :, :], m[:, :, :], SLOPE, m[:, :, :], ALU.mult, ALU.max))
            link(nc.vector.scalar_tensor_tensor(z[:, :, :], z[:, :, :], SLOPE, z[:, :, :], ALU.mult, ALU.max))
            link(nc.vector.tensor_tensor(z[:, :, :], z[:, :, :], m[:, :, :], ALU.subtract))
            link(nc.vector.tensor_copy(c.node[:, 0:sh.NB, 0:HEADS], a_dst))
            nc.vector.tensor_copy(c.node[:, 0:sh.NB, HEADS:2 * HEADS], m[:, :, :]).then_inc(zs, 1)
            nc.vector.memset(c.node[:, sh.NB, :], 0.0)

        @block.scalar
        def _(act):
            act.wait_ge(zs, 1)
            nc.scalar.activation(c.own[:, :, :], z[:, :, :], ACT.Exp)


def attention_update(nc, c):
    sh = c.sh
    G = 7
    ring = Ring(sh.NB, G)
    N = sh.N
    with ExitStack() as st:
        sb = lambda name, shape, dt=F32: st.enter_context(nc.sbuf_tensor(f"{name}_gat", shape, dt))
        pt = lambda name: st.enter_context(nc.psum_tensor(f"{name}_gat", [P, 512], F32))
        sem = lambda name: nc.alloc_semaphore(f"{name}_gat")
        own_row = sb("own_row", [P, G, AW])
        prod = sb("prod", [P, G, D])
        sq, h = sb("sq", [P, G, D]), sb("h", [P, G, D])
        bias, gamma, beta = sb("bias", [P, D]), sb("gamma", [P, D]), sb("beta", [P, D])
        mean, scale = sb("mean", [P, D]), sb("scale", [P, D])
        rden = sb("rden", [P, sh.NB, HEADS])
        stats, moments = sb("stats", [P, G, 6]), sb("moments", [P, G, 2])
        psM, psV = pt("psM"), pt("psV")
        par_in, rowed, chain, summed, centred, squared, varied, hs, xs, stated, freed = [sem(x) for x in (
            "par_in", "rowed", "chain", "summed", "centred", "squared", "varied", "hs", "xs", "stated", "freed")]
        zeroed, varied_rows = sem("zeroed"), sem("varied_rows")
        roots = [sem(x) for x in ("begun", "rooted_all", "ended")]
        var_in, var_root = sem("var_in"), sem("var_root")
        own_in = [sem(f"own_in{s}") for s in range(G)]
        block = st.enter_context(nc.Block())
        flat = lambda ap: ap.rearrange("p a d -> p (a d)")
        heads = lambda ap: ap.rearrange("p (h d) -> p h d", d=DH)
        spread = lambda ap: ap.rearrange("p a h -> p (a h)").unsqueeze(2).to_broadcast([P, HEADS, DH])

        @block.sync
        def _(sp):
            for to, of in ((bias, c.bias2_in), (gamma, c.gamma_in), (beta, c.beta_in)):
                sp.dma_start(to[:, :], row(of, D)).then_inc(par_in, 16)
            sp.wait_ge(zeroed, 1)

            def step(i, u):
                t = ring.at(i, u)
                T = ring.count(t) - 1
                rows = sh.LAST if isinstance(T, int) and T == sh.NB - 1 else P
                wait_count(sp, freed, ring.count(t, G))
                sp.dma_start(own_row[0:rows, u, :], c.gtab[bass.ds(P * T, rows), :]).then_inc(own_in[u], 16)
            ring.run(sp, step)
            sp.wait_ge(par_in, 48)

        @block.vector
        def _(dve):
            gate = Gate(dve, c.passed["dve"])
            nc.vector.memset(own_row[:, :, :], 0.0).then_inc(zeroed, 1)
            nc.vector.tensor_tensor(rden[:, :, :], c.acc[:, 0:sh.NB, D:AW], c.own[:, :, :], ALU.add).then_inc(chain, 1)
            dve.wait_ge(chain, 1)
            nc.vector.reciprocal(rden[:, :, :], rden[:, :, :]).then_inc(chain, 1)
            dve.wait_ge(chain, 2)
            dve.wait_ge(par_in, 48)

            def mean_rows(i):
                dve.wait_ge(rowed, 3 * i)
                for s in range(G):
                    dve.wait_ge(own_in[s], 16 * (i + 1))
                    nc.vector.tensor_tensor(heads(prod[:, s, :]), heads(own_row[:, s, 0:D]),
                                            spread(c.own[:, bass.ds(G * i + s, 1), :]), ALU.mult).then_inc(freed, 1)
                dve.wait_ge(freed, G * i + G)
                for s in range(G):
                    last = nc.vector.tensor_tensor(prod[:, s, :], prod[:, s, :], flat(c.acc[:, bass.ds(G * i + s, 1), 0:D]), ALU.add)
                last.then_inc(rowed, 1)
                dve.wait_ge(rowed, 3 * i + 1)
                for s in range(G):
                    last = nc.vector.tensor_tensor(heads(prod[:, s, :]), heads(prod[:, s, :]),
                                                   spread(rden[:, bass.ds(G * i + s, 1), :]), ALU.mult)
                last.then_inc(rowed, 1)
                dve.wait_ge(rowed, 3 * i + 2)
                for s in range(G):
                    last = nc.vector.tensor_tensor(flat(c.acc[:, bass.ds(G * i + s, 1), 0:D]), prod[:, s, :], bias[:, :], ALU.add)
                last.then_inc(rowed, 1)

            with dve.Fori(0, ring.rounds) as i:
                mean_rows(i)
            dve.wait_ge(summed, 1)
            nc.vector.tensor_scalar(mean[:, :], psM[:, 0:D], 1.0 / N, None, ALU.mult).then_inc(chain, 1)
            dve.wait_ge(chain, 3)
            with dve.Fori(0, sh.NB) as T:
                here = flat(c.acc[:, bass.ds(T, 1), 0:D])
                nc.vector.tensor_tensor(here, here, mean[:, :], ALU.subtract).then_inc(centred, 1)
            dve.wait_ge(varied, 1)
            nc.vector.tensor_scalar(scale[:, :], psV[:, 0:D], 1.0 / N, EPS, ALU.mult, ALU.add).then_inc(var_in, 1)
            dve.wait_ge(var_root, 1)
            nc.vector.reciprocal(scale[:, :], scale[:, :]).then_inc(chain, 1)
            dve.wait_ge(chain, 4)
            nc.vector.tensor_tensor(scale[:, :], scale[:, :], gamma[:, :], ALU.mult).then_inc(chain, 1)
            dve.wait_ge(chain, 5)
            dve.wait_ge(centred, sh.NB)
            with dve.Fori(0, ring.rounds) as i:
                dve.wait_ge(xs, 3 * i)
                for s in range(G):
                    nc.vector.tensor_tensor(prod[:, s, :], flat(c.acc[:, bass.ds(G * i + s, 1), 0:D]), scale[:, :], ALU.mult)
                    dve.wait_ge(hs, G * i + s + 1)
                    here = flat(c.x[:, bass.ds(G * i + s, 1), :])
                    last = nc.vector.tensor_tensor(here, here, h[:, s, :], ALU.add)
                last.then_inc(xs, 1)
                dve.wait_ge(xs, 3 * i + 1)
                for s in range(G):
                    last = nc.vector.tensor_tensor(prod[:, s, :], prod[:, s, :], beta[:, :], ALU.add)
                last.then_inc(xs, 1)
                dve.wait_ge(xs, 3 * i + 2)
                for s in range(G):
                    here = flat(c.x[:, bass.ds(G * i + s, 1), :])
                    last = nc.vector.tensor_tensor(here, here, prod[:, s, :], ALU.add)
                last.then_inc(xs, 1)
                dve.wait_ge(xs, 3 * i + 3)
                gate.step()
                norm_steps(nc, c, dve, gate, ring, i, (stats, moments), stated)
            norm_ends(nc, c, dve, roots)

        @block.scalar
        def _(act):
            with act.Fori(0, ring.rounds) as i:
                for s in range(G):
                    act.wait_ge(centred, G * i + s + 1)
                    if s == 0:
                        act.wait_ge(varied_rows, G * i)
                    nc.scalar.activation(sq[:, s, :], flat(c.acc[:, bass.ds(G * i + s, 1), 0:D]), ACT.Square).then_inc(squared, 1)
            act.wait_ge(var_in, 1)
            nc.scalar.sqrt(scale[:, :], scale[:, :]).then_inc(var_root, 1)
            with act.Fori(0, ring.rounds) as i:
                act.wait_ge(xs, 3 * i)
                for s in range(G):
                    T = G * i + s
                    nc.scalar.activation(h[:, s, :], flat(c.x[:, bass.ds(T, 1), :]), ACT.Relu,
                                         bias=c.nbias[:, bass.ds(T, 1)], scale=c.rstd[:, bass.ds(T, 1)]).then_inc(hs, 1)
            norm_roots(nc, c, act, roots)

        @block.tensor
        def _(pe):
            def over_nodes(rows_of, ps, ready, done, each):
                def step(i, u):
                    t = ring.at(i, u)
                    T = ring.count(t) - 1
                    rows = sh.LAST if isinstance(T, int) and T == sh.NB - 1 else P
                    ready(t)
                    last = nc.tensor.matmul(ps[:, 0:D], c.ones[0:rows, :], rows_of(T, u, rows),
                                            start=isinstance(T, int) and T == 0, stop=isinstance(T, int) and T == sh.NB - 1,
                                            skip_group_check=True)
                    if each is not None:
                        last.then_inc(each, 1)
                ring.run(pe, step)
                nc.tensor.matmul(ps[:, 256:258], c.ones[:, :], c.ones[:, 0:2], start=False, stop=True,
                                 skip_group_check=True).then_inc(done, 1)

            over_nodes(lambda T, u, rows: c.acc[0:rows, bass.ds(T, 1), 0:D].rearrange("p a d -> p (a d)"), psM,
                       lambda t: pe.wait_ge(rowed, 3 * t[0] + 3) if t[1] == 0 else None, summed, None)
            over_nodes(lambda T, u, rows: sq[0:rows, u, :], psV,
                       lambda t: pe.wait_ge(squared, ring.count(t)), varied, varied_rows)


def gcn_output(nc, c):
    sh = c.sh
    G = 7
    ring = Ring(sh.NB, G)
    with ExitStack() as st:
        sb = lambda name, shape, dt=F32: st.enter_context(nc.sbuf_tensor(f"{name}_gcn", shape, dt))
        pt = lambda name: st.enter_context(nc.psum_tensor(f"{name}_gcn", [P, 512], F32))
        sem = lambda name: nc.alloc_semaphore(f"{name}_gcn")
        w, bias = sb("w", [P, 2, D]), sb("bias", [P, D])
        a, aT = sb("a", [P, G, D]), sb("aT", [P, G, D])
        y, z = sb("y", [P, G, D]), sb("z", [P, G, D])
        psT = [pt("psT0"), pt("psT1")]
        psO = [pt("psO0"), pt("psO1")]
        w_in, scaled, turned, aTs, made, ys, zs, outs = [sem(x) for x in (
            "w_in", "scaled", "turned", "aTs", "made", "ys", "zs", "outs")]
        left = [sem(f"left{s}") for s in range(G)]
        block = st.enter_context(nc.Block())
        flat = lambda ap: ap.rearrange("p a d -> p (a d)")

        @block.sync
        def _(sp):
            sp.dma_start(w[:, :, :], c.w3_in.rearrange("(k p) n -> p k n", p=P)).then_inc(w_in, 16)
            sp.dma_start(bias[:, :], row(c.bias3_in, D)).then_inc(w_in, 16)

            def step(i, u):
                t = ring.at(i, u)
                T = ring.count(t) - 1
                rows = sh.LAST if isinstance(T, int) and T == sh.NB - 1 else P
                sp.wait_ge(outs, ring.count(t))
                sp.dma_start(c.out[bass.ds(P * T, rows), :], z[0:rows, u, :]).then_inc(left[u], 16)
            ring.run(sp, step)
            sp.wait_ge(w_in, 32)
            for s in range(G):
                sp.wait_ge(left[s], 16 * ring.rounds)

        @block.scalar
        def _(act):
            def step(i, u):
                if (t := ring.at(i, u)) is not None:
                    T = ring.count(t) - 1
                    wait_count(act, turned, ring.count(t, G))
                    nc.scalar.activation(a[:, u, :], flat(c.acc[:, bass.ds(T, 1), 0:D]), ACT.Copy,
                                         scale=c.dinv[:, bass.ds(T, 1)]).then_inc(scaled, 1)
                if (t := ring.at(i, u, 2)) is not None:
                    act.wait_ge(turned, ring.count(t))
                    wait_count(act, made, ring.count(t, G - 2))
                    nc.scalar.copy(aT[:, t[1], :], psT[t[1] % 2][:, 0:D]).then_inc(aTs, 1)
            ring.run(act, step, lag=2)

        @block.tensor
        def _(pe):
            pe.wait_ge(w_in, 32)

            def step(i, u):
                if (t := ring.at(i, u)) is not None:
                    pe.wait_ge(scaled, ring.count(t))
                    wait_count(pe, aTs, ring.count(t, 1 if u == 0 else 2))
                    for k in range(2):
                        last = nc.tensor.transpose(psT[u % 2][:, k * P:(k + 1) * P], a[:, u, k * P:(k + 1) * P], c.ident[:, :])
                    last.then_inc(turned, 1)
                if (t := ring.at(i, u, 1)) is not None:
                    pe.wait_ge(aTs, ring.count(t))
                    wait_count(pe, ys, ring.count(t, 1 if t[1] == 0 else 2))
                    for k in range(2):
                        last = nc.tensor.matmul(psO[t[1] % 2][:, 0:D], aT[:, t[1], k * P:(k + 1) * P], w[:, k, :],
                                                start=(k == 0), stop=(k == 1))
                    last.then_inc(made, 1)
            ring.run(pe, step, lag=1)

        @block.vector
        def _(dve):
            dve.wait_ge(w_in, 32)

            def step(i, u):
                if (t := ring.at(i, u)) is not None:
                    dve.wait_ge(made, ring.count(t))
                    wait_count(dve, outs, ring.count(t, G))
                    nc.vector.tensor_tensor(y[:, u, :], psO[u % 2][:, 0:D], bias[:, :], ALU.add).then_inc(ys, 1)
                if (t := ring.at(i, u, 2)) is not None:
                    dve.wait_ge(ys, ring.count(t))
                    if not (isinstance(t[0], int) and t[0] == 0):
                        dve.wait_ge(left[t[1]], 16 * t[0])
                    nc.vector.scalar_tensor_tensor(z[:, t[1], :], y[:, t[1], :], SLOPE, y[:, t[1], :], ALU.mult, ALU.max).then_inc(zs, 1)
                if (t := ring.at(i, u, 4)) is not None:
                    dve.wait_ge(zs, ring.count(t))
                    nc.vector.tensor_tensor(z[:, t[1], :], z[:, t[1], :], flat(c.x[:, bass.ds(ring.count(t) - 1, 1), :]),
                                            ALU.add).then_inc(outs, 1)
            ring.run(dve, step, lag=4)


class Core:

    def __init__(self, sh):
        self.sh = sh
        self.stages = 0

    def stage(self):
        self.stages += 1
        return self.stages


def stage(nc, build, *args):
    with nc.cleanup_on_exit():
        build(nc, *args)


def gnn_stack(nc, x_in, src_in, dst_in, attr_in, type_in, w1t_in, b1_in, w2t_in, wrel_in, bias1_in, watt_in,
              att_src_in, att_dst_in, bias2_in, gamma_in, beta_in, w3_in, bias3_in, out):
    sh = Shapes(x_in.shape[0], src_in.shape[0])
    c = Core(sh)
    c.x_in, c.src_in, c.dst_in, c.attr_in, c.type_in = x_in, src_in, dst_in, attr_in, type_in
    c.w1t_in, c.b1_in, c.w2t_in = w1t_in, b1_in, w2t_in
    c.wrel_in, c.bias1_in = wrel_in, bias1_in
    c.watt_in, c.att_src_in, c.att_dst_in = watt_in, att_src_in, att_dst_in
    c.bias2_in, c.gamma_in, c.beta_in, c.w3_in, c.bias3_in, c.out = bias2_in, gamma_in, beta_in, w3_in, bias3_in, out
    dram = lambda name, shape: nc.dram_tensor("dram_" + name, shape, F32, kind="Internal").ap()
    c.rec_dst, c.rec_src = dram("rec_dst", [sh.EP, REC]), dram("rec_src", [sh.EP, REC])
    c.ptab, c.xtab = dram("ptab", [sh.N, D]), dram("xtab", [NREL * sh.N, D])
    c.gtab, c.stab, c.htab = dram("gtab", [sh.N, AW]), dram("stab", [sh.N, HEADS]), dram("htab", [sh.N, D])
    with ExitStack() as ctx:
        sb = lambda name, shape, dt=F32: ctx.enter_context(nc.sbuf_tensor(name, shape, dt))
        c.tiles = {k: (sb(f"base_{k}", [P, sh.NT]), sb(f"place_{k}", [1, sh.NT], I32), sb(f"off_{k}", [1, sh.NT], I32))
                   for k in ("dst", "src")}
        c.node_i = sb("node_i", [1, sh.NT], I32)
        c.unsorted, c.wide = sb("unsorted", [1, 1], I32), sb("wide", [1, 1], I32)
        c.passed = {e: ctx.enter_context(nc.semaphore(f"passed_{e}")) for e in ("sp", "dve", "pool")}
        constants(nc, c, ctx)
        rounds = sh.COLS // U
        with ExitStack() as by_dst:
            edges = Edges(nc, c, "dst", by_dst)
            stage(nc, list_stage, c, edges)
            with nc.If(nc.values_load(c.unsorted[0:1, 0:1], min_val=0, max_val=sh.E) != 0):
                stage(nc, place_stage, c, edges)
                stage(nc, scatter_stage, c, edges, 0, rounds)
            nc.all_engine_barrier()
        with ExitStack() as by_src:
            edges = Edges(nc, c, "src", by_src)
            stage(nc, list_stage, c, edges)
            stage(nc, place_stage, c, edges)
            cuts = [round(rounds * share) for share in (0.0, 0.33, 0.56, 1.0)]
            stage(nc, stats_stage, c)
            stage(nc, table_stage, c, 0, edges, cuts[0], cuts[1])
            with nc.sbuf_tensor("sage_sums", [P, sh.NB + 1, AW], F32) as c.acc:
                stage(nc, edge_pass, c, "dst", c.ptab, D, 0, "edge_mlp")
                stage(nc, sage_update, c, edges, cuts[1], cuts[2])
            stage(nc, table_stage, c, 1, edges, cuts[2], cuts[3])
        c.acc = sb("sums", [P, sh.NB + 1, AW])
        c.top, c.node = sb("top", [P, sh.NB + 1, 2 * HEADS]), sb("node", [P, sh.NB + 1, 2 * HEADS])
        c.own = sb("own", [P, sh.NB, HEADS])
        c.dinv = sb("dinv", [P, sh.NB])
        stage(nc, edge_pass, c, "src", c.xtab, D, 0, "plain")
        stage(nc, rgcn_update, c)
        stage(nc, table_stage, c, 2)
        stage(nc, range_stage, c)
        with nc.If(nc.values_load(c.wide[0:1, 0:1], min_val=0, max_val=1) != 0):
            stage(nc, edge_pass, c, "dst", c.stab, HEADS, 0, "max")
        nc.all_engine_barrier()
        stage(nc, attention_guard, c)
        stage(nc, edge_pass, c, "dst", c.gtab, AW, 0, "attend")
        stage(nc, attention_update, c)
        stage(nc, table_stage, c, 3)
        stage(nc, edge_pass, c, "src", c.htab, D, 2, "plain")
        stage(nc, gcn_output, c)


def kernel(x, src, dst, edge_attr_3, edge_type_8, L0_gnn_W1, L0_gnn_b1, L0_gnn_W2, L1_gnn_weight, L1_gnn_bias,
           L2_gnn_W, L2_gnn_att_src, L2_gnn_att_dst, L2_gnn_bias, L2_gnn_gamma, L2_gnn_beta, L3_gnn_W, L3_gnn_b):
    import concourse.bacc as bacc
    from concourse.bass_utils import run_bass_kernel_spmd

    arrays = {
        "x_in": x, "src_in": src, "dst_in": dst, "attr_in": np.asarray(edge_attr_3).reshape(-1), "type_in": edge_type_8,
        "w1t_in": np.asarray(L0_gnn_W1).T, "b1_in": L0_gnn_b1, "w2t_in": np.asarray(L0_gnn_W2).T,
        "wrel_in": L1_gnn_weight, "bias1_in": L1_gnn_bias, "watt_in": L2_gnn_W, "att_src_in": L2_gnn_att_src,
        "att_dst_in": L2_gnn_att_dst, "bias2_in": L2_gnn_bias, "gamma_in": L2_gnn_gamma, "beta_in": L2_gnn_beta,
        "w3_in": L3_gnn_W, "bias3_in": L3_gnn_b,
    }
    arrays = {k: np.ascontiguousarray(v) for k, v in arrays.items()}
    nc = bacc.Bacc("TRN2", target_bir_lowering=False, num_devices=1)
    args = {k: nc.dram_tensor(k, v.shape, mybir.dt.from_np(v.dtype), kind="ExternalInput").ap() for k, v in arrays.items()}
    out = nc.dram_tensor("out", arrays["x_in"].shape, F32, kind="ExternalOutput").ap()
    gnn_stack(nc, **args, out=out)
    r = run_bass_kernel_spmd(nc, [arrays], core_ids=[0])
    return r.results[0]["out"]
```

```python
from contextlib import ExitStack

import numpy as np

import concourse.bass as bass
from concourse import mybir

F32 = mybir.dt.float32
BF16 = mybir.dt.bfloat16
I32 = mybir.dt.int32
ALU = mybir.AluOpType
ACT = mybir.ActivationFunctionType
AX = mybir.AxisListType
P = 128
D = 256
HEADS, DH = 8, 32
NREL = 8
EPS = 1e-5
SLOPE = 0.2
CUTS = 0.04, 0.12, 0.27, 0.52
U = 16
REC = 8
PLACE = 7
AW = D + HEADS
BIG = 1e30
SPAN = 60.0


class Ring:

    def __init__(self, n, size):
        assert n % size == 0 and n // size >= 3
        self.n, self.size, self.rounds = n, size, n // size

    def at(self, i, u, back=0):
        q, s = divmod(u - back, self.size)
        j = i + q
        if isinstance(j, int) and not 0 <= self.size * j + s < self.n:
            return None
        return j, s

    def count(self, t, back=0):
        c = self.size * t[0] + t[1] + 1 - back
        return None if isinstance(c, int) and c <= 0 else c

    def run(self, eng, step, lag=0):
        for u in range(self.size):
            step(0, u)
        with eng.Fori(1, self.rounds - 1) as i:
            for u in range(self.size):
                step(i, u)
        for u in range(self.size):
            step(self.rounds - 1, u)
        for u in range(lag):
            step(self.rounds, u)


def peeled(eng, n, body):
    body(0)
    with eng.Fori(1, n) as i:
        body(i)


def wait_count(eng, sem, count):
    if count is not None and not (isinstance(count, int) and count <= 0):
        eng.wait_ge(sem, count)


class Places:

    def __init__(self, eng, values, ring, back, max_val):
        self.eng, self.values, self.ring, self.back, self.max_val = eng, values, ring, back, max_val

    def load(self, i):
        there = [(u, t) for u in range(self.ring.size) if (t := self.ring.at(i, u, self.back)) is not None]
        first, n = self.ring.count(there[0][1]) - 1, len(there)
        _, held = self.eng.bass.values_load_multi_w_load_instructions(
            self.values[0:1, bass.ds(first, n)], engines=[self.eng.engine], min_val=0, max_val=self.max_val,
            skip_runtime_bounds_check_because="the lists hold at most NB buckets' places, and offsets up to EP - P")
        self.held = {u: v for (u, _), v in zip(there, held)}

    def of(self, u):
        return self.held[u]


class Gate:

    def __init__(self, eng, semaphore):
        self.eng, self.semaphore = eng, semaphore

    def step(self):
        self.eng.sem_inc(self.semaphore, 1)


class Shapes:
    def __init__(self, n_nodes, n_edges):
        self.N, self.E = n_nodes, n_edges
        self.NB = -(-n_nodes // P)
        self.LAST = n_nodes - (self.NB - 1) * P
        cols = -(-n_edges // P)
        self.COLS = -(-cols // U) * U
        self.EP = P * self.COLS
        tiles = (n_edges + self.NB * (P - 1)) // P
        self.NT = -(-tiles // U) * U
        self.ND = -(-self.NB // 4) * 4
        assert n_edges > (P - 1) * self.COLS
        self.NOWHERE = float(P * (self.NB + 3))


def constants(nc, c, ctx):
    sh = c.sh
    sb = lambda name, shape, dt: ctx.enter_context(nc.sbuf_tensor(name, shape, dt))
    c.iota = sb("iota", [P, P], F32)
    c.iota_bf = sb("iota_bf", [P, P], BF16)
    c.ident = sb("ident", [P, P], F32)
    c.ident_bf = sb("ident_bf", [P, P], BF16)
    c.ones = sb("ones", [P, P], F32)
    c.x = sb("x_sb", [P, sh.NB, D], F32)
    c.stat = sb("stat", [P, sh.NB, 2], F32)
    c.rstd = sb("rstd", [P, sh.NB], F32)
    c.nbias = sb("nbias", [P, sh.NB], F32)
    with ExitStack() as st:
        sem = lambda name: nc.alloc_semaphore(name)
        made = sem("made")
        block = st.enter_context(nc.Block())

        @block.gpsimd
        def _(pool):
            nc.gpsimd.iota(c.iota[:, :], pattern=[[1, P]], base=0, channel_multiplier=0,
                           allow_small_or_imprecise_dtypes=True)
            nc.gpsimd.iota(c.iota_bf[:, :], pattern=[[1, P]], base=0, channel_multiplier=0,
                           allow_small_or_imprecise_dtypes=True)
            nc.gpsimd.memset(c.ones[:, :], 1.0).then_inc(made, 1)
            nc.gpsimd.memset(c.ident[:, :], 0.0).then_inc(made, 1)
            nc.gpsimd.memset(c.ident_bf[:, :], 0.0).then_inc(made, 1)
            pool.wait_ge(made, 3)
            for m in (c.ident, c.ident_bf):
                nc.gpsimd.affine_select(out=m[:, :], in_=m[:, :], compare_op=ALU.not_equal, fill=1.0,
                                        base=0, pattern=[[-1, P]], channel_multiplier=1)

        @block.vector
        def _(dve):
            nc.vector.memset(c.x[:, sh.NB - 1, :], 0.0)


class Edges:

    def __init__(self, nc, c, kind, ctx):
        sh = c.sh
        sb = lambda name, shape, dt=F32: ctx.enter_context(nc.sbuf_tensor(f"{name}_{kind}", shape, dt))
        self.kind = kind
        self.rec = sb("rec", [P, sh.COLS, REC])
        self.key = sb("key", [P, sh.COLS])
        self.offs = sb("offs", [P, sh.ND])
        self.digits = sb("digits", [P, sh.ND])
        self.stage_rec = sb("stage_rec", [P, 2, U // 2, REC])
        self.to = c.rec_dst if kind == "dst" else c.rec_src


def list_stage(nc, c, edges, other=None, first=0, end=0):
    sh = c.sh
    NB, ND, COLS, NT = sh.NB, sh.ND, sh.COLS, sh.NT
    kind = edges.kind
    by_dst = kind == "dst"
    rec, key, offs, digits = edges.rec, edges.key, edges.offs, edges.digits
    base_f, place_i, off_i = c.tiles[kind]
    own = sh.E - (P - 1) * COLS
    counts_ring = Ring(ND, 4)
    with ExitStack() as st:
        sb = lambda name, shape, dt=F32: st.enter_context(nc.sbuf_tensor(f"{name}_{kind}", shape, dt))
        sem = lambda name: nc.alloc_semaphore(f"{name}_{kind}")
        src_i, dst_i = sb("src_i", [P, COLS], I32), sb("dst_i", [P, COLS], I32)
        third = sb("third", [P, COLS * 3] if by_dst else [P, COLS], F32 if by_dst else I32)
        next_i = sb("next_i", [P, COLS], I32) if by_dst else None
        rest = sb("rest", [P, COLS * 3]) if by_dst else None
        key_i, mask = sb("key_i", [P, COLS], I32), sb("mask", [P, COLS])
        key_bf, same = sb("key_bf", [P, COLS], BF16), sb("same", [P, 4, COLS], BF16)
        allone = sb("allone", [P, ND])
        falls = sb("falls", [P, 1])
        counts, tot, incl = sb("counts", [P, ND]), sb("tot", [P, ND]), sb("incl", [P, ND])
        before = sb("before", [P, P])
        upto = sb("upto", [P, P])
        nb, nt_i, nt, over = sb("nb", [P, 1]), sb("nt_i", [P, 1], I32), sb("nt", [P, 1]), sb("over", [P, 1])
        past, tile_no = sb("past", [P, NT]), sb("tile_no", [P, NT])
        off_f = sb("off_f", [P, NT])
        ps = [st.enter_context(nc.psum_tensor(f"ps{k}_{kind}", [P, 512], F32)) for k in range(8)]
        loaded, zeroed, tri = sem("loaded"), sem("zeroed"), sem("tri")
        counted, totals, tiled = sem("counted"), sem("totals"), sem("tiled")
        prefixed, listed, summed, compared, fallen = [sem(x) for x in ("prefixed", "listed", "summed", "compared", "fallen")]
        chain, recorded, written, x_in = sem("chain"), sem("recorded"), sem("written"), sem("x_in")
        scatter = Scatter(nc, c, other, first, end)
        block = st.enter_context(nc.Block())
        halves = ((0, 512), (512, NT)) if NT > 512 else ((0, NT),)
        loads = 3 * 2 + (2 if by_dst else 0)

        @block.sync
        def _(sp):
            sp.wait_ge(zeroed, 2)
            parts = [(src_i, c.src_in, 1, 0), (dst_i, c.dst_in, 1, 0),
                     (third, c.attr_in if by_dst else c.type_in, 3 if by_dst else 1, 0)]
            if by_dst:
                parts.append((next_i, c.dst_in, 1, 1))
            for to, of, w, ahead in parts:
                full = (P - 1) * COLS * w
                sp.dma_start(to[0:P - 1, :], of[ahead:full + ahead].rearrange("(p n) -> p n", p=P - 1)).then_inc(loaded, 16)
                sp.dma_start(to[P - 1:P, 0:own * w - ahead], of[full + ahead:full + own * w].rearrange("(p n) -> p n", p=1)
                             ).then_inc(loaded, 16)
            if not by_dst:
                full = (sh.NB - 1) * P
                sp.dma_start(c.x[:, 0:sh.NB - 1, :],
                             c.x_in[0:full, :].rearrange("(i p) d -> p i d", p=P)).then_inc(x_in, 16)
                sp.dma_start(c.x[0:sh.LAST, sh.NB - 1, :], c.x_in[full:sh.N, :]).then_inc(x_in, 16)
                sp.wait_ge(x_in, 32)
            sp.wait_ge(loaded, 16 * loads)
            if by_dst:
                sp.wait_ge(recorded, 1)
                sp.dma_start(edges.to.rearrange("(p n) w -> p (n w)", p=P), rec[:, :, :].rearrange("p n w -> p (n w)")).then_inc(written, 16)
                sp.wait_ge(written, 16)

        @block.gpsimd
        def _(pool):
            nc.gpsimd.memset(third[:, :], 0.0 if by_dst else 0).then_inc(zeroed, 1)
            nc.gpsimd.iota(digits[:, :], pattern=[[1, ND]], base=0, channel_multiplier=0,
                           allow_small_or_imprecise_dtypes=True)
            nc.gpsimd.iota(tile_no[:, :], pattern=[[1, NT]], base=0, channel_multiplier=0,
                           allow_small_or_imprecise_dtypes=True)
            nc.gpsimd.memset(before[:, :], 1.0)
            nc.gpsimd.memset(upto[:, :], 1.0).then_inc(tri, 1)
            pool.wait_ge(tri, 1)
            nc.gpsimd.affine_select(out=before[:, :], in_=before[:, :], compare_op=ALU.is_gt, fill=0.0,
                                    base=0, pattern=[[1, P]], channel_multiplier=-1)
            nc.gpsimd.affine_select(out=upto[:, :], in_=upto[:, :], compare_op=ALU.is_ge, fill=0.0,
                                    base=0, pattern=[[1, P]], channel_multiplier=-1).then_inc(tri, 1)
            scatter.run(pool)

        @block.vector
        def _(dve):
            chained = [0]

            def link(instruction):
                chained[0] += 1
                instruction.then_inc(chain, 1)
                dve.wait_ge(chain, chained[0])

            nc.vector.memset(allone[:, :], 1.0)
            nc.vector.memset(src_i[:, :], 0 if by_dst else int(sh.NOWHERE))
            if by_dst:
                nc.vector.memset(next_i[:, :], int(sh.NOWHERE))
            nc.vector.memset(dst_i[:, :], int(sh.NOWHERE) if by_dst else 0).then_inc(zeroed, 1)
            link(nc.vector.memset(rec[:, :, :], 0.0))
            dve.wait_ge(loaded, 16 * loads)
            node_i = dst_i if by_dst else src_i
            rec_i = rec[:, :, :].bitcast(I32)
            link(nc.vector.tensor_single_scalar(key_i[:, :], node_i[:, :], 7, ALU.arith_shift_right))
            nc.vector.tensor_copy(rec[:, :, 1], node_i[:, :])
            nc.vector.tensor_copy(key_bf[:, :], key_i[:, :])
            link(nc.vector.tensor_copy(key[:, :], key_i[:, :]))
            dve.wait_ge(tri, 2)
            def count(i, u):
                t = counts_ring.at(i, u)
                wait_count(dve, counted, counts_ring.count(t, 4))
                d = counts_ring.count(t) - 1
                nc.vector.tensor_scalar(same[:, u, :], key_bf[:, :], digits[:, bass.ds(d, 1)], None, ALU.is_equal,
                                        ALU.add, accum_out=counts[:, bass.ds(d, 1)]).then_inc(counted, 1)
            counts_ring.run(dve, count)
            dve.wait_ge(counted, ND)
            if by_dst:
                nc.vector.tensor_copy(rec_i[:, :, 0], src_i[:, :])
                part = lambda k: rec[:, :, :].bitcast(BF16)[:, :, 4 + 3 * k:7 + 3 * k]
                of3 = lambda ap: ap[:, :].rearrange("p (n k) -> p n k", k=3)
                link(nc.vector.tensor_copy(part(0), of3(third)))
                link(nc.vector.tensor_tensor(of3(rest), of3(third), part(0), ALU.subtract))
                link(nc.vector.tensor_copy(part(1), of3(rest)))
                link(nc.vector.tensor_tensor(of3(rest), of3(rest), part(1), ALU.subtract))
                nc.vector.tensor_copy(part(2), of3(rest)).then_inc(recorded, 1)
                nc.vector.tensor_tensor(mask[:, :], dst_i[:, :], next_i[:, :], ALU.is_gt).then_inc(compared, 1)
                dve.wait_ge(compared, 1)
                nc.vector.tensor_reduce(falls[:, :], mask[:, :], AX.X, ALU.add).then_inc(compared, 1)
            else:
                nc.vector.tensor_copy(rec_i[:, :, 2], dst_i[:, :])
                link(nc.vector.tensor_scalar(rec_i[:, :, 0], third[:, :], sh.N, None, ALU.mult))
                link(nc.vector.tensor_tensor(rec_i[:, :, 0], rec_i[:, :, 0], dst_i[:, :], ALU.add))
            dve.wait_ge(totals, 2)
            link(nc.vector.tensor_copy(tot[:, :], ps[1][:, 0:ND]))
            link(nc.vector.tensor_tensor_scan(incl[:, :], allone[:, :], tot[:, :], 0.0, ALU.mult, ALU.add))
            link(nc.vector.tensor_tensor(incl[:, :], incl[:, :], tot[:, :], ALU.subtract))
            link(nc.vector.scalar_tensor_tensor(offs[:, :], incl[:, :], -1.0, ps[0][:, 0:ND], ALU.add, ALU.add))
            dve.wait_ge(totals, 3)
            link(nc.vector.tensor_copy(nb[0:NB, :], ps[2][0:NB, 0:1]))
            link(nc.vector.tensor_scalar(nt[0:NB, :], nb[0:NB, :], float(P - 1), None, ALU.add))
            link(nc.vector.tensor_copy(nt_i[0:NB, :], nt[0:NB, :]))
            link(nc.vector.tensor_single_scalar(nt_i[0:NB, :], nt_i[0:NB, :], 7, ALU.arith_shift_right))
            link(nc.vector.tensor_copy(nt[0:NB, :], nt_i[0:NB, :]))
            nc.vector.scalar_tensor_tensor(over[0:NB, :], nt[0:NB, :], float(-P), nb[0:NB, :],
                                           ALU.mult, ALU.add).then_inc(tiled, 1)
            dve.wait_ge(prefixed, 1)
            link(nc.vector.tensor_copy(nb[0:NB, :], ps[2][0:NB, 8:9]))
            nc.vector.tensor_scalar(past[0:NB, :], tile_no[0:NB, :], nb[0:NB, 0:1], None,
                                    ALU.is_ge).then_inc(listed, 1)
            dve.wait_ge(summed, 2 * len(halves))
            for k, (a, z) in enumerate(halves):
                nc.vector.tensor_scalar(base_f[:, a:z], ps[3 + k][:, 0:z - a], float(P), None, ALU.mult)
                nc.vector.tensor_scalar(place_i[:, a:z], ps[3 + k][0:1, 0:z - a], float(AW), None, ALU.mult)
                if by_dst:
                    nc.vector.tensor_scalar(c.node_i[:, a:z], ps[3 + k][0:1, 0:z - a], float(2 * HEADS), None, ALU.mult)
                link(nc.vector.scalar_tensor_tensor(off_f[:, a:z], tile_no[:, a:z], float(P), ps[5 + k][:, 0:z - a],
                                                    ALU.mult, ALU.add))
            link(nc.vector.tensor_scalar(off_i[:, :], off_f[0:1, :], float(sh.EP - P), None, ALU.min))
            if by_dst:
                dve.wait_ge(fallen, 1)
                link(nc.vector.tensor_copy(c.unsorted[:, :], ps[7][0:1, 0:1]))

        @block.tensor
        def _(pe):
            pe.wait_ge(tri, 2)
            pe.wait_ge(counted, ND)
            nc.tensor.matmul(ps[0][:, 0:ND], before[:, :], counts[:, :], start=True, stop=True).then_inc(totals, 1)
            nc.tensor.matmul(ps[1][:, 0:ND], c.ones[:, :], counts[:, :], start=True, stop=True).then_inc(totals, 1)
            nc.tensor.matmul(ps[2][0:ND, 0:1], counts[:, :], c.ones[:, 0:1], start=True, stop=True).then_inc(totals, 1)
            if by_dst:
                pe.wait_ge(compared, 2)
                nc.tensor.matmul(ps[7][:, 0:1], c.ones[:, :], falls[:, :], start=True, stop=True).then_inc(fallen, 1)
            pe.wait_ge(tiled, 1)
            nc.tensor.matmul(ps[2][0:NB, 8:9], upto[0:NB, 0:NB], nt[0:NB, 0:1], start=True, stop=True).then_inc(prefixed, 1)
            pe.wait_ge(listed, 1)
            for k, (a, z) in enumerate(halves):
                nc.tensor.matmul(ps[3 + k][:, 0:z - a], c.ones[0:NB, :], past[0:NB, a:z], start=True, stop=True).then_inc(summed, 1)
                nc.tensor.matmul(ps[5 + k][:, 0:z - a], over[0:NB, 0:1].to_broadcast([NB, P]), past[0:NB, a:z],
                                 start=True, stop=True).then_inc(summed, 1)


def place_stage(nc, c, edges):
    sh = c.sh
    ND, COLS = sh.ND, sh.COLS
    kind = edges.kind
    ring = Ring(ND, 4)
    with ExitStack() as st:
        sb = lambda name, shape, dt=F32: st.enter_context(nc.sbuf_tensor(f"{name}_{kind}", shape, dt))
        sem = lambda name: nc.alloc_semaphore(f"{name}_{kind}")
        pos, allone = sb("pos", [P, COLS]), sb("alls", [P, COLS])
        minus = sb("minus", [P, ND])
        gap, mask, run = sb("gap", [P, 4, COLS]), sb("masks", [P, 4, COLS]), sb("run", [P, 4, COLS])
        ready, gaps, masks, runs, found, added = [sem(x) for x in ("ready", "gaps", "masks", "runs", "found", "added")]
        block = st.enter_context(nc.Block())

        @block.gpsimd
        def _(pool):
            nc.gpsimd.iota(pos[:, :], pattern=[[1, COLS]], base=0, channel_multiplier=COLS,
                           allow_small_or_imprecise_dtypes=True).then_inc(added, 1)
            pool.wait_ge(added, 1)
            nc.gpsimd.affine_select(out=pos[:, :], in_=pos[:, :], compare_op=ALU.is_ge, fill=0.0,
                                    base=-sh.E, pattern=[[1, COLS]], channel_multiplier=COLS).then_inc(added, 1)

            def step(i, u):
                t = ring.at(i, u)
                pool.wait_ge(found, ring.count(t))
                pool.wait_ge(added, ring.count(t) + 1)
                nc.gpsimd.tensor_tensor(pos[:, :], pos[:, :], run[:, u, :], ALU.add).then_inc(added, 1)
            ring.run(pool, step)

        @block.scalar
        def _(act):
            act.wait_ge(ready, 1)

            def step(i, u):
                t = ring.at(i, u)
                wait_count(act, masks, ring.count(t, 4))
                nc.scalar.activation(gap[:, u, :], edges.key[:, :], ACT.Abs, bias=minus[:, bass.ds(ring.count(t) - 1, 1)]).then_inc(gaps, 1)
                act.wait_ge(gaps, ring.count(t))
                wait_count(act, found, ring.count(t, 4))
                nc.scalar.activation(mask[:, u, :], gap[:, u, :], ACT.Relu, bias=c.ones[:, 0:1], scale=-1.0).then_inc(masks, 1)
            ring.run(act, step)

        @block.vector
        def _(dve):
            nc.vector.memset(allone[:, :], 1.0)
            nc.vector.tensor_scalar(minus[:, :], edges.digits[:, :], -1.0, None, ALU.mult).then_inc(ready, 1)
            dve.wait_ge(ready, 1)

            def step(i, u):
                if (t := ring.at(i, u)) is not None:
                    dve.wait_ge(masks, ring.count(t))
                    back = ring.count(t, 4)
                    if back is not None:
                        dve.wait_ge(added, back + 2)
                    nc.vector.tensor_tensor_scan(run[:, u, :], allone[:, :], mask[:, u, :], 0.0, ALU.mult, ALU.add).then_inc(runs, 1)
                if (t := ring.at(i, u, 1)) is not None:
                    dve.wait_ge(runs, ring.count(t))
                    here = run[:, t[1], :]
                    nc.vector.scalar_tensor_tensor(here, here, edges.offs[:, bass.ds(ring.count(t) - 1, 1)],
                                                   mask[:, t[1], :], ALU.add, ALU.mult).then_inc(found, 1)
            ring.run(dve, step, lag=1)
            dve.wait_ge(added, ND + 2)
            nc.vector.tensor_copy(edges.rec[:, :, PLACE:PLACE + 1].bitcast(I32).rearrange("p n a -> p (n a)"), pos[:, :])

        @block.tensor
        def _(pe):
            pe.wait_ge(added, ND + 2)

        @block.sync
        def _(sp):
            sp.wait_ge(added, ND + 2)


class Scatter:

    def __init__(self, nc, c, edges, first, end):
        self.nc, self.edges, self.first, self.end = nc, edges, first, end
        self.gate = Gate(nc.gpsimd, c.passed["pool"])
        if end > first:
            self.staged = nc.alloc_semaphore(f"staged_{edges.kind}_{first}")
            self.left = [nc.alloc_semaphore(f"left{h}_{edges.kind}_{first}") for h in range(2)]

    def run(self, pool):
        if self.end <= self.first:
            return
        nc, edges, half = self.nc, self.edges, U // 2

        def a_round(i):
            for h in range(2):
                column = U * (self.first + i) + half * h
                if not (isinstance(i, int) and i == 0):
                    pool.wait_ge(self.left[h], 16 * half * i)
                    self.gate.step()
                nc.gpsimd.tensor_copy(edges.stage_rec[:, h, :, :], edges.rec[:, bass.ds(column, half), :]).then_inc(self.staged, 1)
                pool.wait_ge(self.staged, 2 * i + h + 1)
                self.gate.step()
                for k in range(half):
                    nc.gpsimd.indirect_dma_start(
                        edges.to, bass.IndirectOffsetOnAxis(edges.stage_rec[:, h, k, PLACE:PLACE + 1].bitcast(I32), 0),
                        edges.stage_rec[:, h, k, :], None).then_inc(self.left[h], 16)

        rounds = self.end - self.first
        a_round(0)
        if rounds > 1:
            with pool.Fori(1, rounds) as i:
                a_round(i)
        for h in range(2):
            pool.wait_ge(self.left[h], 16 * half * rounds)


def scatter_stage(nc, c, edges, first, end):
    with nc.Block() as block:
        scatter = Scatter(nc, c, edges, first, end)

        @block.gpsimd
        def _(pool):
            scatter.run(pool)


def edge_pass(nc, c, kind, table, width, index_word, mode):
    sh = c.sh
    NT = sh.NT
    base_f, place_i, off_i = c.tiles[kind]
    rec_d = c.rec_dst if kind == "dst" else c.rec_src
    ring = Ring(NT, U)
    lag = 8
    nm = f"{mode}_{index_word}_{kind}"
    cols = {"plain": D + 1, "edge_mlp": D, "attend": AW, "max": 0}[mode]
    with ExitStack() as st:
        sb = lambda name, shape, dt: st.enter_context(nc.sbuf_tensor(f"{name}_{nm}", shape, dt))
        pt = lambda name, shape=(P, 512): st.enter_context(nc.psum_tensor(f"{name}_{nm}", list(shape), F32))
        sem = lambda name: nc.alloc_semaphore(f"{name}_{nm}")
        rec = sb("recs", [P, U, REC], F32)
        rec_i = rec[:, :, :].bitcast(I32)
        got = sb("got", [P, U, HEADS if mode == "max" else AW], F32)
        hot = sb("hot", [P, U, P], BF16 if mode == "max" else F32)
        rel = sb("rel", [P, 2, 4], F32)
        rels = sem("rels")
        rec_in = [sem(f"rec_in{s}") for s in range(U)]
        row_in = [sem(f"row_in{s}") for s in range(U)]
        hots, sums, added, start = sem("hots"), sem("sums"), sem("added"), sem("start")
        cleared = sem("cleared")
        if mode == "edge_mlp":
            spread = sb("spread", [P, 4, 27], BF16)
            feat = sb("feat", [27, 4, P], BF16)
            w27 = sb("w27", [27, D], BF16)
            w_part = sb("w_part", [3, 3, D], BF16)
            w_rest = sb("w_rest", [3, D], F32)
            msg = sb("msg", [P, 8, D], F32)
            pre = sb("pre", [P, 4, D], F32)
            w1b = sb("w1b", [3, D], F32)
            turned, feats, edged, pres, msgs, w_in = [sem(x) for x in ("turned", "feats", "edged", "pres", "msgs", "w_in")]
            spreads, w_split, w_laid = sem("spreads"), sem("w_split"), sem("w_laid")
            psF = [st.enter_context(nc.psum_tensor(f"psF{k}_{nm}", [P, 1024], BF16)) for k in range(2)]
            psE = [pt("psE0"), pt("psE1")]
        if mode == "attend":
            hotT = sb("hotT", [P, 4, P], F32)
            z = sb("z", [P, 2, 2, HEADS], F32)
            msg = sb("msg", [P, 8, AW], F32)
            turned, hotTs, nodes, ws, msgs, zchain = [sem(x) for x in ("turned", "hotTs", "nodes", "ws", "msgs", "zchain")]
            psF = [pt("psF0"), pt("psF1")]
            psN = [pt("psN0"), pt("psN1")]
        if mode == "max":
            out_of = sb("out_of", [P, 4, P], BF16)
            diag = sb("diag", [P, 4, HEADS, P], BF16)
            ident4 = sb("ident4", [P, 4, P], BF16)
            top = sb("top", [P, 4, HEADS], F32)
            diag_a, diag_v, outs_, tops = [sem(x) for x in ("diag_a", "diag_v", "outs", "tops")]
            psM = [pt(f"psM{k}", (P, 1024)) for k in range(4)]
        else:
            psS = [pt(f"psS{k}") for k in range(4)]

        def fours(t):
            return U // 4 * t[0] + t[1] // 4 + 1

        def pair(t):
            return U // 2 * t[0] + t[1] // 2

        def pairs_done(t, back):
            n = pair(t) + 1 - back
            return None if isinstance(n, int) and n <= 0 else n

        block = st.enter_context(nc.Block())

        @block.sync
        def _(sp):
            if mode == "edge_mlp":
                sp.dma_start(w1b[:, :], c.w1t_in[D:D + 3, :]).then_inc(w_in, 16)
                sp.wait_ge(w_split, 5)
                for i in range(3):
                    for j in range(3):
                        r = 9 * i + 3 * j
                        sp.dma_start(w27[r:r + 3, :], w_part[:, j, :]).then_inc(w_laid, 16)
            gate = Gate(sp, c.passed["sp"])
            offs = Places(nc.sync, off_i, ring, 0, sh.EP - P)

            def step(i, u):
                if u == 0:
                    offs.load(i)
                off = offs.of(u)
                if (old := ring.at(i, u, U)) is not None:
                    sp.wait_ge(row_in[u], 16 * (old[0] + 1))
                    gate.step()
                    sp.wait_ge(hots, fours(old))
                    gate.step()
                    if mode == "edge_mlp":
                        wait_count(sp, spreads, ring.count(old))
                        gate.step()
                sp.dma_start(rec[:, u, :], rec_d[bass.ds(off, P), :]).then_inc(rec_in[u], 16)

            ring.run(sp, step)
            if mode == "edge_mlp":
                sp.wait_ge(w_laid, 9 * 16)

        @block.gpsimd
        def _(pool):
            nc.gpsimd.memset(got[:, :, :], 1.0).then_inc(start, 1)
            pool.wait_ge(start, 1)
            gate = Gate(pool, c.passed["pool"])

            def step(i, u):
                t = ring.at(i, u)
                free = msgs if mode in ("edge_mlp", "attend") else sums
                if (old := ring.at(i, u, U)) is not None:
                    wait_count(pool, free, ring.count(old))
                pool.wait_ge(rec_in[u], 16 * (t[0] + 1))
                gate.step()
                w = HEADS if mode == "max" else width
                nc.gpsimd.indirect_dma_start(got[:, u, 0:w], None, table,
                                             bass.IndirectOffsetOnAxis(rec_i[:, u, index_word:index_word + 1], 0)
                                             ).then_inc(row_in[u], 16)

            ring.run(pool, step)

        @block.vector
        def _(dve):
            if mode == "edge_mlp":
                dve.wait_ge(w_in, 16)
                for n, instruction in enumerate((
                        lambda: nc.vector.tensor_copy(w_part[:, 0, :], w1b[:, :]),
                        lambda: nc.vector.tensor_tensor(w_rest[:, :], w1b[:, :], w_part[:, 0, :], ALU.subtract),
                        lambda: nc.vector.tensor_copy(w_part[:, 1, :], w_rest[:, :]),
                        lambda: nc.vector.tensor_tensor(w_rest[:, :], w_rest[:, :], w_part[:, 1, :], ALU.subtract),
                        lambda: nc.vector.tensor_copy(w_part[:, 2, :], w_rest[:, :]))):
                    instruction().then_inc(w_split, 1)
                    dve.wait_ge(w_split, n + 1)
            if mode == "max":
                for k in range(4):
                    nc.vector.tensor_copy(ident4[:, k, :], c.ident_bf[:, :])
                nc.vector.memset(c.top[:, :, :], -BIG).then_inc(cleared, 1)
            elif mode != "attend":
                nc.vector.memset(c.acc[:, :, :], 0.0).then_inc(cleared, 1)

            places = Places(nc.vector, c.node_i if mode == "max" else place_i, ring,
                            {"max": 5, "attend": lag + 5}.get(mode, lag), sh.NB * (2 * HEADS if mode == "max" else AW))

            def add(i, u, back):
                if u == 0:
                    places.load(i)
                t = ring.at(i, u, back)
                if t is None:
                    return
                place = places.of(u)
                if isinstance(t[0], int) and t == (0, 0):
                    dve.wait_ge(cleared, 1)
                dve.wait_ge(sums, ring.count(t))
                wait_count(dve, added, ring.count(t, 1))
                if mode == "max":
                    k = t[1] % 4
                    nc.vector.tensor_reduce(top[:, k, :], psM[k][:, :].rearrange("p (h e) -> p h e", e=P),
                                            AX.X, ALU.max).then_inc(tops, 1)
                    dve.wait_ge(tops, ring.count(t))
                    here = c.top[:, :, :].rearrange("p b h -> p (b h)")[:, bass.ds(place, HEADS)]
                    nc.vector.tensor_tensor(here, here, top[:, k, :], ALU.max).then_inc(added, 1)
                else:
                    here = c.acc[:, :, :].rearrange("p b w -> p (b w)")[:, bass.ds(place, cols)]
                    nc.vector.tensor_tensor(here, here, psS[t[1] % 4][:, 0:cols], ALU.add).then_inc(added, 1)

            def begin(i, u):
                t = ring.at(i, u)
                if t is None or u % 4:
                    return
                for s_ in range(u, u + 4):
                    dve.wait_ge(rec_in[s_], 16 * (t[0] + 1))
                nc.vector.tensor_tensor(rel[:, u // 4 % 2, :], rec[:, u:u + 4, 1],
                                        base_f[:, bass.ds(ring.count(t) - 1, 4)], ALU.subtract).then_inc(rels, 1)

            def one_hot(i, u):
                t = ring.at(i, u)
                if t is None or u % 4:
                    return
                dve.wait_ge(rels, fours(t))
                iota = c.iota_bf if mode == "max" else c.iota
                nc.vector.tensor_tensor(hot[:, u:u + 4, :], iota[:, :].unsqueeze(1).to_broadcast([P, 4, P]),
                                        rel[:, u // 4 % 2, :].unsqueeze(2).to_broadcast([P, 4, P]), ALU.is_equal).then_inc(hots, 1)

            if mode == "plain":
                def step(i, u):
                    begin(i, u)
                    add(i, u, lag)
                    one_hot(i, u)
            elif mode == "edge_mlp":
                def step(i, u):
                    begin(i, u)
                    if (t := ring.at(i, u, 4)) is not None:
                        dve.wait_ge(row_in[t[1]], 16 * (t[0] + 1))
                        dve.wait_ge(edged, ring.count(t))
                        wait_count(dve, msgs, ring.count(t, 4))
                        nc.vector.tensor_tensor(pre[:, t[1] % 4, :], got[:, t[1], 0:D],
                                                psE[t[1] % 2][:, 0:D], ALU.add).then_inc(pres, 1)
                    add(i, u, lag)
                    one_hot(i, u)
            elif mode == "attend":
                def step(i, u):
                    begin(i, u)
                    scores = ring.at(i, u, 6)
                    if scores is not None and not scores[1] % 2:
                        scores = None
                    if scores is not None:
                        k, q = scores[1] // 2 % 2, 3 * pair(scores)
                        n = psN[k][:, 0:4 * HEADS].rearrange("p (t w) -> p t w", t=2)
                        for s_ in (scores[1] - 1, scores[1]):
                            dve.wait_ge(row_in[s_], 16 * (scores[0] + 1))
                        dve.wait_ge(nodes, ring.count(scores))
                        wait_count(dve, ws, pairs_done(scores, 2))
                        nc.vector.tensor_tensor(z[:, k, :, :], n[:, :, 0:HEADS], got[:, scores[1] - 1:scores[1] + 1, D:AW],
                                                ALU.add).then_inc(zchain, 1)
                    if (t := ring.at(i, u, 10)) is not None:
                        dve.wait_ge(ws, pair(t) + 1)
                        nc.vector.tensor_tensor(
                            msg[:, t[1] % 8, 0:D].rearrange("p (h d) -> p h d", d=DH),
                            got[:, t[1], 0:D].rearrange("p (h d) -> p h d", d=DH),
                            msg[:, t[1] % 8, D:AW].unsqueeze(2).to_broadcast([P, HEADS, DH]), ALU.mult).then_inc(msgs, 1)
                    if scores is not None:
                        dve.wait_ge(zchain, q + 1)
                        nc.vector.scalar_tensor_tensor(z[:, k, :, :], z[:, k, :, :], SLOPE, z[:, k, :, :],
                                                       ALU.mult, ALU.max).then_inc(zchain, 1)
                    add(i, u, lag + 5)
                    if scores is not None:
                        dve.wait_ge(zchain, q + 2)
                        nc.vector.scalar_tensor_tensor(z[:, k, :, :], z[:, k, :, :], c.peak[:, 0:1], n[:, :, HEADS:2 * HEADS],
                                                       ALU.subtract, ALU.subtract).then_inc(zchain, 1)
                    one_hot(i, u)
            else:
                def step(i, u):
                    begin(i, u)
                    one_hot(i, u)
                    if (t := ring.at(i, u)) is not None:
                        k = u % 4
                        dve.wait_ge(hots, fours(t))
                        wait_count(dve, sums, ring.count(t, 4))
                        nc.vector.tensor_scalar(out_of[:, k, :], hot[:, u, :], -1.0, BIG, ALU.add, ALU.mult).then_inc(outs_, 1)
                    if (t := ring.at(i, u, 3)) is not None:
                        k = t[1] % 4
                        dve.wait_ge(row_in[t[1]], 16 * (t[0] + 1))
                        wait_count(dve, sums, ring.count(t, 4))
                        for h in range(HEADS // 2):
                            last = nc.vector.tensor_scalar(diag[:, k, h, :], c.ident_bf[:, :], got[:, t[1], h:h + 1], None, ALU.mult)
                        last.then_inc(diag_v, 1)
                    add(i, u, 5)
            ring.run(dve, step, lag={"max": 5, "attend": lag + 5}.get(mode, lag))

        @block.scalar
        def _(act):
            if mode == "edge_mlp":
                def step(i, u):
                    if (t := ring.at(i, u)) is not None:
                        act.wait_ge(rec_in[u], 16 * (t[0] + 1))
                        wait_count(act, turned, ring.count(t, 4))
                        parts = rec[:, u, :].bitcast(BF16)[:, 4:13].rearrange("p (i k) -> p i k", k=3)
                        nc.scalar.copy(spread[:, u % 4, :].rearrange("p (i j k) -> p i j k", j=3, k=3),
                                       parts.unsqueeze(2).to_broadcast([P, 3, 3, 3])).then_inc(spreads, 1)
                    if (t := ring.at(i, u, 1)) is not None:
                        act.wait_ge(turned, ring.count(t))
                        wait_count(act, edged, ring.count(t, 4))
                        nc.scalar.copy(feat[:, t[1] % 4, :], psF[t[1] % 2][0:27, 0:P]).then_inc(feats, 1)
                    if (t := ring.at(i, u, 4)) is not None:
                        act.wait_ge(pres, ring.count(t))
                        wait_count(act, sums, ring.count(t, 8))
                        nc.scalar.activation(msg[:, t[1] % 8, :], pre[:, t[1] % 4, :], ACT.Relu).then_inc(msgs, 1)
                ring.run(act, step, lag=4)
            elif mode == "attend":
                nc.scalar.activation(c.acc[:, :, :], c.ones[:, 0:1].unsqueeze(2).to_broadcast([P, sh.NB + 1, AW]),
                                     ACT.Copy, scale=0.0).then_inc(cleared, 1)

                def step(i, u):
                    if (t := ring.at(i, u, 7)) is not None and t[1] % 2:
                        act.wait_ge(zchain, 3 * pair(t) + 3)
                        wait_count(act, sums, ring.count(t, 8))
                        m = t[1] % 8
                        nc.scalar.activation(msg[:, m - 1:m + 1, D:AW], z[:, t[1] // 2 % 2, :, :], ACT.Exp).then_inc(ws, 1)
                    if (t := ring.at(i, u)) is not None:
                        act.wait_ge(turned, ring.count(t))
                        wait_count(act, nodes, ring.count(t, 4))
                        nc.scalar.copy(hotT[:, u % 4, :], psF[u % 2][:, 0:P]).then_inc(hotTs, 1)
                ring.run(act, step, lag=7)
            elif mode == "max":
                def step(i, u):
                    if (t := ring.at(i, u, 3)) is not None:
                        k = t[1] % 4
                        act.wait_ge(row_in[t[1]], 16 * (t[0] + 1))
                        wait_count(act, sums, ring.count(t, 4))
                        for h in range(HEADS // 2, HEADS):
                            last = nc.scalar.activation(diag[:, k, h, :], c.ident_bf[:, :], ACT.Copy, scale=got[:, t[1], h:h + 1])
                        last.then_inc(diag_a, 1)
                ring.run(act, step, lag=3)

        @block.tensor
        def _(pe):
            if mode == "edge_mlp":
                pe.wait_ge(w_laid, 9 * 16)

            def gather_sum(i, u, back, rows, ready):
                t = ring.at(i, u, back)
                if t is None:
                    return
                for s_, n_ in ready(t):
                    pe.wait_ge(s_, n_)
                wait_count(pe, added, ring.count(t, 4))
                nc.tensor.matmul(psS[t[1] % 4][:, 0:cols], hot[:, t[1], :], rows(t), start=True, stop=True).then_inc(sums, 1)

            if mode == "plain":
                def step(i, u):
                    gather_sum(i, u, 0, lambda t: got[:, t[1], 0:cols],
                               lambda t: [(row_in[t[1]], 16 * (t[0] + 1)), (hots, fours(t))])
                ring.run(pe, step)
            elif mode == "edge_mlp":
                def step(i, u):
                    if (t := ring.at(i, u)) is not None:
                        pe.wait_ge(spreads, ring.count(t))
                        wait_count(pe, feats, ring.count(t, 2))
                        nc.tensor.transpose(psF[u % 2][0:27, 0:P], spread[:, u % 4, :],
                                            c.ident_bf[:, :]).then_inc(turned, 1)
                    if (t := ring.at(i, u, 2)) is not None:
                        pe.wait_ge(feats, ring.count(t))
                        wait_count(pe, pres, ring.count(t, 2))
                        nc.tensor.matmul(psE[t[1] % 2][:, 0:D], feat[:, t[1] % 4, :], w27[:, :], start=True, stop=True).then_inc(edged, 1)
                    gather_sum(i, u, 6, lambda t: msg[:, t[1] % 8, :],
                               lambda t: [(msgs, ring.count(t)), (hots, fours(t))])
                ring.run(pe, step, lag=6)
            elif mode == "attend":
                places = Places(nc.tensor, c.node_i, ring, 4, sh.NB * 2 * HEADS)

                def step(i, u):
                    if u == 0:
                        places.load(i)
                    gather_sum(i, u, 11, lambda t: msg[:, t[1] % 8, :],
                               lambda t: [(msgs, ring.count(t))])
                    if (t := ring.at(i, u, 4)) is not None:
                        place = places.of(u)
                        pe.wait_ge(hotTs, ring.count(t))
                        done = pairs_done(t, 2)
                        wait_count(pe, zchain, None if done is None else 3 * done)
                        nc.tensor.matmul(psN[t[1] // 2 % 2][:, 2 * HEADS * (t[1] % 2):2 * HEADS * (t[1] % 2 + 1)],
                                         hotT[:, t[1] % 4, :],
                                         c.node[:, :, :].rearrange("p b w -> p (b w)")[:, bass.ds(place, 2 * HEADS)],
                                         start=True, stop=True).then_inc(nodes, 1)
                    if (t := ring.at(i, u)) is not None:
                        pe.wait_ge(hots, fours(t))
                        wait_count(pe, hotTs, ring.count(t, 2))
                        nc.tensor.transpose(psF[u % 2][:, 0:P], hot[:, u, :], c.ident[:, :]).then_inc(turned, 1)
                ring.run(pe, step, lag=11)
            else:
                def step(i, u):
                    if (t := ring.at(i, u, 4)) is not None:
                        k = t[1] % 4
                        ps = psM[k]
                        pe.wait_ge(outs_, ring.count(t))
                        wait_count(pe, tops, ring.count(t, 4))
                        pe.wait_ge(diag_v, ring.count(t))
                        pe.wait_ge(diag_a, ring.count(t))
                        for half in range(2):
                            o = ps[:, 512 * half:512 * half + 512]
                            nc.tensor.matmul(o, out_of[:, k, :], ident4[:, :, :], start=True, stop=False)
                            last = nc.tensor.matmul(o, hot[:, t[1], :], diag[:, k, 4 * half:4 * half + 4, :], start=False, stop=True)
                        last.then_inc(sums, 1)
                ring.run(pe, step, lag=4)


def norm_steps(nc, c, dve, gate, ring, i, buf, stated):
    stats, moments = buf
    G = ring.size
    for u in range(G):
        last = nc.vector.bn_stats(stats[:, u, :], c.x[:, bass.ds(G * i + u, 1), :].rearrange("p a d -> p (a d)"))
    last.then_inc(stated, 1)
    dve.wait_ge(stated, 3 * i + 1)
    gate.step()
    for u in range(G):
        last = nc.vector.bn_aggr(moments[:, u, :], stats[:, u, :])
    last.then_inc(stated, 1)
    dve.wait_ge(stated, 3 * i + 2)
    nc.vector.tensor_copy(c.stat[:, bass.ds(G * i, G), :], moments[:, :, :]).then_inc(stated, 1)
    dve.wait_ge(stated, 3 * i + 3)
    gate.step()


def norm_ends(nc, c, dve, roots):
    begun, rooted, ended = roots
    nc.vector.tensor_scalar(c.rstd[:, :], c.stat[:, :, 1], EPS, None, ALU.add).then_inc(begun, 1)
    dve.wait_ge(rooted, 1)
    nc.vector.reciprocal(c.rstd[:, :], c.rstd[:, :]).then_inc(ended, 1)
    dve.wait_ge(ended, 1)
    nc.vector.scalar_tensor_tensor(c.nbias[:, :], c.stat[:, :, 0], -1.0, c.rstd[:, :], ALU.mult, ALU.mult)


def norm_roots(nc, c, act, roots):
    begun, rooted, ended = roots
    act.wait_ge(begun, 1)
    nc.scalar.sqrt(c.rstd[:, :], c.rstd[:, :]).then_inc(rooted, 1)


def row(ap, n):
    return ap.rearrange("(a n) -> a n", a=1).to_broadcast([P, n])


def stats_stage(nc, c, edges, first, end):
    sh = c.sh
    ring = Ring(sh.NB, 7)
    nm = "stats"
    with ExitStack() as st:
        sb = lambda name, shape, dt=F32: st.enter_context(nc.sbuf_tensor(f"{name}_{nm}", shape, dt))
        stats, moments = sb("stats", [P, 7, 6]), sb("moments", [P, 7, 2])
        stated = nc.alloc_semaphore(f"stated_{nm}")
        roots = [nc.alloc_semaphore(f"{x}_{nm}") for x in ("begun", "rooted", "ended")]
        scatter = Scatter(nc, c, edges, first, end)
        block = st.enter_context(nc.Block())

        @block.gpsimd
        def _(pool):
            scatter.run(pool)

        @block.vector
        def _(dve):
            gate = Gate(dve, c.passed["dve"])

            def a_round(i):
                norm_steps(nc, c, dve, gate, ring, i, (stats, moments), stated)
            peeled(dve, ring.rounds, a_round)
            norm_ends(nc, c, dve, roots)

        @block.scalar
        def _(act):
            norm_roots(nc, c, act, roots)


def table_stage(nc, c, layer, edges, first, end):
    sh = c.sh
    G = 7
    ring = Ring(sh.NB, G)
    nm = f"tab{layer}"
    width = {0: D, 1: NREL * D}[layer]
    blocks = [(a, min(a + 512, width)) for a in range(0, width, 512)]
    NBK = len(blocks)
    with ExitStack() as st:
        sb = lambda name, shape, dt=F32: st.enter_context(nc.sbuf_tensor(f"{name}_{nm}", shape, dt))
        pt = lambda name: st.enter_context(nc.psum_tensor(f"{name}_{nm}", [P, 512], F32))
        sem = lambda name: nc.alloc_semaphore(f"{name}_{nm}")
        w = sb("w", [P, 2, width])
        h = sb("h", [P, G, D])
        hT = sb("hT", [P, G, D])
        SL = G if width < 512 else 3
        out = sb("out", [P, SL, width])
        bias = sb("bias", [P, D])
        psT = [pt("psT0"), pt("psT1")]
        psO = [pt(f"psO{k}") for k in range(4)]
        w_in, hs, turned, hTs, made, outs = [sem(x) for x in ("w_in", "hs", "turned", "hTs", "made", "outs")]
        left = [sem(f"left{s}") for s in range(SL)]
        scatter = Scatter(nc, c, edges, first, end)
        block = st.enter_context(nc.Block())

        @block.gpsimd
        def _(pool):
            scatter.run(pool)

        def slot(t):
            return t[1] % SL

        @block.sync
        def _(sp):
            if layer == 0:
                sp.dma_start(w[:, :, :], c.w1t_in[0:D, :].rearrange("(k p) n -> p k n", p=P)).then_inc(w_in, 16)
                sp.dma_start(bias[:, :], row(c.b1_in, D)).then_inc(w_in, 16)
            else:
                for r in range(NREL):
                    sp.dma_start(w[:, :, r * D:(r + 1) * D],
                                 c.wrel_in[r, :, :].rearrange("(k p) n -> p k n", p=P)).then_inc(w_in, 16)

            def step(i, u):
                t = ring.at(i, u)
                T = ring.count(t) - 1
                rows = sh.LAST if isinstance(T, int) and T == sh.NB - 1 else P
                s = slot(t)
                sp.wait_ge(outs, NBK * ring.count(t))
                if layer == 1:
                    to = c.xtab.rearrange("(r n) d -> n r d", r=NREL)[bass.ds(P * T, rows), :, :]
                    sp.dma_start(to, out[0:rows, s, :].rearrange("p (r d) -> p r d", d=D)).then_inc(left[s], 16)
                else:
                    sp.dma_start(c.ptab[bass.ds(P * T, rows), :], out[0:rows, s, :]).then_inc(left[s], 16)

            ring.run(sp, step)
            for s in range(SL):
                per = len([u for u in range(G) if u % SL == s]) * ring.rounds
                sp.wait_ge(left[s], 16 * per)

        def wait_left(eng, t):
            s = slot(t)
            per = len([u for u in range(G) if u % SL == s])
            n = per * t[0] + t[1] // SL
            if isinstance(n, int) and n <= 0:
                return
            eng.wait_ge(left[s], 16 * n)

        @block.scalar
        def _(act):
            def step(i, u):
                if (t := ring.at(i, u)) is not None:
                    T = ring.count(t) - 1
                    wait_count(act, turned, ring.count(t, G))
                    nc.scalar.activation(h[:, u, :], c.x[:, bass.ds(T, 1), :].rearrange("p a d -> p (a d)"), ACT.Relu,
                                         bias=c.nbias[:, bass.ds(T, 1)], scale=c.rstd[:, bass.ds(T, 1)]).then_inc(hs, 1)
                if (t := ring.at(i, u, 2)) is not None:
                    act.wait_ge(turned, ring.count(t))
                    wait_count(act, made, ring.count(t, G - 2))
                    nc.scalar.copy(hT[:, t[1], :], psT[t[1] % 2][:, 0:D]).then_inc(hTs, 1)
            ring.run(act, step, lag=2)

        @block.vector
        def _(dve):
            def step(i, u):
                t = ring.at(i, u)
                wait_left(dve, t)
                if layer == 0:
                    dve.wait_ge(w_in, 32)
                for b, (a, z) in enumerate(blocks):
                    dve.wait_ge(made, NBK * (ring.count(t) - 1) + b + 1)
                    ps = psO[(NBK * u + b) % 4][:, 0:z - a]
                    o = out[:, slot(t), a:z]
                    if layer == 0:
                        last = nc.vector.tensor_tensor(o, ps, bias[:, :], ALU.add)
                    else:
                        last = nc.vector.tensor_copy(o, ps)
                    last.then_inc(outs, 1)
            ring.run(dve, step)

        @block.tensor
        def _(pe):
            pe.wait_ge(w_in, 16 * {0: 2, 1: NREL}[layer])

            def step(i, u):
                if (t := ring.at(i, u)) is not None:
                    pe.wait_ge(hs, ring.count(t))
                    wait_count(pe, hTs, ring.count(t, 1 if u == 0 else 2))
                    for k in range(2):
                        last = nc.tensor.transpose(psT[u % 2][:, k * P:(k + 1) * P], h[:, u, k * P:(k + 1) * P], c.ident[:, :])
                    last.then_inc(turned, 1)
                if (t := ring.at(i, u, 1)) is not None:
                    pe.wait_ge(hTs, ring.count(t))
                    for b, (a, z) in enumerate(blocks):
                        n = NBK * (ring.count(t) - 1) + b
                        back = 4 if NBK * t[1] + b >= 4 else (4 if (NBK * G) % 4 == 0 else (NBK * t[1] + b) + 1)
                        if not (isinstance(n, int) and n - back + 1 <= 0):
                            pe.wait_ge(outs, n - back + 1)
                        for k in range(2):
                            last = nc.tensor.matmul(psO[(NBK * t[1] + b) % 4][:, 0:z - a], hT[:, t[1], k * P:(k + 1) * P],
                                                    w[:, k, a:z], start=(k == 0), stop=(k == 1))
                        last.then_inc(made, 1)
            ring.run(pe, step, lag=1)


def sage_update(nc, c, edges, first, end):
    sh = c.sh
    G = 7
    ring = Ring(sh.NB, G)
    with ExitStack() as st:
        sb = lambda name, shape, dt=F32: st.enter_context(nc.sbuf_tensor(f"{name}_sage", shape, dt))
        pt = lambda name: st.enter_context(nc.psum_tensor(f"{name}_sage", [P, 512], F32))
        sem = lambda name: nc.alloc_semaphore(f"{name}_sage")
        w = sb("w", [P, 4, D])
        hn = sb("hn", [P, G, 2 * D])
        hnT = sb("hnT", [P, G, 2 * D])
        r, sq = sb("r", [P, G, D]), sb("sq", [P, G, D])
        ss, nrm = sb("ss", [P, G]), sb("nrm", [P, G])
        stats, moments = sb("stats", [P, G, 6]), sb("moments", [P, G, 2])
        psT = [pt("psT0"), pt("psT1")]
        psO = [pt("psO0"), pt("psO1")]
        w_in, hns, turned, turned_back, made, rs, sqs, step_, stated = [sem(x) for x in (
            "w_in", "hns", "turned", "turned_back", "made", "rs", "sqs", "step_", "stated")]
        rooted = sem("rooted")
        roots = [sem(x) for x in ("begun", "rooted_all", "ended")]
        scatter = Scatter(nc, c, edges, first, end)
        block = st.enter_context(nc.Block())

        @block.gpsimd
        def _(pool):
            scatter.run(pool)

        @block.sync
        def _(sp):
            sp.dma_start(w[:, :, :], c.w2t_in.rearrange("(k p) n -> p k n", p=P)).then_inc(w_in, 16)
            sp.wait_ge(w_in, 16)

        @block.scalar
        def _(act):
            def step(i, u):
                if (t := ring.at(i, u)) is not None:
                    T = ring.count(t) - 1
                    wait_count(act, turned, ring.count(t, G))
                    nc.scalar.activation(hn[:, u, 0:D], c.x[:, bass.ds(T, 1), :].rearrange("p a d -> p (a d)"), ACT.Relu,
                                         bias=c.nbias[:, bass.ds(T, 1)], scale=c.rstd[:, bass.ds(T, 1)])
                    nc.scalar.copy(hn[:, u, D:2 * D], c.acc[:, bass.ds(T, 1), 0:D].rearrange("p a d -> p (a d)")).then_inc(hns, 1)
                if (t := ring.at(i, u, 4)) is not None:
                    act.wait_ge(made, ring.count(t))
                    if not (isinstance(t[0], int) and t[0] == 0):
                        act.wait_ge(step_, 3 * t[0])
                    nc.scalar.activation(r[:, t[1], :], psO[t[1] % 2][:, 0:D], ACT.Relu).then_inc(rs, 1)
                    act.wait_ge(rs, ring.count(t))
                    nc.scalar.activation(sq[:, t[1], :], r[:, t[1], :], ACT.Square,
                                         accum_out=ss[:, t[1]:t[1] + 1]).then_inc(sqs, 1)
                    if t[1] == G - 1:
                        act.wait_ge(sqs, ring.count(t))
                        nc.scalar.sqrt(nrm[:, :], ss[:, :]).then_inc(rooted, 1)
            ring.run(act, step, lag=4)
            norm_roots(nc, c, act, roots)

        @block.tensor
        def _(pe):
            pe.wait_ge(w_in, 16)

            def step(i, u):
                if (t := ring.at(i, u)) is not None:
                    pe.wait_ge(hns, ring.count(t))
                    wait_count(pe, turned_back, ring.count(t, 1 if u == 0 else 2))
                    for k in range(4):
                        last = nc.tensor.transpose(psT[u % 2][:, k * P:(k + 1) * P], hn[:, u, k * P:(k + 1) * P], c.ident[:, :])
                    last.then_inc(turned, 1)
                if (t := ring.at(i, u, 2)) is not None:
                    pe.wait_ge(turned_back, ring.count(t))
                    wait_count(pe, rs, ring.count(t, 1 if t[1] == 0 else 2))
                    for k in range(4):
                        last = nc.tensor.matmul(psO[t[1] % 2][:, 0:D], hnT[:, t[1], k * P:(k + 1) * P], w[:, k, :],
                                                start=(k == 0), stop=(k == 3))
                    last.then_inc(made, 1)
            ring.run(pe, step, lag=2)

        @block.vector
        def _(dve):
            def round_end(i):
                dve.wait_ge(rooted, i + 1)
                nc.vector.tensor_scalar(nrm[:, :], nrm[:, :], 1e-12, None, ALU.max).then_inc(step_, 1)
                dve.wait_ge(step_, 3 * i + 1)
                nc.vector.reciprocal(nrm[:, :], nrm[:, :]).then_inc(step_, 1)
                dve.wait_ge(step_, 3 * i + 2)
                for s in range(G):
                    here = c.x[:, bass.ds(G * i + s, 1), :].rearrange("p a d -> p (a d)")
                    last = nc.vector.scalar_tensor_tensor(here, r[:, s, :], nrm[:, s:s + 1], here, ALU.mult, ALU.add)
                last.then_inc(step_, 1)
                dve.wait_ge(step_, 3 * i + 3)
                gate.step()
                norm_steps(nc, c, dve, gate, ring, i, (stats, moments), stated)

            gate = Gate(dve, c.passed["dve"])

            def a_round(i):
                for s in range(G):
                    t = (i, s)
                    dve.wait_ge(turned, ring.count(t))
                    nc.vector.tensor_copy(hnT[:, s, :], psT[s % 2][:, :]).then_inc(turned_back, 1)
                round_end(i)
            peeled(dve, ring.rounds, a_round)
            norm_ends(nc, c, dve, roots)


def rgcn_update(nc, c):
    sh = c.sh
    G = 7
    ring = Ring(sh.NB, G)
    R = ring.rounds
    width = D + 2 * HEADS
    with ExitStack() as st:
        sb = lambda name, shape, dt=F32: st.enter_context(nc.sbuf_tensor(f"{name}_rgcn", shape, dt))
        pt = lambda name: st.enter_context(nc.psum_tensor(f"{name}_rgcn", [P, 512], F32))
        sem = lambda name: nc.alloc_semaphore(f"{name}_rgcn")
        flat = lambda ap: ap.rearrange("p a d -> p (a d)")
        bias = sb("bias", [P, D])
        w, att, prod = sb("w", [P, 2, width]), sb("att", [P, 2, D]), sb("prod", [P, 2, D])
        t1, t2 = sb("t1", [P, G, D]), sb("t2", [P, G, D])
        h, hT = sb("h", [P, G, D]), sb("hT", [P, G, D])
        out = sb("out", [P, G, width])
        deg, pos = sb("deg", [P, sh.NB]), sb("pos", [P, sh.NB])
        stats, moments = sb("stats", [P, G, 6]), sb("moments", [P, G, 2])
        scl, shift = sb("scl", [P, G]), sb("shift", [P, G])
        psT = [pt("psT0"), pt("psT1")]
        psO = [pt(f"psO{k}") for k in range(4)]
        b_in, degs, deg_root, t1s, t2s, xs, stated = [sem(x) for x in ("b_in", "degs", "deg_root", "t1s", "t2s", "xs", "stated")]
        w_in, w_made, begun, rooted, scaled, normed = [sem(x) for x in ("w_in", "w_made", "begun", "rooted", "scaled", "normed")]
        hs, turned, hTs, made, outs, noted = [sem(x) for x in ("hs", "turned", "hTs", "made", "outs", "noted")]
        left = [sem(f"left{s}") for s in range(G)]
        block = st.enter_context(nc.Block())

        @block.sync
        def _(sp):
            sp.dma_start(bias[:, :], row(c.bias1_in, D)).then_inc(b_in, 16)
            sp.dma_start(w[:, :, 0:D], c.watt_in.rearrange("(k p) n -> p k n", p=P)).then_inc(w_in, 16)
            sp.dma_start(att[:, 0, :], row(c.att_src_in.rearrange("h d -> (h d)"), D)).then_inc(w_in, 16)
            sp.dma_start(att[:, 1, :], row(c.att_dst_in.rearrange("h d -> (h d)"), D)).then_inc(w_in, 16)

            def send(i, u):
                t = ring.at(i, u)
                T = ring.count(t) - 1
                rows = sh.LAST if isinstance(T, int) and T == sh.NB - 1 else P
                sp.wait_ge(outs, ring.count(t))
                sp.dma_start(c.gtab[bass.ds(P * T, rows), :], out[0:rows, u, 0:AW]).then_inc(left[u], 16)
                sp.dma_start(c.stab[bass.ds(P * T, rows), :], out[0:rows, u, D:AW]).then_inc(left[u], 16)
            ring.run(sp, send)
            sp.wait_ge(b_in, 16)
            sp.wait_ge(w_in, 48)
            for s in range(G):
                sp.wait_ge(left[s], 32 * R)

        @block.gpsimd
        def _(pool):
            pool.wait_ge(b_in, 16)

            def a_round(i):
                for s in range(G):
                    wait_count(pool, t2s, G * i)
                    nc.gpsimd.tensor_tensor(t1[:, s, :], flat(c.acc[:, bass.ds(G * i + s, 1), 0:D]), bias[:, :],
                                            ALU.add).then_inc(t1s, 1)
            peeled(pool, R, a_round)

        @block.scalar
        def _(act):
            act.wait_ge(degs, 1)
            nc.scalar.sqrt(deg[:, :], deg[:, :]).then_inc(deg_root, 1)

            def relus(i):
                for s in range(G):
                    act.wait_ge(t1s, G * i + s + 1)
                    if s == 0:
                        wait_count(act, xs, i)
                    nc.scalar.activation(t2[:, s, :], t1[:, s, :], ACT.Relu).then_inc(t2s, 1)

            def rows(i):
                act.wait_ge(normed, i + 1)
                for s in range(G + 2):
                    if s < G:
                        T = G * i + s
                        if s == 0:
                            wait_count(act, turned, G * i)
                        nc.scalar.activation(h[:, s, :], flat(c.x[:, bass.ds(T, 1), :]), ACT.Relu,
                                             bias=c.nbias[:, bass.ds(T, 1)], scale=c.rstd[:, bass.ds(T, 1)]).then_inc(hs, 1)
                    if s >= 2:
                        act.wait_ge(turned, G * i + s - 1)
                        wait_count(act, made, G * i)
                        nc.scalar.copy(hT[:, s - 2, :], psT[s % 2][:, 0:D]).then_inc(hTs, 1)

            def roots(i):
                act.wait_ge(begun, i + 1)
                nc.scalar.sqrt(scl[:, :], scl[:, :]).then_inc(rooted, 1)

            relus(0)
            roots(0)
            with act.Fori(1, R) as i:
                relus(i)
                rows(i - 1)
                roots(i)
            rows(R - 1)

        @block.vector
        def _(dve):
            gate = Gate(dve, c.passed["dve"])
            counts = c.acc[:, 0:sh.NB, D]
            nc.vector.tensor_scalar(deg[:, :], counts, 1.0, None, ALU.max).then_inc(degs, 1)
            nc.vector.tensor_scalar(pos[:, :], counts, 0.0, None, ALU.is_gt).then_inc(degs, 1)
            dve.wait_ge(deg_root, 1)
            nc.vector.reciprocal(deg[:, :], deg[:, :]).then_inc(degs, 1)
            dve.wait_ge(degs, 3)
            nc.vector.tensor_tensor(c.dinv[:, :], deg[:, :], pos[:, :], ALU.mult)
            dve.wait_ge(w_in, 48)
            n = 0
            for a in range(2):
                for k in range(2):
                    nc.vector.tensor_tensor(prod[:, k, :], w[:, k, 0:D], att[:, a, :], ALU.mult).then_inc(w_made, 1)
                    n += 1
                    dve.wait_ge(w_made, n)
                    nc.vector.tensor_reduce(w[:, k, D + HEADS * a:D + HEADS * (a + 1)],
                                            prod[:, k, :].rearrange("p (h d) -> p h d", d=DH), AX.X, ALU.add).then_inc(w_made, 1)
                    n += 1
                    dve.wait_ge(w_made, n)

            def update(i):
                for s in range(G):
                    dve.wait_ge(t2s, G * i + s + 1)
                    here = flat(c.x[:, bass.ds(G * i + s, 1), :])
                    last = nc.vector.tensor_tensor(here, here, t2[:, s, :], ALU.add)
                last.then_inc(xs, 1)

            def send(i):
                for s in range(G):
                    dve.wait_ge(made, G * i + s + 1)
                    wait_count(dve, left[s], 32 * i)
                    nc.vector.tensor_copy(out[:, s, :], psO[s % 4][:, 0:width]).then_inc(outs, 1)
                    nc.vector.tensor_copy(flat(c.node[:, bass.ds(G * i + s, 1), 0:2 * HEADS]),
                                          psO[s % 4][:, D:width]).then_inc(noted, 1)

            def spreads(i):
                dve.wait_ge(xs, i + 1)
                gate.step()
                for s in range(G):
                    last = nc.vector.bn_stats(stats[:, s, :], flat(c.x[:, bass.ds(G * i + s, 1), :]))
                last.then_inc(stated, 1)
                dve.wait_ge(stated, 2 * i + 1)
                gate.step()
                for s in range(G):
                    last = nc.vector.bn_aggr(moments[:, s, :], stats[:, s, :])
                last.then_inc(stated, 1)
                dve.wait_ge(stated, 2 * i + 2)
                nc.vector.tensor_scalar(scl[:, :], moments[:, :, 1], EPS, None, ALU.add).then_inc(begun, 1)

            def norms(i):
                dve.wait_ge(rooted, i + 1)
                nc.vector.reciprocal(scl[:, :], scl[:, :]).then_inc(scaled, 1)
                dve.wait_ge(scaled, 2 * i + 1)
                nc.vector.scalar_tensor_tensor(shift[:, :], moments[:, :, 0], -1.0, scl[:, :], ALU.mult, ALU.mult).then_inc(scaled, 1)
                dve.wait_ge(scaled, 2 * i + 2)
                nc.vector.tensor_copy(c.rstd[:, bass.ds(G * i, G)], scl[:, :])
                nc.vector.tensor_copy(c.nbias[:, bass.ds(G * i, G)], shift[:, :]).then_inc(normed, 1)
                dve.wait_ge(normed, i + 1)

            update(0)
            spreads(0)
            norms(0)
            with dve.Fori(1, R) as i:
                update(i)
                spreads(i)
                send(i - 1)
                norms(i)
            send(R - 1)

        @block.tensor
        def _(pe):
            pe.wait_ge(w_made, 8)

            def a_round(i):
                for s in range(G + 1):
                    if s < G:
                        pe.wait_ge(hs, G * i + s + 1)
                        wait_count(pe, hTs, G * i + s - 1 if s else G * i)
                        for k in range(2):
                            last = nc.tensor.transpose(psT[s % 2][:, k * P:(k + 1) * P], h[:, s, k * P:(k + 1) * P], c.ident[:, :])
                        last.then_inc(turned, 1)
                    if s:
                        t = s - 1
                        pe.wait_ge(hTs, G * i + t + 1)
                        wait_count(pe, outs, G * i + max(t - 3, 0))
                        wait_count(pe, noted, G * i + max(t - 3, 0))
                        for k in range(2):
                            last = nc.tensor.matmul(psO[t % 4][:, 0:width], hT[:, t, k * P:(k + 1) * P], w[:, k, :],
                                                    start=(k == 0), stop=(k == 1))
                        last.then_inc(made, 1)
            peeled(pe, R, a_round)


def range_stage(nc, c):
    sh = c.sh
    with ExitStack() as st:
        sb = lambda name, shape, dt=F32: st.enter_context(nc.sbuf_tensor(f"{name}_range", shape, dt))
        sem = lambda name: nc.alloc_semaphore(f"{name}_range")
        most, every = sb("most", [P, 2 * HEADS]), sb("every", [P, 2 * HEADS])
        span = sb("span", [P, HEADS])
        widest = sb("widest", [P, 1])
        tops, alls, chain = sem("tops"), sem("alls"), sem("chain")
        block = st.enter_context(nc.Block())
        by_head = c.node[:, 0:sh.NB, 0:HEADS].rearrange("p b h -> p h b")

        @block.gpsimd
        def _(pool):
            pool.wait_ge(tops, 3)
            nc.gpsimd.partition_all_reduce(every[:, :], most[:, :], P, bass.bass_isa.ReduceOp.max).then_inc(alls, 1)

        @block.vector
        def _(dve):
            nc.vector.tensor_reduce(most[:, 0:HEADS], by_head, AX.X, ALU.max).then_inc(tops, 1)
            nc.vector.tensor_reduce(most[:, HEADS:2 * HEADS], by_head, AX.X, ALU.min).then_inc(tops, 1)
            dve.wait_ge(tops, 2)
            nc.vector.tensor_scalar(most[:, HEADS:2 * HEADS], most[:, HEADS:2 * HEADS], -1.0, None, ALU.mult).then_inc(tops, 1)
            dve.wait_ge(alls, 1)
            nc.vector.tensor_tensor(span[:, :], every[:, 0:HEADS], every[:, HEADS:2 * HEADS], ALU.add).then_inc(chain, 1)
            nc.vector.tensor_reduce(c.peak[:, :], every[:, 0:HEADS], AX.X, ALU.max)
            nc.vector.tensor_copy(c.top[:, :, 0:HEADS], every[:, 0:HEADS].unsqueeze(1).to_broadcast([P, sh.NB + 1, HEADS]))
            dve.wait_ge(chain, 1)
            nc.vector.tensor_reduce(widest[:, :], span[:, :], AX.X, ALU.max).then_inc(chain, 1)
            dve.wait_ge(chain, 2)
            nc.vector.tensor_scalar(c.wide[:, :], widest[0:1, :], SPAN, None, ALU.is_gt)


def attention_guard(nc, c):
    sh = c.sh
    with ExitStack() as st:
        sb = lambda name, shape, dt=F32: st.enter_context(nc.sbuf_tensor(f"{name}_guard", shape, dt))
        m, z = sb("m", [P, sh.NB, HEADS]), sb("z", [P, sh.NB, HEADS])
        most, every, low = sb("most", [P, 1]), sb("every", [P, 1]), sb("low", [P, 1])
        chain, zs, mosts, alls = [nc.alloc_semaphore(f"{x}_guard") for x in ("chain", "zs", "mosts", "alls")]
        block = st.enter_context(nc.Block())
        a_src, a_dst = c.node[:, 0:sh.NB, 0:HEADS], c.node[:, 0:sh.NB, HEADS:2 * HEADS]
        top = c.top[:, 0:sh.NB, 0:HEADS]

        @block.gpsimd
        def _(pool):
            pool.wait_ge(mosts, 1)
            nc.gpsimd.partition_all_reduce(every[:, :], most[:, :], P, bass.bass_isa.ReduceOp.max).then_inc(alls, 1)

        @block.vector
        def _(dve):
            n = [0]

            def link(instruction):
                n[0] += 1
                instruction.then_inc(chain, 1)
                dve.wait_ge(chain, n[0])

            nc.vector.tensor_copy(c.own[:, :, :], a_src)
            link(nc.vector.tensor_tensor(m[:, :, :], top, a_src, ALU.max))
            link(nc.vector.tensor_tensor(m[:, :, :], m[:, :, :], a_dst, ALU.add))
            link(nc.vector.scalar_tensor_tensor(m[:, :, :], m[:, :, :], SLOPE, m[:, :, :], ALU.mult, ALU.max))
            nc.vector.tensor_reduce(most[:, :], m[:, :, :].rearrange("p b h -> p (b h)"), AX.X, ALU.max).then_inc(mosts, 1)
            link(nc.vector.tensor_tensor(z[:, :, :], a_src, a_dst, ALU.add))
            link(nc.vector.scalar_tensor_tensor(z[:, :, :], z[:, :, :], SLOPE, z[:, :, :], ALU.mult, ALU.max))
            nc.vector.tensor_tensor(z[:, :, :], z[:, :, :], m[:, :, :], ALU.subtract).then_inc(zs, 1)
            link(nc.vector.scalar_tensor_tensor(low[:, :], c.peak[:, :], SLOPE, c.peak[:, :], ALU.mult, ALU.max))
            dve.wait_ge(alls, 1)
            link(nc.vector.tensor_tensor(c.peak[:, :], low[:, :], every[:, :], ALU.max))
            link(nc.vector.tensor_copy(c.node[:, 0:sh.NB, 0:HEADS], a_dst))
            nc.vector.tensor_scalar(c.node[:, 0:sh.NB, HEADS:2 * HEADS], m[:, :, :], c.peak[:, 0:1], None, ALU.subtract)
            nc.vector.memset(c.node[:, sh.NB, :], 0.0)

        @block.scalar
        def _(act):
            act.wait_ge(zs, 1)
            nc.scalar.activation(c.own[:, :, :], z[:, :, :], ACT.Exp)


def attention_update(nc, c):
    sh = c.sh
    G = 7
    ring = Ring(sh.NB, G)
    N = sh.N
    with ExitStack() as st:
        sb = lambda name, shape, dt=F32: st.enter_context(nc.sbuf_tensor(f"{name}_gat", shape, dt))
        pt = lambda name: st.enter_context(nc.psum_tensor(f"{name}_gat", [P, 512], F32))
        sem = lambda name: nc.alloc_semaphore(f"{name}_gat")
        own_row = sb("own_row", [P, G, AW])
        prod = sb("prod", [P, G, D])
        sq, h = sb("sq", [P, G, D]), sb("h", [P, G, D])
        bias, gamma, beta = sb("bias", [P, D]), sb("gamma", [P, D]), sb("beta", [P, D])
        mean, scale = sb("mean", [P, D]), sb("scale", [P, D])
        rden = sb("rden", [P, sh.NB, HEADS])
        stats, moments = sb("stats", [P, G, 6]), sb("moments", [P, G, 2])
        psM, psV = pt("psM"), pt("psV")
        par_in, rowed, chain, summed, centred, squared, varied, hs, xs, stated, freed = [sem(x) for x in (
            "par_in", "rowed", "chain", "summed", "centred", "squared", "varied", "hs", "xs", "stated", "freed")]
        zeroed, varied_rows = sem("zeroed"), sem("varied_rows")
        hb_s, xh_s, begun, rooted, shifted, outs = [sem(x) for x in ("hb_s", "xh_s", "begun", "rooted", "shifted", "outs")]
        scl, shift = sb("scl", [P, G]), sb("shift", [P, G])
        out = sb("out", [P, G, D])
        left = [sem(f"left{s}") for s in range(G)]
        var_in, var_root = sem("var_in"), sem("var_root")
        own_in = [sem(f"own_in{s}") for s in range(G)]
        block = st.enter_context(nc.Block())
        flat = lambda ap: ap.rearrange("p a d -> p (a d)")
        heads = lambda ap: ap.rearrange("p (h d) -> p h d", d=DH)
        spread = lambda ap: ap.rearrange("p a h -> p (a h)").unsqueeze(2).to_broadcast([P, HEADS, DH])

        @block.sync
        def _(sp):
            for to, of in ((bias, c.bias2_in), (gamma, c.gamma_in), (beta, c.beta_in)):
                sp.dma_start(to[:, :], row(of, D)).then_inc(par_in, 16)
            sp.wait_ge(zeroed, 1)

            def step(i, u):
                t = ring.at(i, u)
                T = ring.count(t) - 1
                rows = sh.LAST if isinstance(T, int) and T == sh.NB - 1 else P
                wait_count(sp, freed, ring.count(t, G))
                sp.dma_start(own_row[0:rows, u, :], c.gtab[bass.ds(P * T, rows), :]).then_inc(own_in[u], 16)
            ring.run(sp, step)
            sp.wait_ge(par_in, 48)

            def send(i, u):
                t = ring.at(i, u)
                T = ring.count(t) - 1
                rows = sh.LAST if isinstance(T, int) and T == sh.NB - 1 else P
                sp.wait_ge(outs, ring.count(t))
                sp.dma_start(c.htab[bass.ds(P * T, rows), :], out[0:rows, u, :]).then_inc(left[u], 16)
            ring.run(sp, send)
            for s in range(G):
                sp.wait_ge(left[s], 16 * ring.rounds)

        @block.gpsimd
        def _(pool):
            gate = Gate(pool, c.passed["pool"])
            pool.wait_ge(par_in, 48)
            def a_round(i):
                for s in range(G):
                    pool.wait_ge(hs, G * i + s + 1)
                    nc.gpsimd.tensor_tensor(h[:, s, :], h[:, s, :], beta[:, :], ALU.add).then_inc(hb_s, 1)
                pool.wait_ge(hb_s, G * i + G)
                gate.step()
                for s in range(G):
                    here = flat(c.x[:, bass.ds(G * i + s, 1), :])
                    nc.gpsimd.tensor_tensor(here, here, h[:, s, :], ALU.add).then_inc(xh_s, 1)
            peeled(pool, ring.rounds, a_round)

        @block.vector
        def _(dve):
            gate = Gate(dve, c.passed["dve"])
            nc.vector.memset(own_row[:, :, :], 0.0).then_inc(zeroed, 1)
            nc.vector.tensor_tensor(rden[:, :, :], c.acc[:, 0:sh.NB, D:AW], c.own[:, :, :], ALU.add).then_inc(chain, 1)
            dve.wait_ge(chain, 1)
            nc.vector.reciprocal(rden[:, :, :], rden[:, :, :]).then_inc(chain, 1)
            dve.wait_ge(chain, 2)
            dve.wait_ge(par_in, 48)

            def mean_rows(i):
                wait_count(dve, rowed, 3 * i)
                for s in range(G):
                    dve.wait_ge(own_in[s], 16 * (i + 1))
                    nc.vector.tensor_tensor(heads(prod[:, s, :]), heads(own_row[:, s, 0:D]),
                                            spread(c.own[:, bass.ds(G * i + s, 1), :]), ALU.mult).then_inc(freed, 1)
                dve.wait_ge(freed, G * i + G)
                for s in range(G):
                    last = nc.vector.tensor_tensor(prod[:, s, :], prod[:, s, :], flat(c.acc[:, bass.ds(G * i + s, 1), 0:D]), ALU.add)
                last.then_inc(rowed, 1)
                dve.wait_ge(rowed, 3 * i + 1)
                for s in range(G):
                    last = nc.vector.tensor_tensor(heads(prod[:, s, :]), heads(prod[:, s, :]),
                                                   spread(rden[:, bass.ds(G * i + s, 1), :]), ALU.mult)
                last.then_inc(rowed, 1)
                dve.wait_ge(rowed, 3 * i + 2)
                for s in range(G):
                    last = nc.vector.tensor_tensor(flat(c.acc[:, bass.ds(G * i + s, 1), 0:D]), prod[:, s, :], bias[:, :], ALU.add)
                last.then_inc(rowed, 1)

            def a_round(i):
                mean_rows(i)
            peeled(dve, ring.rounds, a_round)
            dve.wait_ge(summed, 1)
            nc.vector.tensor_scalar(mean[:, :], psM[:, 0:D], 1.0 / N, None, ALU.mult).then_inc(chain, 1)
            dve.wait_ge(chain, 3)

            def a_tile(T):
                here = flat(c.acc[:, bass.ds(T, 1), 0:D])
                nc.vector.tensor_tensor(here, here, mean[:, :], ALU.subtract).then_inc(centred, 1)
            peeled(dve, sh.NB, a_tile)
            dve.wait_ge(varied, 1)
            nc.vector.tensor_scalar(scale[:, :], psV[:, 0:D], 1.0 / N, EPS, ALU.mult, ALU.add).then_inc(var_in, 1)
            dve.wait_ge(var_root, 1)
            nc.vector.reciprocal(scale[:, :], scale[:, :]).then_inc(chain, 1)
            dve.wait_ge(chain, 4)
            nc.vector.tensor_tensor(scale[:, :], scale[:, :], gamma[:, :], ALU.mult).then_inc(chain, 1)
            dve.wait_ge(chain, 5)
            dve.wait_ge(centred, sh.NB)

            def a_round(i):
                wait_count(dve, stated, 2 * i)
                for s in range(G):
                    nc.vector.tensor_tensor(prod[:, s, :], flat(c.acc[:, bass.ds(G * i + s, 1), 0:D]), scale[:, :],
                                            ALU.mult).then_inc(xs, 1)
                dve.wait_ge(xs, 2 * G * i + G)
                dve.wait_ge(xh_s, G * i + G)
                for s in range(G):
                    here = flat(c.x[:, bass.ds(G * i + s, 1), :])
                    nc.vector.tensor_tensor(here, here, prod[:, s, :], ALU.add).then_inc(xs, 1)
                dve.wait_ge(xs, 2 * G * i + 2 * G)
                gate.step()
                for s in range(G):
                    last = nc.vector.bn_stats(stats[:, s, :], flat(c.x[:, bass.ds(G * i + s, 1), :]))
                last.then_inc(stated, 1)
                dve.wait_ge(stated, 2 * i + 1)
                gate.step()
                for s in range(G):
                    last = nc.vector.bn_aggr(moments[:, s, :], stats[:, s, :])
                last.then_inc(stated, 1)
                dve.wait_ge(stated, 2 * i + 2)
                wait_count(dve, outs, G * i)
                nc.vector.tensor_scalar(scl[:, :], moments[:, :, 1], EPS, None, ALU.add).then_inc(begun, 1)
                dve.wait_ge(rooted, i + 1)
                nc.vector.reciprocal(scl[:, :], scl[:, :]).then_inc(shifted, 1)
                dve.wait_ge(shifted, 3 * i + 1)
                nc.vector.tensor_tensor(scl[:, :], scl[:, :], c.dinv[:, bass.ds(G * i, G)], ALU.mult).then_inc(shifted, 1)
                dve.wait_ge(shifted, 3 * i + 2)
                nc.vector.scalar_tensor_tensor(shift[:, :], moments[:, :, 0], -1.0, scl[:, :], ALU.mult, ALU.mult).then_inc(shifted, 1)
            peeled(dve, ring.rounds, a_round)

        @block.scalar
        def _(act):

            def a_round(i):
                for s in range(G):
                    T = G * i + s
                    wait_count(act, xh_s, T - s)
                    nc.scalar.activation(h[:, s, :], flat(c.x[:, bass.ds(T, 1), :]), ACT.Relu,
                                         bias=c.nbias[:, bass.ds(T, 1)], scale=c.rstd[:, bass.ds(T, 1)]).then_inc(hs, 1)
            peeled(act, ring.rounds, a_round)
            def a_round(i):
                for s in range(G):
                    act.wait_ge(centred, G * i + s + 1)
                    if s == 0:
                        wait_count(act, varied_rows, G * i)
                    nc.scalar.activation(sq[:, s, :], flat(c.acc[:, bass.ds(G * i + s, 1), 0:D]), ACT.Square).then_inc(squared, 1)
            peeled(act, ring.rounds, a_round)
            act.wait_ge(var_in, 1)
            nc.scalar.sqrt(scale[:, :], scale[:, :]).then_inc(var_root, 1)

            def a_round(i):
                act.wait_ge(begun, i + 1)
                nc.scalar.sqrt(scl[:, :], scl[:, :]).then_inc(rooted, 1)
                act.wait_ge(shifted, 3 * i + 3)
                for s in range(G):
                    wait_count(act, left[s], 16 * i)
                    nc.scalar.activation(out[:, s, :], flat(c.x[:, bass.ds(G * i + s, 1), :]), ACT.Relu,
                                         bias=shift[:, s:s + 1], scale=scl[:, s:s + 1]).then_inc(outs, 1)
            peeled(act, ring.rounds, a_round)

        @block.tensor
        def _(pe):
            def over_nodes(rows_of, ps, ready, done, each):
                def step(i, u):
                    t = ring.at(i, u)
                    T = ring.count(t) - 1
                    rows = sh.LAST if isinstance(T, int) and T == sh.NB - 1 else P
                    ready(t)
                    last = nc.tensor.matmul(ps[:, 0:D], c.ones[0:rows, :], rows_of(T, u, rows),
                                            start=isinstance(T, int) and T == 0, stop=isinstance(T, int) and T == sh.NB - 1,
                                            skip_group_check=True)
                    if each is not None:
                        last.then_inc(each, 1)
                ring.run(pe, step)
                nc.tensor.matmul(ps[:, 256:258], c.ones[:, :], c.ones[:, 0:2], start=False, stop=True,
                                 skip_group_check=True).then_inc(done, 1)

            over_nodes(lambda T, u, rows: c.acc[0:rows, bass.ds(T, 1), 0:D].rearrange("p a d -> p (a d)"), psM,
                       lambda t: pe.wait_ge(rowed, 3 * t[0] + 3) if t[1] == 0 else None, summed, None)
            over_nodes(lambda T, u, rows: sq[0:rows, u, :], psV,
                       lambda t: pe.wait_ge(squared, ring.count(t)), varied, varied_rows)


def gcn_output(nc, c):
    sh = c.sh
    G = 7
    ring = Ring(sh.NB, G)
    with ExitStack() as st:
        sb = lambda name, shape, dt=F32: st.enter_context(nc.sbuf_tensor(f"{name}_gcn", shape, dt))
        pt = lambda name: st.enter_context(nc.psum_tensor(f"{name}_gcn", [P, 512], F32))
        sem = lambda name: nc.alloc_semaphore(f"{name}_gcn")
        w, bias = sb("w", [P, 2, D]), sb("bias", [P, D])
        a, aT = sb("a", [P, G, D]), sb("aT", [P, G, D])
        y, z = sb("y", [P, G, D]), sb("z", [P, G, D])
        psT = [pt("psT0"), pt("psT1")]
        psO = [pt("psO0"), pt("psO1")]
        w_in, scaled, turned, aTs, made, ys, zs, outs = [sem(x) for x in (
            "w_in", "scaled", "turned", "aTs", "made", "ys", "zs", "outs")]
        left = [sem(f"left{s}") for s in range(G)]
        block = st.enter_context(nc.Block())
        flat = lambda ap: ap.rearrange("p a d -> p (a d)")

        @block.sync
        def _(sp):
            sp.dma_start(w[:, :, :], c.w3_in.rearrange("(k p) n -> p k n", p=P)).then_inc(w_in, 16)
            sp.dma_start(bias[:, :], row(c.bias3_in, D)).then_inc(w_in, 16)

            def step(i, u):
                t = ring.at(i, u)
                T = ring.count(t) - 1
                rows = sh.LAST if isinstance(T, int) and T == sh.NB - 1 else P
                sp.wait_ge(outs, ring.count(t))
                sp.dma_start(c.out[bass.ds(P * T, rows), :], z[0:rows, u, :]).then_inc(left[u], 16)
            ring.run(sp, step)
            sp.wait_ge(w_in, 32)
            for s in range(G):
                sp.wait_ge(left[s], 16 * ring.rounds)

        @block.scalar
        def _(act):
            def step(i, u):
                if (t := ring.at(i, u)) is not None:
                    T = ring.count(t) - 1
                    wait_count(act, turned, ring.count(t, G))
                    nc.scalar.activation(a[:, u, :], flat(c.acc[:, bass.ds(T, 1), 0:D]), ACT.Copy,
                                         scale=c.dinv[:, bass.ds(T, 1)]).then_inc(scaled, 1)
                if (t := ring.at(i, u, 2)) is not None:
                    act.wait_ge(turned, ring.count(t))
                    wait_count(act, made, ring.count(t, G - 2))
                    nc.scalar.copy(aT[:, t[1], :], psT[t[1] % 2][:, 0:D]).then_inc(aTs, 1)
            ring.run(act, step, lag=2)

        @block.tensor
        def _(pe):
            pe.wait_ge(w_in, 32)

            def step(i, u):
                if (t := ring.at(i, u)) is not None:
                    pe.wait_ge(scaled, ring.count(t))
                    wait_count(pe, aTs, ring.count(t, 1 if u == 0 else 2))
                    for k in range(2):
                        last = nc.tensor.transpose(psT[u % 2][:, k * P:(k + 1) * P], a[:, u, k * P:(k + 1) * P], c.ident[:, :])
                    last.then_inc(turned, 1)
                if (t := ring.at(i, u, 1)) is not None:
                    pe.wait_ge(aTs, ring.count(t))
                    wait_count(pe, ys, ring.count(t, 1 if t[1] == 0 else 2))
                    for k in range(2):
                        last = nc.tensor.matmul(psO[t[1] % 2][:, 0:D], aT[:, t[1], k * P:(k + 1) * P], w[:, k, :],
                                                start=(k == 0), stop=(k == 1))
                    last.then_inc(made, 1)
            ring.run(pe, step, lag=1)

        @block.vector
        def _(dve):
            dve.wait_ge(w_in, 32)

            def step(i, u):
                if (t := ring.at(i, u)) is not None:
                    dve.wait_ge(made, ring.count(t))
                    wait_count(dve, outs, ring.count(t, G))
                    nc.vector.tensor_tensor(y[:, u, :], psO[u % 2][:, 0:D], bias[:, :], ALU.add).then_inc(ys, 1)
                if (t := ring.at(i, u, 2)) is not None:
                    dve.wait_ge(ys, ring.count(t))
                    if not (isinstance(t[0], int) and t[0] == 0):
                        dve.wait_ge(left[t[1]], 16 * t[0])
                    nc.vector.scalar_tensor_tensor(z[:, t[1], :], y[:, t[1], :], SLOPE, y[:, t[1], :], ALU.mult, ALU.max).then_inc(zs, 1)
                if (t := ring.at(i, u, 4)) is not None:
                    dve.wait_ge(zs, ring.count(t))
                    nc.vector.tensor_tensor(z[:, t[1], :], z[:, t[1], :], flat(c.x[:, bass.ds(ring.count(t) - 1, 1), :]),
                                            ALU.add).then_inc(outs, 1)
            ring.run(dve, step, lag=4)


class Core:

    def __init__(self, sh):
        self.sh = sh


def stage(nc, build, *args):
    with nc.cleanup_on_exit():
        build(nc, *args)


def gnn_stack(nc, x_in, src_in, dst_in, attr_in, type_in, w1t_in, b1_in, w2t_in, wrel_in, bias1_in, watt_in,
              att_src_in, att_dst_in, bias2_in, gamma_in, beta_in, w3_in, bias3_in, out):
    sh = Shapes(x_in.shape[0], src_in.shape[0])
    c = Core(sh)
    c.x_in, c.src_in, c.dst_in, c.attr_in, c.type_in = x_in, src_in, dst_in, attr_in, type_in
    c.w1t_in, c.b1_in, c.w2t_in = w1t_in, b1_in, w2t_in
    c.wrel_in, c.bias1_in = wrel_in, bias1_in
    c.watt_in, c.att_src_in, c.att_dst_in = watt_in, att_src_in, att_dst_in
    c.bias2_in, c.gamma_in, c.beta_in, c.w3_in, c.bias3_in, c.out = bias2_in, gamma_in, beta_in, w3_in, bias3_in, out
    dram = lambda name, shape: nc.dram_tensor("dram_" + name, shape, F32, kind="Internal").ap()
    c.rec_dst, c.rec_src = dram("rec_dst", [sh.EP, REC]), dram("rec_src", [sh.EP, REC])
    c.ptab, c.xtab = dram("ptab", [sh.N, D]), dram("xtab", [NREL * sh.N, D])
    c.gtab, c.stab, c.htab = dram("gtab", [sh.N, AW]), dram("stab", [sh.N, HEADS]), dram("htab", [sh.N, D])
    with ExitStack() as ctx:
        sb = lambda name, shape, dt=F32: ctx.enter_context(nc.sbuf_tensor(name, shape, dt))
        c.tiles = {k: (sb(f"base_{k}", [P, sh.NT]), sb(f"place_{k}", [1, sh.NT], I32), sb(f"off_{k}", [1, sh.NT], I32))
                   for k in ("dst", "src")}
        c.node_i = sb("node_i", [1, sh.NT], I32)
        c.unsorted, c.wide = sb("unsorted", [1, 1], I32), sb("wide", [1, 1], I32)
        c.passed = {e: ctx.enter_context(nc.semaphore(f"passed_{e}")) for e in ("sp", "dve", "pool")}
        constants(nc, c, ctx)
        rounds = sh.COLS // U
        with ExitStack() as by_src:
            of_src = Edges(nc, c, "src", by_src)
            stage(nc, list_stage, c, of_src)
            stage(nc, place_stage, c, of_src)
            cut = [round(rounds * share) for share in CUTS]
            stage(nc, stats_stage, c, of_src, 0, cut[0])
            stage(nc, table_stage, c, 0, of_src, cut[0], cut[1])
            with ExitStack() as by_dst:
                of_dst = Edges(nc, c, "dst", by_dst)
                stage(nc, list_stage, c, of_dst, of_src, cut[1], cut[2])
                with nc.If(nc.values_load(c.unsorted[0:1, 0:1], min_val=0, max_val=sh.E) != 0):
                    stage(nc, place_stage, c, of_dst)
                    stage(nc, scatter_stage, c, of_dst, 0, rounds)
                nc.all_engine_barrier()
            with nc.sbuf_tensor("sage_sums", [P, sh.NB + 1, AW], F32) as c.acc:
                stage(nc, edge_pass, c, "dst", c.ptab, D, 0, "edge_mlp")
                stage(nc, sage_update, c, of_src, cut[2], cut[3])
            stage(nc, table_stage, c, 1, of_src, cut[3], rounds)
        c.acc = sb("sums", [P, sh.NB + 1, AW])
        c.top, c.node = sb("top", [P, sh.NB + 1, 2 * HEADS]), sb("node", [P, sh.NB + 1, 2 * HEADS])
        c.peak = sb("peak", [P, 1])
        c.own = sb("own", [P, sh.NB, HEADS])
        c.dinv = sb("dinv", [P, sh.NB])
        stage(nc, edge_pass, c, "src", c.xtab, D, 0, "plain")
        stage(nc, rgcn_update, c)
        stage(nc, range_stage, c)
        with nc.If(nc.values_load(c.wide[0:1, 0:1], min_val=0, max_val=1) != 0):
            stage(nc, edge_pass, c, "dst", c.stab, HEADS, 0, "max")
        nc.all_engine_barrier()
        stage(nc, attention_guard, c)
        stage(nc, edge_pass, c, "dst", c.gtab, AW, 0, "attend")
        stage(nc, attention_update, c)
        stage(nc, edge_pass, c, "src", c.htab, D, 2, "plain")
        stage(nc, gcn_output, c)


def kernel(x, src, dst, edge_attr_3, edge_type_8, L0_gnn_W1, L0_gnn_b1, L0_gnn_W2, L1_gnn_weight, L1_gnn_bias,
           L2_gnn_W, L2_gnn_att_src, L2_gnn_att_dst, L2_gnn_bias, L2_gnn_gamma, L2_gnn_beta, L3_gnn_W, L3_gnn_b):
    import concourse.bacc as bacc
    from concourse.bass_utils import run_bass_kernel_spmd

    arrays = {
        "x_in": x, "src_in": src, "dst_in": dst, "attr_in": np.asarray(edge_attr_3).reshape(-1), "type_in": edge_type_8,
        "w1t_in": np.asarray(L0_gnn_W1).T, "b1_in": L0_gnn_b1, "w2t_in": np.asarray(L0_gnn_W2).T,
        "wrel_in": L1_gnn_weight, "bias1_in": L1_gnn_bias, "watt_in": L2_gnn_W, "att_src_in": L2_gnn_att_src,
        "att_dst_in": L2_gnn_att_dst, "bias2_in": L2_gnn_bias, "gamma_in": L2_gnn_gamma, "beta_in": L2_gnn_beta,
        "w3_in": L3_gnn_W, "bias3_in": L3_gnn_b,
    }
    arrays = {k: np.ascontiguousarray(v) for k, v in arrays.items()}
    nc = bacc.Bacc("TRN2", target_bir_lowering=False, num_devices=1)
    args = {k: nc.dram_tensor(k, v.shape, mybir.dt.from_np(v.dtype), kind="ExternalInput").ap() for k, v in arrays.items()}
    out = nc.dram_tensor("out", arrays["x_in"].shape, F32, kind="ExternalOutput").ap()
    gnn_stack(nc, **args, out=out)
    r = run_bass_kernel_spmd(nc, [arrays], core_ids=[0])
    return r.results[0]["out"]
```
